# Optimizing a Trainium2 kernel written in Bass

```python
import numpy as np
import jax
import jax.numpy as jnp

def _softmax(x, axis=-1):
    return jax.nn.softmax(x, axis=axis)

def _gelu(x):
    return jax.nn.gelu(x, approximate=True)

def _silu(x):
    return jax.nn.silu(x)

def _sigmoid(x):
    return jax.nn.sigmoid(x)

def _layernorm(x, axis=-1, eps=1e-05):
    m = jnp.mean(x, axis=axis, keepdims=True)
    v = jnp.var(x, axis=axis, keepdims=True)
    return (x - m) / jnp.sqrt(v + eps)

def _scatter_add(tgt, idx, src, axis=0):
    return tgt.at[idx].add(src)

def _segment_sum(src, seg, n):
    return jax.ops.segment_sum(src, seg, n)
kernel_name = 'mk_gnn_resnorm_d4_gnn_r32_793c2e'

def setup_inputs(seed: int=0):
    np.random.seed(seed)
    _w = jnp.asarray

    def _rec_inputs():
        import jax
        import jax.numpy as jnp
        _gk = jax.random.key(seed)
        x = -8.776e-05 + 1 * jax.random.normal(jax.random.fold_in(_gk, 1), (3125, 256), jnp.float32)
        _s = jax.random.randint(jax.random.fold_in(_gk, 2), (25000,), 0, 3125, jnp.int32)
        _d = jax.random.randint(jax.random.fold_in(_gk, 3), (25000,), 0, 3125, jnp.int32)
        _loop = jnp.arange(3125, dtype=jnp.int32)
        src = jnp.concatenate([_s, _d, _loop])
        dst = jnp.concatenate([_d, _s, _loop])
        _o = jnp.argsort(dst, stable=True)
        src = src[_o]
        dst = dst[_o]
        edge_attr_32 = 0.000398968 + 1.00027 * jax.random.normal(jax.random.fold_in(_gk, 12), (53125, 32), jnp.float32)
        edge_type_3 = jax.random.randint(jax.random.fold_in(_gk, 14), (53125,), 0, 3, jnp.int32)
        edge_type_8 = jax.random.randint(jax.random.fold_in(_gk, 15), (53125,), 0, 8, jnp.int32)
        node_type_4 = jax.random.randint(jax.random.fold_in(_gk, 16), (3125,), 0, 4, jnp.int32)
        return (x, src, dst, edge_attr_32, edge_type_3, edge_type_8, node_type_4)
    x, src, dst, edge_attr_32, edge_type_3, edge_type_8, node_type_4 = _rec_inputs()

    def _L0_gnn_setup():
        import jax, jax.numpy as jnp
        import numpy as np
        N_NODES = 625
        N_EDGES = 10000
        IN_DIM = 256
        OUT_DIM = 256
        N_HEADS = 4
        D_K = OUT_DIM // N_HEADS
        N_NTYPES = 4
        N_RELS = 8
        SQRT_DK = float(np.sqrt(D_K))

        def _typed_matmul(x, W, node_type):
            all_t = jnp.einsum('ni,tio->tno', x, W)
            return all_t[node_type, jnp.arange(x.shape[0])]
        key = jax.random.key(seed)
        ks = jax.random.split(key, 12)
        xav = lambda k, shape, fan: jax.random.normal(k, shape, jnp.float32) * (1.0 / np.sqrt(fan))
        return {'h': jax.random.normal(ks[0], (N_NODES, IN_DIM), jnp.float32), 'k_linears': xav(ks[1], (N_NTYPES, IN_DIM, OUT_DIM), IN_DIM), 'q_linears': xav(ks[2], (N_NTYPES, IN_DIM, OUT_DIM), IN_DIM), 'v_linears': xav(ks[3], (N_NTYPES, IN_DIM, OUT_DIM), IN_DIM), 'a_linears': xav(ks[4], (N_NTYPES, OUT_DIM, OUT_DIM), OUT_DIM), 'relation_att': xav(ks[5], (N_RELS, N_HEADS, D_K, D_K), D_K), 'relation_msg': xav(ks[6], (N_RELS, N_HEADS, D_K, D_K), D_K), 'relation_pri': jnp.ones((N_RELS, N_HEADS), jnp.float32), 'skip': jnp.ones((N_NTYPES,), jnp.float32), 'node_type': jax.random.randint(ks[7], (N_NODES,), 0, N_NTYPES), 'etype': jnp.sort(jax.random.randint(ks[8], (N_EDGES,), 0, N_RELS)), 'row_idx': jax.random.randint(ks[9], (N_EDGES,), 0, N_NODES), 'col_idx': jax.random.randint(ks[10], (N_EDGES,), 0, N_NODES)}
    _L0_gnn_all = _L0_gnn_setup()
    _L0_gnn_in = {k: v for k, v in _L0_gnn_all.items() if k in ('k_linears', 'q_linears', 'v_linears', 'a_linears', 'relation_att', 'relation_msg', 'relation_pri', 'skip')}
    del _L0_gnn_all

    def _L1_gnn_setup():
        import jax, jax.numpy as jnp
        import numpy as np
        N_NODES = 512
        N_EDGES = 8192
        D_IN = 256
        D = 256
        H = 512
        E = 64
        TOP_K = 2
        CAP = 1024
        BN_EPS = 1e-05

        def _moe_ff(x, Wg, bg, w1, b1, w2, b2):
            N = x.shape[0]
            logits = x @ Wg + bg
            vals, idx = jax.lax.top_k(logits, TOP_K)
            gates = jax.nn.softmax(vals, axis=-1)
            e_flat = idx.reshape(-1)
            g_flat = gates.reshape(-1)
            tok = jnp.arange(N * TOP_K) // TOP_K
            order = jnp.argsort(e_flat)
            e_s, tok_s, g_s = (e_flat[order], tok[order], g_flat[order])
            counts = jnp.bincount(e_flat, length=E)
            offs = jnp.concatenate([jnp.zeros((1,), counts.dtype), jnp.cumsum(counts)[:-1]])
            rank = jnp.arange(N * TOP_K) - offs[e_s]
            valid = rank < CAP
            slot = jnp.where(valid, e_s * CAP + rank, E * CAP)
            buf = jnp.zeros((E * CAP + 1, D), x.dtype).at[slot].set(x[tok_s])
            h = buf[:E * CAP].reshape(E, CAP, D)
            h1 = jax.nn.gelu(jnp.einsum('ecd,edh->ech', h, w1) + b1[:, None, :], approximate=False)
            h2 = jnp.einsum('ech,ehd->ecd', h1, w2) + b2[:, None, :]
            out_buf = h2.reshape(E * CAP, D)
            y_s = jnp.where(valid[:, None], out_buf[jnp.minimum(slot, E * CAP - 1)], 0.0)
            return jnp.zeros((N, D), x.dtype).at[tok_s].add(g_s[:, None] * y_s)

        def _forward(feats, W_gc, b_gc, W_res, b_res, Wg, bg, w1, b1, w2, b2, gamma, beta, src, dst):
            n = feats.shape[0]
            ones = jnp.ones((src.shape[0],), feats.dtype)
            deg_out = jnp.clip(jax.ops.segment_sum(ones, src, num_segments=n), 1.0)
            deg_in = jnp.clip(jax.ops.segment_sum(ones, dst, num_segments=n), 1.0)
            h = feats * jax.lax.rsqrt(deg_out)[:, None]
            m = jax.ops.segment_sum(h[src], dst, num_segments=n) * jax.lax.rsqrt(deg_in)[:, None]
            gc = m @ W_gc + b_gc
            x = gc + (feats @ W_res + b_res)
            core = _moe_ff(x, Wg, bg, w1, b1, w2, b2)
            y = x + core
            mean = jnp.mean(y, axis=0)
            var = jnp.mean((y - mean) ** 2, axis=0)
            return (y - mean) * jax.lax.rsqrt(var + BN_EPS) * gamma + beta
        key = jax.random.key(seed)
        ks = jax.random.split(key, 16)
        s = lambda d: 1.0 / np.sqrt(d)
        inp = {'feats': jax.random.normal(ks[0], (N_NODES, D_IN), jnp.float32), 'W_gc': jax.random.normal(ks[1], (D_IN, D), jnp.float32) * s(D_IN), 'b_gc': jnp.zeros((D,), jnp.float32), 'W_res': jax.random.normal(ks[2], (D_IN, D), jnp.float32) * s(D_IN), 'b_res': jnp.zeros((D,), jnp.float32), 'Wg': jax.random.normal(ks[3], (D, E), jnp.float32) * s(D), 'bg': jnp.zeros((E,), jnp.float32), 'w1': jax.random.normal(ks[4], (E, D, H), jnp.float32) * s(D), 'b1': jnp.zeros((E, H), jnp.float32), 'w2': jax.random.normal(ks[5], (E, H, D), jnp.float32) * s(H), 'b2': jnp.zeros((E, D), jnp.float32), 'gamma': jnp.ones((D,), jnp.float32), 'beta': jnp.zeros((D,), jnp.float32), 'src': jax.random.randint(ks[6], (N_EDGES,), 0, N_NODES), 'dst': jax.random.randint(ks[7], (N_EDGES,), 0, N_NODES)}
        return inp
    _L1_gnn_all = _L1_gnn_setup()
    _L1_gnn_in = {k: v for k, v in _L1_gnn_all.items() if k in ('W_gc', 'b_gc', 'W_res', 'b_res', 'Wg', 'bg', 'w1', 'b1', 'w2', 'b2', 'gamma', 'beta')}
    del _L1_gnn_all

    def _L2_gnn_setup():
        import jax, jax.numpy as jnp
        import numpy as np
        BN_EPS = 1e-05
        key = jax.random.key(seed)
        k1, k2, k3 = jax.random.split(key, 3)
        N, F, H, E = (50000, 256, 256, 50000)
        x = jax.random.normal(k1, (N, F), dtype=jnp.float32)
        edge_index = jax.random.randint(k2, (2, E), 0, N, dtype=jnp.int64)
        lim = 1.0 / np.sqrt(F)
        W = jax.random.uniform(k3, (H, F), dtype=jnp.float32, minval=-lim, maxval=lim)
        b = jnp.zeros((H,), dtype=jnp.float32)
        bn_w = jnp.ones((H,), dtype=jnp.float32)
        bn_b = jnp.zeros((H,), dtype=jnp.float32)
        return {'x': x, 'edge_index': edge_index, 'W': W, 'b': b, 'bn_w': bn_w, 'bn_b': bn_b}
    _L2_gnn_all = _L2_gnn_setup()
    _L2_gnn_in = {k: v for k, v in _L2_gnn_all.items() if k in ('W', 'b', 'bn_w', 'bn_b')}
    del _L2_gnn_all

    def _L3_gnn_setup():
        import jax, jax.numpy as jnp
        import numpy as np
        N_NODES = 10000
        N_EDGES = 5000
        D = 256
        NUM_REL = 3
        NUM_DISTS = 32
        N_LAYERS = 3

        def _gcn_forward(x, edge_index, edge_type, edge_attr, weights, roots, biases, edge_w, edge_b):
            n = x.shape[0]
            src, dst = (edge_index[0], edge_index[1])
            ew = edge_attr @ edge_w + edge_b
            rel_masks = [(edge_type == i).astype(x.dtype) for i in range(NUM_REL)]
            inv_cnt = [1.0 / jnp.maximum(jax.ops.segment_sum(m, dst, num_segments=n), 1.0) for m in rel_masks]
            for l in range(N_LAYERS):
                residual = x
                msg = jax.nn.relu(x[src] * ew)
                out = jnp.zeros((n, D), dtype=x.dtype)
                for i in range(NUM_REL):
                    h = jax.ops.segment_sum(msg * rel_masks[i][:, None], dst, num_segments=n)
                    h = h * inv_cnt[i][:, None]
                    out = out + h @ weights[l, i]
                out = out + x @ roots[l] + biases[l]
                x = residual + jax.nn.relu(out)
            return x
        key = jax.random.key(seed)
        ks = jax.random.split(key, 12)
        s = 1.0 / np.sqrt(D)
        inp = {'x': jax.random.normal(ks[0], (N_NODES, D), dtype=jnp.float32), 'edge_index': jax.random.randint(ks[1], (2, N_EDGES), 0, N_NODES, dtype=jnp.int32), 'edge_type': jax.random.randint(ks[2], (N_EDGES,), 0, NUM_REL, dtype=jnp.int32), 'edge_attr': jax.random.normal(ks[3], (N_EDGES, NUM_DISTS), dtype=jnp.float32), 'weights': jax.random.normal(ks[4], (N_LAYERS, NUM_REL, D, D), dtype=jnp.float32) * s, 'roots': jax.random.normal(ks[5], (N_LAYERS, D, D), dtype=jnp.float32) * s, 'biases': jax.random.normal(ks[6], (N_LAYERS, D), dtype=jnp.float32) * 0.01, 'edge_w': jax.random.normal(ks[7], (NUM_DISTS, D), dtype=jnp.float32) * (1.0 / np.sqrt(NUM_DISTS)), 'edge_b': jax.random.normal(ks[8], (D,), dtype=jnp.float32) * 0.01}
        return inp
    _L3_gnn_all = _L3_gnn_setup()
    _L3_gnn_in = {k: v for k, v in _L3_gnn_all.items() if k in ('weights', 'roots', 'biases', 'edge_w', 'edge_b')}
    del _L3_gnn_all
    return {'x': x, 'src': src, 'dst': dst, 'edge_attr_32': edge_attr_32, 'edge_type_3': edge_type_3, 'edge_type_8': edge_type_8, 'node_type_4': node_type_4, 'L0_gnn_k_linears': _L0_gnn_in['k_linears'], 'L0_gnn_q_linears': _L0_gnn_in['q_linears'], 'L0_gnn_v_linears': _L0_gnn_in['v_linears'], 'L0_gnn_a_linears': _L0_gnn_in['a_linears'], 'L0_gnn_relation_att': _L0_gnn_in['relation_att'], 'L0_gnn_relation_msg': _L0_gnn_in['relation_msg'], 'L0_gnn_relation_pri': _L0_gnn_in['relation_pri'], 'L0_gnn_skip': _L0_gnn_in['skip'], 'L1_gnn_W_gc': _L1_gnn_in['W_gc'], 'L1_gnn_b_gc': _L1_gnn_in['b_gc'], 'L1_gnn_W_res': _L1_gnn_in['W_res'], 'L1_gnn_b_res': _L1_gnn_in['b_res'], 'L1_gnn_Wg': _L1_gnn_in['Wg'], 'L1_gnn_bg': _L1_gnn_in['bg'], 'L1_gnn_w1': _L1_gnn_in['w1'], 'L1_gnn_b1': _L1_gnn_in['b1'], 'L1_gnn_w2': _L1_gnn_in['w2'], 'L1_gnn_b2': _L1_gnn_in['b2'], 'L1_gnn_gamma': _L1_gnn_in['gamma'], 'L1_gnn_beta': _L1_gnn_in['beta'], 'L2_gnn_W': _L2_gnn_in['W'], 'L2_gnn_b': _L2_gnn_in['b'], 'L2_gnn_bn_w': _L2_gnn_in['bn_w'], 'L2_gnn_bn_b': _L2_gnn_in['bn_b'], 'L3_gnn_weights': _L3_gnn_in['weights'], 'L3_gnn_roots': _L3_gnn_in['roots'], 'L3_gnn_biases': _L3_gnn_in['biases'], 'L3_gnn_edge_w': _L3_gnn_in['edge_w'], 'L3_gnn_edge_b': _L3_gnn_in['edge_b']}

def reference(x, src, dst, edge_attr_32, edge_type_3, edge_type_8, node_type_4, L0_gnn_k_linears, L0_gnn_q_linears, L0_gnn_v_linears, L0_gnn_a_linears, L0_gnn_relation_att, L0_gnn_relation_msg, L0_gnn_relation_pri, L0_gnn_skip, L1_gnn_W_gc, L1_gnn_b_gc, L1_gnn_W_res, L1_gnn_b_res, L1_gnn_Wg, L1_gnn_bg, L1_gnn_w1, L1_gnn_b1, L1_gnn_w2, L1_gnn_b2, L1_gnn_gamma, L1_gnn_beta, L2_gnn_W, L2_gnn_b, L2_gnn_bn_w, L2_gnn_bn_b, L3_gnn_weights, L3_gnn_roots, L3_gnn_biases, L3_gnn_edge_w, L3_gnn_edge_b):
    import jax
    import jax.numpy as jnp

    def _L0_gnn_ref(h, k_linears, q_linears, v_linears, a_linears, relation_att, relation_msg, relation_pri, skip, node_type, etype, row_idx, col_idx):
        import jax, jax.numpy as jnp
        import numpy as np
        N_NODES = 625
        N_EDGES = 10000
        IN_DIM = 256
        OUT_DIM = 256
        N_HEADS = 4
        D_K = OUT_DIM // N_HEADS
        N_NTYPES = 4
        N_RELS = 8
        SQRT_DK = float(np.sqrt(D_K))

        def _typed_matmul(x, W, node_type):
            all_t = jnp.einsum('ni,tio->tno', x, W)
            return all_t[node_type, jnp.arange(x.shape[0])]
        n = h.shape[0]
        k = _typed_matmul(h, k_linears, node_type).reshape(n, N_HEADS, D_K)
        q = _typed_matmul(h, q_linears, node_type).reshape(n, N_HEADS, D_K)
        v = _typed_matmul(h, v_linears, node_type).reshape(n, N_HEADS, D_K)
        q_att = jnp.einsum('nhd,rhde->rnhe', q, relation_att)
        v_msg = jnp.einsum('nhd,rhde->rnhe', v, relation_msg)
        aw_q_edge = q_att[etype, col_idx]
        msg_edge = v_msg[etype, row_idx]
        attn_score = jnp.sum(aw_q_edge * k[row_idx], axis=-1)
        score = attn_score * (relation_pri[etype] / SQRT_DK)
        m = jax.ops.segment_max(score, col_idx, num_segments=n)
        ex = jnp.exp(score - m[col_idx])
        denom = jax.ops.segment_sum(ex, col_idx, num_segments=n)
        alpha = ex / denom[col_idx]
        agg = jax.ops.segment_sum(alpha[..., None] * msg_edge, col_idx, num_segments=n)
        agg = agg.reshape(n, OUT_DIM)
        out = _typed_matmul(agg, a_linears, node_type)
        out = jax.nn.sigmoid(skip)[node_type][:, None] * out
        return out

    def _L1_gnn_ref(feats, W_gc, b_gc, W_res, b_res, Wg, bg, w1, b1, w2, b2, gamma, beta, src, dst):
        import jax, jax.numpy as jnp
        import numpy as np
        N_NODES = 512
        N_EDGES = 8192
        D_IN = 256
        D = 256
        H = 512
        E = 64
        TOP_K = 2
        CAP = 1024
        BN_EPS = 1e-05

        def _moe_ff(x, Wg, bg, w1, b1, w2, b2):
            N = x.shape[0]
            logits = x @ Wg + bg
            vals, idx = jax.lax.top_k(logits, TOP_K)
            gates = jax.nn.softmax(vals, axis=-1)
            e_flat = idx.reshape(-1)
            g_flat = gates.reshape(-1)
            tok = jnp.arange(N * TOP_K) // TOP_K
            order = jnp.argsort(e_flat)
            e_s, tok_s, g_s = (e_flat[order], tok[order], g_flat[order])
            counts = jnp.bincount(e_flat, length=E)
            offs = jnp.concatenate([jnp.zeros((1,), counts.dtype), jnp.cumsum(counts)[:-1]])
            rank = jnp.arange(N * TOP_K) - offs[e_s]
            valid = rank < CAP
            slot = jnp.where(valid, e_s * CAP + rank, E * CAP)
            buf = jnp.zeros((E * CAP + 1, D), x.dtype).at[slot].set(x[tok_s])
            h = buf[:E * CAP].reshape(E, CAP, D)
            h1 = jax.nn.gelu(jnp.einsum('ecd,edh->ech', h, w1) + b1[:, None, :], approximate=False)
            h2 = jnp.einsum('ech,ehd->ecd', h1, w2) + b2[:, None, :]
            out_buf = h2.reshape(E * CAP, D)
            y_s = jnp.where(valid[:, None], out_buf[jnp.minimum(slot, E * CAP - 1)], 0.0)
            return jnp.zeros((N, D), x.dtype).at[tok_s].add(g_s[:, None] * y_s)

        def _forward(feats, W_gc, b_gc, W_res, b_res, Wg, bg, w1, b1, w2, b2, gamma, beta, src, dst):
            n = feats.shape[0]
            ones = jnp.ones((src.shape[0],), feats.dtype)
            deg_out = jnp.clip(jax.ops.segment_sum(ones, src, num_segments=n), 1.0)
            deg_in = jnp.clip(jax.ops.segment_sum(ones, dst, num_segments=n), 1.0)
            h = feats * jax.lax.rsqrt(deg_out)[:, None]
            m = jax.ops.segment_sum(h[src], dst, num_segments=n) * jax.lax.rsqrt(deg_in)[:, None]
            gc = m @ W_gc + b_gc
            x = gc + (feats @ W_res + b_res)
            core = _moe_ff(x, Wg, bg, w1, b1, w2, b2)
            y = x + core
            mean = jnp.mean(y, axis=0)
            var = jnp.mean((y - mean) ** 2, axis=0)
            return (y - mean) * jax.lax.rsqrt(var + BN_EPS) * gamma + beta
        return _forward(feats, W_gc, b_gc, W_res, b_res, Wg, bg, w1, b1, w2, b2, gamma, beta, src, dst)

    def _L2_gnn_ref(x, edge_index, W, b, bn_w, bn_b):
        import jax, jax.numpy as jnp
        import numpy as np
        BN_EPS = 1e-05
        N = x.shape[0]
        src, dst = (edge_index[0], edge_index[1])
        agg = jax.ops.segment_sum(x[src], dst, num_segments=N)
        h = x + agg
        h = jnp.einsum('nf,hf->nh', h, W) + b
        mean = jnp.mean(h, axis=0)
        var = jnp.mean(jnp.square(h - mean), axis=0)
        out = (h - mean) * jax.lax.rsqrt(var + BN_EPS) * bn_w + bn_b
        return out

    def _L3_gnn_ref(x, edge_index, edge_type, edge_attr, weights, roots, biases, edge_w, edge_b):
        import jax, jax.numpy as jnp
        import numpy as np
        N_NODES = 10000
        N_EDGES = 5000
        D = 256
        NUM_REL = 3
        NUM_DISTS = 32
        N_LAYERS = 3

        def _gcn_forward(x, edge_index, edge_type, edge_attr, weights, roots, biases, edge_w, edge_b):
            n = x.shape[0]
            src, dst = (edge_index[0], edge_index[1])
            ew = edge_attr @ edge_w + edge_b
            rel_masks = [(edge_type == i).astype(x.dtype) for i in range(NUM_REL)]
            inv_cnt = [1.0 / jnp.maximum(jax.ops.segment_sum(m, dst, num_segments=n), 1.0) for m in rel_masks]
            for l in range(N_LAYERS):
                residual = x
                msg = jax.nn.relu(x[src] * ew)
                out = jnp.zeros((n, D), dtype=x.dtype)
                for i in range(NUM_REL):
                    h = jax.ops.segment_sum(msg * rel_masks[i][:, None], dst, num_segments=n)
                    h = h * inv_cnt[i][:, None]
                    out = out + h @ weights[l, i]
                out = out + x @ roots[l] + biases[l]
                x = residual + jax.nn.relu(out)
            return x
        return _gcn_forward(x, edge_index, edge_type, edge_attr, weights, roots, biases, edge_w, edge_b)
    edge_index = jnp.stack([src, dst])
    x = _layernorm(x + _L0_gnn_ref(x, L0_gnn_k_linears, L0_gnn_q_linears, L0_gnn_v_linears, L0_gnn_a_linears, L0_gnn_relation_att, L0_gnn_relation_msg, L0_gnn_relation_pri, L0_gnn_skip, node_type_4, edge_type_8, src, dst), axis=-1)
    x = _layernorm(x + _L1_gnn_ref(x, L1_gnn_W_gc, L1_gnn_b_gc, L1_gnn_W_res, L1_gnn_b_res, L1_gnn_Wg, L1_gnn_bg, L1_gnn_w1, L1_gnn_b1, L1_gnn_w2, L1_gnn_b2, L1_gnn_gamma, L1_gnn_beta, src, dst), axis=-1)
    x = _layernorm(x + _L2_gnn_ref(x, edge_index, L2_gnn_W, L2_gnn_b, L2_gnn_bn_w, L2_gnn_bn_b), axis=-1)
    x = _layernorm(x + _L3_gnn_ref(x, edge_index, edge_type_3, edge_attr_32, L3_gnn_weights, L3_gnn_roots, L3_gnn_biases, L3_gnn_edge_w, L3_gnn_edge_b), axis=-1)
    return x

_drawn_inputs = setup_inputs


def setup_inputs(seed=0):
    import zlib

    import numpy as np

    out = dict(_drawn_inputs(seed))
    spreads = {'L0_gnn_relation_pri': (1.0, 0.2),
     'L0_gnn_skip': (1.0, 0.2),
     'L1_gnn_b_gc': (0.0, 0.1),
     'L1_gnn_b_res': (0.0, 0.1),
     'L1_gnn_bg': (0.0, 0.1),
     'L1_gnn_b1': (0.0, 0.305),
     'L1_gnn_b2': (0.0, 0.1),
     'L1_gnn_gamma': (1.0, 0.2),
     'L1_gnn_beta': (0.0, 0.1),
     'L2_gnn_b': (0.0, 0.8),
     'L2_gnn_bn_w': (1.0, 0.2),
     'L2_gnn_bn_b': (0.0, 0.1)}
    factors = {'L3_gnn_biases': 8.0, 'L3_gnn_edge_b': 8.0}
    for name, (base, spread) in spreads.items():
        noise = np.random.default_rng([zlib.crc32(name.encode()), seed]).standard_normal(out[name].shape)
        drawn = base * np.exp(spread * noise) if base else spread * noise
        out[name] = jnp.asarray(drawn.astype(out[name].dtype))
    for name, factor in factors.items():
        out[name] = (out[name] * factor).astype(out[name].dtype)
    return out
```

```python
from contextlib import ExitStack

import concourse.bass as bass
from concourse import mybir

F32 = mybir.dt.float32
BF16 = mybir.dt.bfloat16
I32 = mybir.dt.int32
ALU = mybir.AluOpType
ACT = mybir.ActivationFunctionType
AX = mybir.AxisListType.X

N, E, D = 3125, 53125, 256
P = 125
NODE_TILES = N // P
EDGE_TILES = E // P
RING = 6
SLOTS = -(-(EDGE_TILES + NODE_TILES - 1) // RING) * RING
ROUNDS = SLOTS // RING
HALF = RING // 2
JC, JP = 5, EDGE_TILES // 5
KC = D // 128
HEADS, DK = 4, 64
NTYPES, RELS, REL3 = 4, 8, 3
EXTRA = 8
SCAN_C = 25
SCAN_S = SLOTS // SCAN_C
SLOT_C, SLOT_P = 5, SLOTS // 5
BIG = 1e30
LN_EPS = 1e-5


def ds(i, n):
    return bass.ds(i, n)


class Chain:

    def __init__(self, eng, sem):
        self.eng, self.sem, self.base, self.n = eng, sem, 0, 0

    def at(self, base):
        self.base, self.n = base, 0

    def __call__(self, ins):
        self.n += 1
        ins.then_inc(self.sem, 1)
        self.eng.wait_ge(self.sem, self.base + self.n)


def known(t, at_least):
    return not isinstance(t, int) or t >= at_least


def by_tiles(eng, body):
    for t in range(3):
        body(t, t % 2, t // 2)
    with eng.Fori(1, NODE_TILES // 2) as k:
        body(2 * k + 1, 1, k)
        body(2 * k + 2, 0, k + 1)


def by_slots(eng, body):
    body(0, 0)
    with eng.Fori(1, ROUNDS) as i:
        body(i * RING, i)


def col(table, s, n=1):
    return table[:, s:s + n] if isinstance(s, int) else table[:, ds(s, n)]


class Core:
    pass


def constants(nc, c):
    with nc.sbuf_tensor("iota_i", [128, 128], I32) as iota_i, nc.sbuf_tensor("part_i", [128, 1], I32) as part_i:
        made, dve = c.sem("iota_made"), c.sem("const_chain")
        with nc.Block() as block:
            @block.gpsimd
            def _(pool):
                pool.iota(iota_i[:, :], [[1, 128]], base=0, channel_multiplier=0).then_inc(made, 1)
                pool.iota(part_i[:, :], [[0, 1]], base=0, channel_multiplier=1).then_inc(made, 1)

            @block.vector
            def _(v):
                do = Chain(v, dve)
                do(v.memset(c.ones[:, :], 1.0))
                v.wait_ge(made, 2)
                do(v.tensor_copy(c.iota[:, :], iota_i[:, :]))
                do(v.tensor_copy(c.part[:, :], part_i[:, :]))
                do(v.tensor_scalar(c.ident[:, :], c.iota[:, :], c.part[:, :], None, ALU.is_equal))
                do(v.tensor_copy(c.ident16[:, :], c.ident[:, :]))
                do(v.tensor_scalar(c.below[:, :], c.iota[:, :], c.part[:, :], None, ALU.is_gt))


def slot_tables(nc, c):
    with ExitStack() as ctx:
        def sb(name, shape, dt=F32):
            return ctx.enter_context(nc.sbuf_tensor(name, shape, dt))
        names = ["dst", "src", "t3", "t8"]
        raw = {n: sb("raw_" + n, [JP, JC, P], I32) for n in names + ["before", "after"]}
        flt = {n: sb("flt_" + n, [JP, JC, P]) for n in names + ["before", "after"]}
        low = sb("low", [JP, NODE_TILES])
        trash = sb("trash", [JP, JC * P])
        key = sb("key", [128, NODE_TILES])
        key_i = sb("key_i", [128, NODE_TILES], I32)
        border_i = sb("border_i", [128, SLOTS], I32)
        border = sb("border", [128, SLOTS])
        slot_i = sb("slot_i", [128, SLOTS], I32)
        tile = sb("tile", [128, SLOTS])
        edge_tile = sb("edge_tile", [128, SLOTS])
        row_i = sb("row_i", [128, JC], I32)
        row_f = sb("row_f", [128, JC])
        pick = sb("pick", [JP, JC, SLOTS])
        dst_s, kv_f, t3_s = sb("dst_s", [P, SLOTS]), sb("kv_f", [P, SLOTS]), sb("t3_s", [P, SLOTS])
        load, pool_done, dve = c.sem("edge_loads"), c.sem("slot_iotas"), c.sem("slot_chain")
        blank, low_ready, low_sum, pick_ready, picked, used = (
            c.sem(n) for n in ("neighbours_blank", "low_ready", "low_sum", "pick_ready", "picked", "pick_copied"))

        def edges(a):
            return a.rearrange("(c p e) -> p c e", c=JC, p=JP)

        with nc.Block() as block:
            @block.sync
            def _(sp):
                for n, a in (("dst", c.dst), ("src", c.src), ("t3", c.t3), ("t8", c.t8)):
                    sp.dma_start(raw[n][:, :, :], edges(a)).then_inc(load, 16)
                sp.wait_ge(blank, 2)
                flat = c.dst.rearrange("(a e) -> a e", a=1)
                b, a = raw["before"], raw["after"]
                sp.dma_start(b[0:1, 0, 1:P], flat[:, 0:P - 1]).then_inc(load, 16)
                sp.dma_start(a[JP - 1:JP, JC - 1, 0:P - 1], flat[:, E - P + 1:E]).then_inc(load, 16)
                for k in range(JC):
                    e0 = k * JP * P
                    r0 = 1 if k == 0 else 0
                    sp.dma_start(b[r0:JP, k, :], c.dst[e0 + r0 * P - 1:e0 + JP * P - 1]
                                 .rearrange("(p e) -> p e", e=P)).then_inc(load, 16)
                    r1 = JP - 1 if k == JC - 1 else JP
                    sp.dma_start(a[0:r1, k, :], c.dst[e0 + 1:e0 + r1 * P + 1]
                                 .rearrange("(p e) -> p e", e=P)).then_inc(load, 16)

            @block.gpsimd
            def _(pool):
                pool.iota(border_i[:, :], [[P, SLOTS]], base=P, channel_multiplier=0).then_inc(pool_done, 1)
                pool.iota(slot_i[:, :], [[1, SLOTS]], base=0, channel_multiplier=0).then_inc(pool_done, 1)
                pool.iota(row_i[:, :], [[JP, JC]], base=0, channel_multiplier=1).then_inc(pool_done, 1)
                pool.iota(key_i[:, :], [[P, NODE_TILES]], base=0, channel_multiplier=0).then_inc(pool_done, 1)

            @block.vector
            def _(v):
                do = Chain(v, dve)
                v.memset(raw["before"][:, :, :], -1).then_inc(blank, 1)
                v.memset(raw["after"][:, :, :], -1).then_inc(blank, 1)
                v.wait_ge(load, 16 * (6 + 2 * JC))
                for n in raw:
                    do(v.tensor_copy(flt[n][:, :, :], raw[n][:, :, :]))
                flat = flt["dst"][:, :, :].rearrange("p c e -> p (c e)")
                do(v.memset(low[:, 0:1], 0.0))
                for t in range(1, NODE_TILES):
                    ins = v.tensor_scalar(trash[:, :], flat, float(P * t), 0.0, ALU.is_lt, ALU.add,
                                          accum_out=low[:, t:t + 1])
                    do(ins)
                v.sem_inc(low_ready, 1)
                for n in ("before", "after"):
                    do(v.tensor_tensor(flt[n][:, :, :], flt["dst"][:, :, :], flt[n][:, :, :], ALU.is_equal))
                    do(v.tensor_scalar(flt[n][:, :, :], flt[n][:, :, :], -1.0, 1.0, ALU.mult, ALU.add))
                v.wait_ge(pool_done, 4)
                do(v.tensor_copy(border[:, :], border_i[:, :]))
                do(v.tensor_copy(edge_tile[:, :], slot_i[:, :]))
                do(v.tensor_copy(row_f[:, :], row_i[:, :]))
                do(v.tensor_copy(key[:, :], key_i[:, :]))
                v.wait_ge(low_sum, 1)
                do(v.scalar_tensor_tensor(out=key[:, :], in0=c.ps[0][:, 0:NODE_TILES], scalar=float(E - 1),
                                          in1=key[:, :], op0=ALU.min, op1=ALU.add))
                do(v.memset(tile[:, :], 0.0))
                for t in range(1, NODE_TILES):
                    do(v.scalar_tensor_tensor(out=tile[:, :], in0=border[:, :], scalar=key[:, t:t + 1],
                                              in1=tile[:, :], op0=ALU.is_gt, op1=ALU.add))
                do(v.tensor_tensor(edge_tile[:, :], edge_tile[:, :], tile[:, :], ALU.subtract))
                do(v.tensor_copy(c.tile_row[0:1, :], tile[0:1, :]))
                do(v.tensor_scalar(trash[0:1, 0:SLOTS], edge_tile[0:1, :], float(EDGE_TILES - 1), None, ALU.min))
                do(v.tensor_copy(c.edge_row[0:1, :], trash[0:1, 0:SLOTS]))
                for k in range(JC):
                    do(v.tensor_scalar(pick[:, k, :], edge_tile[0:JP, :], row_f[0:JP, k:k + 1], None, ALU.is_equal))
                v.sem_inc(pick_ready, 1)

                def taken(n):
                    v.wait_ge(picked, n + 1)
                    return c.ps[n % 8][0:P, 0:SLOTS]
                do(v.tensor_copy(dst_s[:, :], taken(0)))
                do(v.scalar_tensor_tensor(out=c.dloc[:, :], in0=tile[0:P, :], scalar=-float(P), in1=dst_s[:, :],
                                          op0=ALU.mult, op1=ALU.add))
                do(v.tensor_copy(kv_f[:, :], taken(1)))
                do(v.tensor_copy(c.src_idx[:, :], kv_f[:, :]))
                do(v.scalar_tensor_tensor(out=kv_f[:, :], in0=taken(3), scalar=float(N), in1=kv_f[:, :],
                                          op0=ALU.mult, op1=ALU.add))
                do(v.tensor_copy(c.kv_idx[:, :], kv_f[:, :]))
                do(v.tensor_copy(t3_s[:, :], taken(2)))
                for r in range(REL3):
                    do(v.tensor_scalar(c.edge_cols[:, :, HEADS + 1 + r], t3_s[:, :], float(r), None, ALU.is_equal))
                    do(v.tensor_copy(c.rel_cols[:, :, r], c.edge_cols[:, :, HEADS + 1 + r]))
                do(v.memset(c.edge_cols[:, :, HEADS], 1.0))
                do(v.tensor_scalar(c.valid[:, :], c.dloc[:, :], float(P - 1), None, ALU.is_le))
                do(v.scalar_tensor_tensor(out=c.valid[:, :], in0=c.dloc[:, :], scalar=0.0, in1=c.valid[:, :],
                                          op0=ALU.is_ge, op1=ALU.mult))
                for n, flag in ((4, c.starts), (5, c.ends)):
                    do(v.tensor_tensor(flag[:, :], taken(n), c.valid[:, :], ALU.mult))
                    do(v.tensor_scalar(flag[:, :], flag[:, :], -BIG, None, ALU.mult))

            @block.tensor
            def _(pe):
                pe.wait_ge(low_ready, 1)
                pe.matmul(c.ps[0][:, 0:NODE_TILES], c.ones[0:JP, :], low[:, :], start=True,
                          stop=True).then_inc(low_sum, 1)
                pe.wait_ge(pick_ready, 1)
                for n, name in enumerate(names + ["before", "after"]):
                    for k in range(JC):
                        mm = pe.matmul(c.ps[n % 8][0:P, 0:SLOTS], flt[name][:, k, :], pick[:, k, :],
                                       start=(k == 0), stop=(k == JC - 1))
                    mm.then_inc(picked, 1)


def project(nc, c):
    with ExitStack() as ctx:
        def sb(name, shape, dt=F32):
            return ctx.enter_context(nc.sbuf_tensor(name, shape, dt))
        w = {n: sb("w_" + n, [128, NTYPES, KC, D]) for n in "qkv"}
        rel = {n: sb("rel_" + n, [128, RELS, KC, 128]) for n in ("att", "msg")}
        pri = sb("pri", [128, RELS, HEADS])
        xt = sb("xt", [128, KC, N])
        xm = sb("xm", [128, 2, NTYPES, KC, P])
        kvt = sb("kvt", [128, 2, 2, KC, P])
        stage = sb("stage", [P, 2, RELS, 2 * D])
        load, cleared, dve, xm_ready, proj, proj_out, rel_mm, rel_act, rel_dve, rel_w = (
            c.sem(n) for n in ("proj_loads", "rel_cleared", "proj_chain", "masked_x", "projected", "proj_copied",
                               "related", "related_by_act", "related_by_dve", "rel_weights"))
        stored = [c.sem("kv_stored0"), c.sem("kv_stored1")]

        with nc.Block() as block:
            @block.sync
            def _(sp):
                sp.dma_start(xt[:, :, :], c.xT.rearrange("(c p) n -> p c n", p=128)).then_inc(load, 16)
                sp.dma_start(c.type_row[:, :], c.node_type.partition_broadcast(128)).then_inc(load, 16)
                sp.dma_start(pri[:, :, :], c.pri.partition_broadcast(128)).then_inc(load, 16)
                for n, a in (("q", c.wq), ("k", c.wk), ("v", c.wv)):
                    sp.dma_start(w[n][:, :, :, :], a.rearrange("t (c p) o -> p t c o", p=128)).then_inc(load, 16)
                sp.wait_ge(cleared, 2)
                for n, a in (("att", c.attT), ("msg", c.msg)):
                    for h in range(HEADS):
                        lo = h % 2 * DK
                        sp.dma_start(rel[n][lo:lo + DK, :, h // 2, lo:lo + DK],
                                     a[:, h].rearrange("r e d -> e r d")).then_inc(load, 16)

                def body(t, b, uses):
                    sp.wait_ge(rel_act, 4 * t + 4)
                    sp.wait_ge(rel_dve, 4 * t + 4)
                    for k, table in enumerate((c.key_table, c.msg_table)):
                        to = table.rearrange("(r n) d -> n r d", r=RELS)
                        to = to[t * P:(t + 1) * P] if isinstance(t, int) else to[ds(t * P, P)]
                        sp.dma_start(to, stage[:, b, :, k * D:(k + 1) * D]).then_inc(stored[b], 16)
                by_tiles(sp, body)
                sp.wait_ge(stored[0], 32 * 13)
                sp.wait_ge(stored[1], 32 * 12)

            @block.vector
            def _(v):
                do = Chain(v, dve)
                for n in rel:
                    v.memset(rel[n][:, :, :, :], 0.0).then_inc(cleared, 1)
                v.wait_ge(load, 16 * 14)
                do(v.tensor_scalar(pri[:, :, :], pri[:, :, :], DK ** -0.5, None, ALU.mult))
                for h in range(HEADS):
                    lo = h % 2 * DK
                    blk = rel["att"][:, :, h // 2, lo:lo + DK]
                    do(v.tensor_tensor(blk, blk, pri[:, :, h:h + 1].to_broadcast([128, RELS, DK]), ALU.mult))
                v.sem_inc(rel_w, 1)

                def body(t, b, uses):
                    if known(t, 2):
                        v.wait_ge(proj, t - 1)
                    for y in range(NTYPES):
                        at = slice(t * P, (t + 1) * P) if isinstance(t, int) else ds(t * P, P)
                        m = v.scalar_tensor_tensor(
                            out=xm[:, b, y], in0=c.type_row[:, at].unsqueeze(1).to_broadcast([128, KC, P]),
                            scalar=float(y), in1=xt[:, :, at], op0=ALU.is_equal, op1=ALU.mult)
                    m.then_inc(xm_ready, 1)
                    for r in range(1, RELS, 2):
                        v.wait_ge(rel_mm, RELS * t + r + 1)
                        if r == 1 and known(t, 2):
                            v.wait_ge(stored[b], 32 * uses)
                        v.tensor_copy(stage[:, b, r, :], c.ps[3 + r % 4][0:P, :]).then_inc(rel_dve, 1)
                by_tiles(v, body)

            @block.scalar
            def _(a):
                def body(t, b, uses):
                    a.wait_ge(proj, t + 1)
                    tile = slice(t, t + 1) if isinstance(t, int) else ds(t, 1)
                    a.copy(c.nodes_b[:, tile, :], c.ps[0][0:P, 0:D].unsqueeze(1)).then_inc(proj_out, 1)
                    if known(t, 2):
                        a.wait_ge(rel_mm, RELS * (t - 1))
                    for k in range(2):
                        a.copy(kvt[:, b, k], c.ps[1 + k][:, 0:KC * P].rearrange("p (c n) -> p c n", c=KC))\
                            .then_inc(proj_out, 1)
                    for r in range(0, RELS, 2):
                        a.wait_ge(rel_mm, RELS * t + r + 1)
                        if r == 0 and known(t, 2):
                            a.wait_ge(stored[b], 32 * uses)
                        a.copy(stage[:, b, r, :], c.ps[3 + r % 4][0:P, :]).then_inc(rel_act, 1)
                by_tiles(a, body)

            @block.tensor
            def _(pe):
                def body(t, b, uses):
                    pe.wait_ge(xm_ready, t + 1)
                    if known(t, 1):
                        pe.wait_ge(proj_out, 3 * t)
                    steps = [(y, k) for y in range(NTYPES) for k in range(KC)]
                    for i, (y, k) in enumerate(steps):
                        pe.matmul(c.ps[0][0:P, 0:D], xm[:, b, y, k, :], w["q"][:, y, k, :], start=(i == 0),
                                  stop=(i == len(steps) - 1))
                    for n, name in enumerate("kv"):
                        for o in range(KC):
                            for i, (y, k) in enumerate(steps):
                                mm = pe.matmul(c.ps[1 + n][:, o * P:(o + 1) * P],
                                               w[name][:, y, k, o * 128:(o + 1) * 128], xm[:, b, y, k, :],
                                               start=(i == 0), stop=(i == len(steps) - 1))
                    mm.then_inc(proj, 1)
                    pe.wait_ge(proj_out, 3 * t + 3)
                    if isinstance(t, int) and t == 0:
                        pe.wait_ge(rel_w, 1)
                    for r in range(RELS):
                        if known(t, 1) or r >= 4:
                            pe.wait_ge((rel_act, rel_dve)[r % 2], 4 * t + r // 2 - 1)
                        for n, name in enumerate(("att", "msg")):
                            for o in range(KC):
                                mm = pe.matmul(c.ps[3 + r % 4][0:P, n * D + o * 128:n * D + (o + 1) * 128],
                                               kvt[:, b, n, o, :], rel[name][:, r, o, :], start=True, stop=True)
                        mm.then_inc(rel_mm, 1)
                pe.wait_ge(load, 16 * 14)
                by_tiles(pe, body)


def gather_rows(pool, c, rows, ring, ring_used, copied, table, width, filled, let_go):
    def body(s, i):
        for r in range(RING):
            if known(s, 1):
                pool.wait_ge(ring_used, s + r - RING + 1)
                pool.sem_inc(let_go, 1)
            if r % HALF == 0:
                pool.wait_ge(copied, 2 * i + r // HALF + 1)
                pool.sem_inc(let_go, 1)
            pool.indirect_dma_start(ring[:, r, :], None, table,
                                    bass.IndirectOffsetOnAxis(rows[:, r:r + 1], 0)).then_inc(filled[r], 16)
    by_slots(pool, body)


def copy_rows_half(a, s, i, h, c, table, rows, ring_used, copied):
    if known(s, 1):
        a.wait_ge(ring_used, s - RING + HALF * h + HALF)
    a.copy(rows[:, HALF * h:HALF * (h + 1)], col(table, s + HALF * h, HALF)).then_inc(copied, 1)


def attention_scores(nc, c):
    with ExitStack() as ctx:
        def sb(name, shape, dt=F32):
            return ctx.enter_context(nc.sbuf_tensor(name, shape, dt))
        keys = sb("keys", [P, RING, D])
        rows = sb("rows_a", [P, RING], I32)
        hot = sb("hot16", [P, RING, P], BF16)
        hot_t = sb("hot_t", [P, 2, P])
        prod = sb("prod", [P, 2, D])
        filled = [c.sem(f"keys_in{r}") for r in range(RING)]
        copied, let_go, hot_ready, turned, hot_t_ready, q_ready, prod_done, scored = (
            c.sem(n) for n in ("rows_copied_a", "pool_seen_a", "hot_ready_a", "turned_a", "hot_t_ready", "q_ready",
                               "prod_done", "scored"))
        with nc.Block() as block:
            @block.gpsimd
            def _(pool):
                gather_rows(pool, c, rows, keys, prod_done, copied, c.key_table, D, filled, let_go)

            @block.scalar
            def _(a):
                def body(s, i):
                    for h in range(2):
                        copy_rows_half(a, s, i, h, c, c.kv_idx, rows, prod_done, copied)
                    for r in range(RING):
                        a.wait_ge(turned, s + r + 1)
                        if known(s, 1) or r >= 2:
                            a.wait_ge(q_ready, s + r - 1)
                        a.copy(hot_t[:, r % 2, :], c.ps[r % 2][:, :].bitcast(BF16)[0:P, 0:P]).then_inc(hot_t_ready, 1)
                by_slots(a, body)

            @block.tensor
            def _(pe):
                def turn(s, r):
                    pe.wait_ge(hot_ready, s + r + 1)
                    if known(s, 1) or r >= 2:
                        pe.wait_ge(hot_t_ready, s + r - 1)
                    pe.transpose(c.ps[r % 2][:, :].bitcast(BF16)[0:P, 0:P], hot[:, r, :],
                                 c.ident16[0:P, 0:P]).then_inc(turned, 1)

                def body(s, i):
                    turn(s, 0)
                    turn(s, 1)
                    for r in range(RING):
                        t = pe.value_load(col(c.tile_row, s + r), min_val=0, max_val=NODE_TILES - 1)
                        pe.wait_ge(hot_t_ready, s + r + 1)
                        if known(s, 1) or r >= 2:
                            pe.wait_ge(prod_done, s + r - 1)
                        pe.matmul(c.ps[2 + r % 2][0:P, 0:D], hot_t[:, r % 2, :],
                                  c.nodes_b[:, ds(t, 1), :].rearrange("p a d -> p (a d)"), start=True,
                                  stop=True).then_inc(q_ready, 1)
                        if r + 2 < RING:
                            turn(s, r + 2)
                by_slots(pe, body)

            @block.vector
            def _(v):
                def body(s, i):
                    for r in range(RING):
                        if known(s, 1):
                            v.wait_ge(turned, s + r - RING + 1)
                        v.tensor_scalar(hot[:, r, :], c.iota[0:P, 0:P], col(c.dloc, s + r), None,
                                        ALU.is_equal).then_inc(hot_ready, 1)
                    for r in range(RING):
                        v.wait_ge(q_ready, s + r + 1)
                        v.wait_ge(filled[r], 16 * (i + 1))
                        if known(s, 1) or r >= 2:
                            v.wait_ge(scored, s + r - 1)
                        v.tensor_tensor(prod[:, r % 2, :], keys[:, r, :], c.ps[2 + r % 2][0:P, 0:D],
                                        ALU.mult).then_inc(prod_done, 1)
                        v.wait_ge(prod_done, s + r + 1)
                        to = c.score[:, s + r, :] if isinstance(s, int) else \
                            c.score[:, ds(s + r, 1), :].rearrange("p a h -> p (a h)")
                        v.tensor_reduce(to, prod[:, r % 2, :].rearrange("p (h d) -> p h d", h=HEADS), AX,
                                        ALU.add).then_inc(scored, 1)
                by_slots(v, body)


def segment_softmax(nc, c):
    with ExitStack() as ctx:
        def sb(name, shape, dt=F32):
            return ctx.enter_context(nc.sbuf_tensor(name, shape, dt))
        CH = HEADS * SCAN_C
        L = SCAN_S * P
        turned = sb("turned", [SLOT_P, HEADS + 2, SLOT_C, P])
        seq, fwd, bwd = sb("seq", [CH, L]), sb("fwd", [CH, L]), sb("bwd", [CH, L])
        reset = {n: sb("reset_" + n, [CH, L]) for n in ("start", "end")}
        ends2 = sb("ends2", [CH, 2])
        row = sb("row", [1, 2, CH])
        carry_row = sb("carry_row", [1, CH + 2])
        carry = sb("carry", [CH, 1])
        dve, pe_s, mm_done, out_t, dma_o, dma_i, ready = (
            c.sem(n) for n in ("softmax_chain", "softmax_turned", "softmax_mm", "seq_copied", "seq_stored",
                               "seq_loaded", "seq_ready"))
        n_turn = (HEADS + 2) * SLOT_C

        with nc.Block() as block:
            @block.vector
            def _(v):
                do = Chain(v, dve)
                valid = c.valid[:, :].unsqueeze(2).to_broadcast([P, SLOTS, HEADS])
                do(v.tensor_tensor(c.score[:, :, :], c.score[:, :, :], valid, ALU.mult))
                do(v.tensor_scalar(c.valid[:, :], c.valid[:, :], BIG, -BIG, ALU.mult, ALU.add))
                do(v.tensor_tensor(c.score[:, :, :], c.score[:, :, :], valid, ALU.add))
                v.sem_inc(ready, 1)
                for n in range(n_turn):
                    v.wait_ge(pe_s, n + 1)
                    v.tensor_copy(turned[:, n // SLOT_C, n % SLOT_C, :],
                                  c.ps[n % 8][0:SLOT_P, 0:P]).then_inc(out_t, 1)

                def scan(src, out, flags, step, at_last):
                    view = (lambda a: a[:, ::step])
                    do(v.tensor_tensor_scan(view(out), view(flags), view(src), -BIG, ALU.add, ALU.max))
                    do(v.tensor_copy(ends2[:, 0:1], out[:, at_last:at_last + 1]))
                    do(v.tensor_reduce(ends2[:, 1:2], flags[:, :], AX, ALU.min))
                    v.sem_inc(ready, 1)
                    turn = 0 if step == 1 else 1
                    v.wait_ge(mm_done, 3 * turn + 2)
                    for k in range(2):
                        do(v.tensor_copy(row[0:1, k, :], c.ps[k][0:1, 0:CH]))
                    do(v.memset(carry_row[0:1, :], -BIG))
                    mid = carry_row[0:1, 1:CH + 1]
                    do(v.tensor_tensor_scan(mid[:, ::step], row[0:1, 1, ::step], row[0:1, 0, ::step], -BIG,
                                            ALU.add, ALU.max))
                    v.sem_inc(ready, 1)
                    v.wait_ge(mm_done, 3 * turn + 3)
                    do(v.tensor_copy(carry[:, :], c.ps[2][0:CH, 0:1]))
                    do(v.tensor_tensor_scan(view(out), view(flags), view(src), carry[:, :], ALU.add, ALU.max))
                v.wait_ge(dma_i, 16 * (1 + 2 * HEADS))
                scan(seq, fwd, reset["start"], 1, L - 1)
                scan(fwd, bwd, reset["end"], -1, 0)
                v.sem_inc(ready, 1)
                for n in range(HEADS * SLOT_C):
                    h, k = n // SLOT_C, n % SLOT_C
                    v.wait_ge(pe_s, n_turn + n + 1)
                    at = c.score[:, k * SLOT_P:(k + 1) * SLOT_P, h]
                    v.tensor_tensor(at, at, c.ps[n % 8][0:P, 0:SLOT_P], ALU.subtract).then_inc(out_t, 1)

            @block.tensor
            def _(pe):
                pe.wait_ge(ready, 1)
                for n in range(n_turn):
                    a, k = n // SLOT_C, n % SLOT_C
                    if n >= 8:
                        pe.wait_ge(out_t, n - 7)
                    src = c.score[:, k * SLOT_P:(k + 1) * SLOT_P, a] if a < HEADS else \
                        (c.starts, c.ends)[a - HEADS][:, k * SLOT_P:(k + 1) * SLOT_P]
                    pe.transpose(c.ps[n % 8][0:SLOT_P, 0:P], src, c.ident[0:P, 0:P]).then_inc(pe_s, 1)
                pe.wait_ge(out_t, n_turn)
                for turn in range(2):
                    step = 1 if turn == 0 else -1
                    pe.wait_ge(ready, 2 + 2 * turn)
                    for k in range(2):
                        pe.transpose(c.ps[k][0:1, 0:CH], ends2[:, k:k + 1], c.ident[0:CH, 0:CH]).then_inc(mm_done, 1)
                    pe.wait_ge(ready, 3 + 2 * turn)
                    at = 1 - step
                    pe.transpose(c.ps[2][0:CH, 0:1], carry_row[0:1, at:at + CH],
                                 c.ident[0:1, 0:1]).then_inc(mm_done, 1)
                pe.wait_ge(ready, 6)
                pe.wait_ge(dma_i, 16 * (1 + 2 * HEADS + 1))
                for n in range(HEADS * SLOT_C):
                    if n >= 8:
                        pe.wait_ge(out_t, n_turn + n - 7)
                    pe.transpose(c.ps[n % 8][0:P, 0:SLOT_P], turned[:, n // SLOT_C, n % SLOT_C, :],
                                 c.ident[0:SLOT_P, 0:SLOT_P]).then_inc(pe_s, 1)

            @block.sync
            def _(sp):
                sp.wait_ge(out_t, n_turn)
                for a in range(HEADS + 2):
                    sp.dma_start(c.seq_dram[a].rearrange("(k p) e -> p k e", p=SLOT_P),
                                 turned[:, a]).then_inc(dma_o, 16)
                sp.wait_ge(dma_o, 16 * (HEADS + 2))
                chunks = "(c s) e -> c (s e)"
                sp.dma_start(seq[:, :], c.seq_dram[0:HEADS].rearrange("h (c s) e -> (h c) (s e)", s=SCAN_S))\
                    .then_inc(dma_i, 16)
                for h in range(HEADS):
                    for k, n in enumerate(("start", "end")):
                        sp.dma_start(reset[n][h * SCAN_C:(h + 1) * SCAN_C, :],
                                     c.seq_dram[HEADS + k].rearrange(chunks, s=SCAN_S)).then_inc(dma_i, 16)
                sp.wait_ge(ready, 6)
                sp.dma_start(c.max_dram.rearrange("h (c s) e -> (h c) (s e)", s=SCAN_S), bwd[:, :]).then_inc(dma_o, 16)
                sp.wait_ge(dma_o, 16 * (HEADS + 3))
                sp.dma_start(turned[:, 0:HEADS].rearrange("p h k e -> p (h k) e"),
                             c.max_dram.rearrange("h (k p) e -> p (h k) e", p=SLOT_P)).then_inc(dma_i, 16)

            @block.scalar
            def _(a):
                a.wait_ge(out_t, n_turn + HEADS * SLOT_C)
                a.activation(c.edge_cols[:, :, 0:HEADS], c.score[:, :, :], ACT.Exp).then_inc(dma_o, 1)


def weighted_messages(nc, c):
    W = D + EXTRA
    with ExitStack() as ctx:
        def sb(name, shape, dt=F32):
            return ctx.enter_context(nc.sbuf_tensor(name, shape, dt))
        got = sb("got_b", [P, RING, D])
        rows = sb("rows_b", [P, RING], I32)
        hot = sb("hot_b", [P, RING, P])
        msg = sb("msg_b", [P, 2, D])
        filled = [c.sem(f"msgs_in{r}") for r in range(RING)]
        copied, let_go, hot_ready, weighted, summed, added = (
            c.sem(n) for n in ("rows_copied_b", "pool_seen_b", "hot_ready_b", "weighted", "summed_b", "added_b"))
        clear = c.sem("acc_clear_b")
        with nc.Block() as block:
            @block.gpsimd
            def _(pool):
                gather_rows(pool, c, rows, got, weighted, copied, c.msg_table, D, filled, let_go)

            @block.scalar
            def _(a):
                def body(s, i):
                    for h in range(2):
                        copy_rows_half(a, s, i, h, c, c.kv_idx, rows, weighted, copied)
                by_slots(a, body)

            @block.tensor
            def _(pe):
                def body(s, i):
                    for r in range(RING):
                        pe.wait_ge(weighted, s + r + 1)
                        pe.wait_ge(hot_ready, s + r + 1)
                        if known(s, 1) or r >= 2:
                            pe.wait_ge(added, s + r - 1)
                        pe.matmul(c.ps[r % 2][0:P, 0:D], hot[:, r, :], msg[:, r % 2, :], start=True, stop=True)
                        cols = c.edge_cols[:, s + r, :] if isinstance(s, int) else \
                            c.edge_cols[:, ds(s + r, 1), :].rearrange("p a h -> p (a h)")
                        pe.matmul(c.ps[r % 2][0:P, D:W], hot[:, r, :], cols, start=True, stop=True)\
                            .then_inc(summed, 1)
                by_slots(pe, body)

            @block.vector
            def _(v):
                v.memset(c.acc[:, :, :], 0.0).then_inc(clear, 1)
                v.wait_ge(clear, 1)

                def add(s, r):
                    t = v.value_load(col(c.tile_row, s + r), min_val=0, max_val=NODE_TILES - 1)
                    v.wait_ge(summed, s + r + 1)
                    if known(s, 1) or r >= 1:
                        v.wait_ge(added, s + r)
                    to = c.acc[:, ds(t, 1), 0:W]
                    v.tensor_tensor(to, to, c.ps[r % 2][0:P, 0:W].unsqueeze(1), ALU.add).then_inc(added, 1)

                def body(s, i):
                    for r in range(RING):
                        if known(s, 1):
                            v.wait_ge(summed, s + r - RING + 1)
                        v.tensor_scalar(hot[:, r, :], c.iota[0:P, 0:P], col(c.dloc, s + r), None,
                                        ALU.is_equal).then_inc(hot_ready, 1)
                    for r in range(RING):
                        v.wait_ge(filled[r], 16 * (i + 1))
                        if known(s, 1) or r >= 2:
                            v.wait_ge(summed, s + r - 1)
                        cols = c.edge_cols[:, s + r, 0:HEADS] if isinstance(s, int) else \
                            c.edge_cols[:, ds(s + r, 1), 0:HEADS].rearrange("p a h -> p (a h)")
                        v.tensor_tensor(msg[:, r % 2, :].rearrange("p (h d) -> p h d", h=HEADS),
                                        got[:, r, :].rearrange("p (h d) -> p h d", h=HEADS),
                                        cols.unsqueeze(2).to_broadcast([P, HEADS, DK]), ALU.mult)\
                            .then_inc(weighted, 1)
                        if r:
                            add(s, r - 1)
                    add(s, RING - 1)
                by_slots(v, body)


def attention_output(nc, c):
    with ExitStack() as ctx:
        def sb(name, shape, dt=F32):
            return ctx.enter_context(nc.sbuf_tensor(name, shape, dt))
        wa = sb("wa", [128, NTYPES, KC, D])
        am = sb("am", [128, 2, NTYPES, KC, P])
        agg = sb("agg", [P, 2, D])
        rden = sb("rden", [P, NODE_TILES, HEADS])
        skip, gate_e = sb("skip", [P, NTYPES]), sb("gate_e", [P, NTYPES])
        ntype_i, ntype = sb("ntype_i", [P, NODE_TILES], I32), sb("ntype", [P, NODE_TILES])
        gate, tmp = sb("gate", [P, NODE_TILES]), sb("gate_tmp", [P, NODE_TILES])
        load, dve, act_s, agg_ready, turned, masked, mixed, out_done = (
            c.sem(n) for n in ("att_loads", "att_chain", "att_act", "agg_ready", "agg_turned", "agg_masked",
                               "agg_mixed", "att_out"))
        with nc.Block() as block:
            @block.sync
            def _(sp):
                sp.dma_start(wa[:, :, :, :], c.wa.rearrange("t (c p) o -> p t c o", p=128)).then_inc(load, 16)
                sp.dma_start(skip[:, :], c.skip.partition_broadcast(P)).then_inc(load, 16)
                sp.dma_start(ntype_i[:, :], c.node_type_cols).then_inc(load, 16)
                sp.dma_start(c.nodes[:, :, :], c.x.rearrange("(t p) d -> p t d", p=P)).then_inc(load, 16)

            @block.scalar
            def _(a):
                a.wait_ge(load, 64)
                a.activation(gate_e[:, :], skip[:, :], ACT.Exp, scale=-1.0).then_inc(act_s, 1)
                a.wait_ge(dve, 2)
                a.activation(c.rdeg[:, :], c.cnt[:, :, 0], ACT.Sqrt).then_inc(act_s, 1)

            @block.vector
            def _(v):
                do = Chain(v, dve)
                do(v.tensor_scalar(c.cnt[:, :, :], c.acc[:, :, D + HEADS:D + EXTRA], 1.0, None, ALU.max))
                do(v.tensor_scalar(rden[:, :, :], c.acc[:, :, D:D + HEADS], 1e-30, None, ALU.max))
                do(v.reciprocal(rden[:, :, :], rden[:, :, :]))
                v.wait_ge(act_s, 2)
                do(v.reciprocal(c.rdeg[:, :], c.rdeg[:, :]))
                do(v.reciprocal(c.cnt[:, :, :], c.cnt[:, :, :]))
                do(v.tensor_scalar(gate_e[:, :], gate_e[:, :], 1.0, None, ALU.add))
                do(v.reciprocal(gate_e[:, :], gate_e[:, :]))
                do(v.tensor_copy(ntype[:, :], ntype_i[:, :]))
                do(v.memset(gate[:, :], 0.0))
                for y in range(NTYPES):
                    do(v.tensor_scalar(tmp[:, :], ntype[:, :], float(y), gate_e[:, y:y + 1], ALU.is_equal, ALU.mult))
                    do(v.tensor_tensor(gate[:, :], gate[:, :], tmp[:, :], ALU.add))

                def body(t, b, uses):
                    tile = slice(t, t + 1) if isinstance(t, int) else ds(t, 1)
                    at = slice(t * P, (t + 1) * P) if isinstance(t, int) else ds(t * P, P)
                    if known(t, 2):
                        v.wait_ge(turned, t - 1)
                    v.tensor_tensor(agg[:, b, :].rearrange("p (h d) -> p h d", h=HEADS),
                                    c.acc[:, tile, 0:D].rearrange("p a (h d) -> p (a h) d", h=HEADS),
                                    rden[:, tile, :].rearrange("p a h -> p (a h)").unsqueeze(2)
                                    .to_broadcast([P, HEADS, DK]), ALU.mult).then_inc(agg_ready, 1)
                    v.wait_ge(turned, t + 1)
                    if known(t, 2):
                        v.wait_ge(mixed, t - 1)
                    for y in range(NTYPES):
                        m = v.scalar_tensor_tensor(
                            out=am[:, b, y], in0=c.type_row[:, at].unsqueeze(1).to_broadcast([128, KC, P]),
                            scalar=float(y), in1=c.ps[b][:, 0:KC * P].rearrange("p (c n) -> p c n", c=KC),
                            op0=ALU.is_equal, op1=ALU.mult)
                    m.then_inc(masked, 1)
                    v.wait_ge(mixed, t + 1)
                    v.scalar_tensor_tensor(out=c.nodes_b[:, tile, :], in0=c.ps[2 + b][0:P, 0:D].unsqueeze(1),
                                           scalar=gate[:, tile], in1=c.nodes[:, tile, :], op0=ALU.mult,
                                           op1=ALU.add).then_inc(out_done, 1)
                by_tiles(v, body)

            @block.tensor
            def _(pe):
                pe.wait_ge(load, 64)

                def body(t, b, uses):
                    pe.wait_ge(agg_ready, t + 1)
                    if known(t, 2):
                        pe.wait_ge(masked, t - 1)
                    for k in range(KC):
                        mm = pe.transpose(c.ps[b][:, k * P:(k + 1) * P], agg[:, b, k * 128:(k + 1) * 128],
                                          c.ident[0:P, 0:P])
                    mm.then_inc(turned, 1)
                    pe.wait_ge(masked, t + 1)
                    if known(t, 2):
                        pe.wait_ge(out_done, t - 1)
                    steps = [(y, k) for y in range(NTYPES) for k in range(KC)]
                    for i, (y, k) in enumerate(steps):
                        mm = pe.matmul(c.ps[2 + b][0:P, 0:D], am[:, b, y, k, :], wa[:, y, k, :], start=(i == 0),
                                       stop=(i == len(steps) - 1))
                    mm.then_inc(mixed, 1)
                by_tiles(pe, body)


def row_norm(nc, c, name, src, to_dram, scale=None, final=False):
    with ExitStack() as ctx:
        def sb(n, shape, dt=F32):
            return ctx.enter_context(nc.sbuf_tensor(name + n, shape, dt))
        parts, mv = sb("_parts", [P, 2, 6]), sb("_mv", [P, 2, 2])
        mean, rstd = sb("_mean", [P, NODE_TILES]), sb("_rstd", [P, NODE_TILES])
        chain, seen, act_s, rows, stored = (c.sem(name + n) for n in ("_chain", "_seen", "_sqrt", "_rows", "_stored"))
        scaled = sb("_scaled", [P, NODE_TILES, D]) if scale is not None else c.nodes
        with nc.Block() as block:
            @block.vector
            def _(v):
                do = Chain(v, chain)

                def body(t, b, uses):
                    do.at(4 * t)
                    tile = slice(t, t + 1) if isinstance(t, int) else ds(t, 1)
                    do(v.bn_stats(parts[:, b, :], src[:, tile, :].rearrange("p a d -> p (a d)")))
                    v.sem_inc(seen, 1)
                    do(v.bn_aggr(mv[:, b, :], parts[:, b, :]))
                    do(v.tensor_copy(mean[:, tile], mv[:, b, 0:1]))
                    do(v.tensor_copy(rstd[:, tile], mv[:, b, 1:2]))
                by_tiles(v, body)
                do.at(4 * NODE_TILES)
                do(v.tensor_scalar(rstd[:, :], rstd[:, :], LN_EPS, None, ALU.add))
                v.wait_ge(act_s, 1)
                do(v.reciprocal(rstd[:, :], rstd[:, :]))

                def apply(t, b, uses):
                    tile = slice(t, t + 1) if isinstance(t, int) else ds(t, 1)
                    v.tensor_scalar(c.nodes[:, tile, :], src[:, tile, :], mean[:, tile], rstd[:, tile],
                                    ALU.subtract, ALU.mult).then_inc(rows, 1)
                    if scale is not None:
                        v.wait_ge(rows, 2 * t + 1)
                        v.tensor_scalar(scaled[:, tile, :], c.nodes[:, tile, :], scale[:, tile], None,
                                        ALU.mult).then_inc(rows, 1)
                by_tiles(v, apply)

            @block.scalar
            def _(a):
                a.wait_ge(chain, 4 * NODE_TILES + 1)
                a.activation(rstd[:, :], rstd[:, :], ACT.Sqrt).then_inc(act_s, 1)

            @block.sync
            def _(sp):
                sp.wait_ge(rows, NODE_TILES * (1 if scale is None else 2))
                sp.dma_start(to_dram.rearrange("(t p) d -> p t d", p=P), scaled[:, :, :]).then_inc(stored, 16)
                sp.wait_ge(stored, 16)


EXPERTS, HIDDEN, TOPK, CAP = 64, 512, 2, 1024
HC = HIDDEN // 128
ROW_TILES = N * TOPK // P
STEPS = ROW_TILES + EXPERTS - 1
WRING = 4
BN_EPS = 1e-5


def by_ring(eng, body, count, ring):
    for s in range(ring + 1):
        body(s, s % ring, s // ring)
    with eng.Fori(1, count // ring) as k:
        for i in range(ring):
            body(ring * k + 1 + i, (1 + i) % ring, k + (1 + i) // ring)


def out_degrees(nc, c):
    G = 5
    with ExitStack() as ctx:
        def sb(name, shape, dt=F32):
            return ctx.enter_context(nc.sbuf_tensor(name, shape, dt))
        src_i, lo, hi = sb("src_i", [P, EDGE_TILES], I32), sb("src_lo", [P, EDGE_TILES]), sb("src_hi", [P, EDGE_TILES])
        hot_lo, hot_hi = sb("hot_lo", [P, 2, G, P], BF16), sb("hot_hi", [P, 2, G, NODE_TILES], BF16)
        load, chain, hot_ready, counted, act_s = (
            c.sem(n) for n in ("src_load", "hist_chain", "hist_hot", "hist_counted", "hist_sqrt"))
        with nc.Block() as block:
            @block.sync
            def _(sp):
                sp.dma_start(src_i[:, :], c.src.rearrange("(p k) -> p k", p=P)).then_inc(load, 16)

            @block.vector
            def _(v):
                do = Chain(v, chain)
                v.wait_ge(load, 16)
                do(v.tensor_copy(lo[:, :], src_i[:, :]))
                do(v.memset(hi[:, :], 0.0))
                for t in range(1, NODE_TILES):
                    do(v.scalar_tensor_tensor(out=hi[:, :], in0=lo[:, :], scalar=float(P * t), in1=hi[:, :],
                                              op0=ALU.is_ge, op1=ALU.add))
                do(v.scalar_tensor_tensor(out=lo[:, :], in0=hi[:, :], scalar=-float(P), in1=lo[:, :],
                                          op0=ALU.mult, op1=ALU.add))

                def body(g, b, uses):
                    at = slice(g * G, (g + 1) * G) if isinstance(g, int) else ds(g * G, G)
                    if known(g, 2):
                        v.wait_ge(counted, g - 1)
                    for hot, digit, n in ((hot_lo, lo, P), (hot_hi, hi, NODE_TILES)):
                        v.tensor_tensor(hot[:, b], c.iota[0:P, 0:n].unsqueeze(1).to_broadcast([P, G, n]),
                                        digit[:, at].unsqueeze(2).to_broadcast([P, G, n]),
                                        ALU.is_equal).then_inc(hot_ready, 1)
                by_ring(v, body, EDGE_TILES // G, 2)
                v.wait_ge(counted, EDGE_TILES // G)
                do(v.tensor_scalar(c.rout[:, :], c.ps[0][0:P, 0:NODE_TILES], 1.0, None, ALU.max))
                v.wait_ge(act_s, 1)
                do(v.reciprocal(c.rout[:, :], c.rout[:, :]))

            @block.scalar
            def _(a):
                a.wait_ge(chain, NODE_TILES + 3)
                a.activation(c.rout[:, :], c.rout[:, :], ACT.Sqrt).then_inc(act_s, 1)

            @block.tensor
            def _(pe):
                last = EDGE_TILES // G - 1

                def body(g, b, uses):
                    pe.wait_ge(hot_ready, 2 * g + 2)
                    for k in range(G):
                        mm = pe.matmul(c.ps[0][0:P, 0:NODE_TILES], hot_lo[:, b, k, :], hot_hi[:, b, k, :],
                                       start=(isinstance(g, int) and g == 0 and k == 0), stop=True,
                                       skip_group_check=True)
                    mm.then_inc(counted, 1)
                by_ring(pe, body, EDGE_TILES // G, 2)


def graph_sum(nc, c, name, table, acc):
    banks = RING if RING <= 8 else RING // 2
    with ExitStack() as ctx:
        def sb(n, shape, dt=F32):
            return ctx.enter_context(nc.sbuf_tensor(name + n, shape, dt))
        got = sb("_got", [P, RING, D])
        rows = sb("_rows", [P, RING], I32)
        hot = sb("_hot", [P, RING, P])
        filled = [c.sem(f"{name}_in{r}") for r in range(RING)]
        copied, let_go, hot_ready, summed, added, clear = (
            c.sem(name + n) for n in ("_rows_copied", "_pool_seen", "_hot_ready", "_summed", "_added", "_clear"))
        with nc.Block() as block:
            @block.gpsimd
            def _(pool):
                gather_rows(pool, c, rows, got, summed, copied, table, D, filled, let_go)

            @block.scalar
            def _(a):
                def body(s, i):
                    for h in range(2):
                        copy_rows_half(a, s, i, h, c, c.src_idx, rows, summed, copied)
                by_slots(a, body)

            @block.tensor
            def _(pe):
                def body(s, i):
                    for r in range(RING):
                        pe.wait_ge(filled[r], 16 * (i + 1))
                        pe.wait_ge(hot_ready, s + r + 1)
                        if known(s, 1) or r >= banks:
                            pe.wait_ge(added, s + r - banks + 1)
                        pe.matmul(c.ps[r % banks][0:P, 0:D], hot[:, r, :], got[:, r, :], start=True,
                                  stop=True).then_inc(summed, 1)
                by_slots(pe, body)

            @block.vector
            def _(v):
                v.memset(acc[:, :, :], 0.0).then_inc(clear, 1)
                v.wait_ge(clear, 1)

                def body(s, i):
                    for r in range(RING):
                        if known(s, 1):
                            v.wait_ge(summed, s + r - RING + 1)
                        v.tensor_scalar(hot[:, r, :], c.iota[0:P, 0:P], col(c.dloc, s + r), None,
                                        ALU.is_equal).then_inc(hot_ready, 1)
                    for r in range(RING):
                        t = v.value_load(col(c.tile_row, s + r), min_val=0, max_val=NODE_TILES - 1)
                        v.wait_ge(summed, s + r + 1)
                        if known(s, 1) or r >= 1:
                            v.wait_ge(added, s + r)
                        to = acc[:, ds(t, 1), :]
                        v.tensor_tensor(to, to, c.ps[r % banks][0:P, 0:D].unsqueeze(1), ALU.add).then_inc(added, 1)
                by_slots(v, body)


def tile_at(t, n=1):
    return slice(t, t + n) if isinstance(t, int) else ds(t, n)


def flat(ap):
    return ap.rearrange("p a d -> p (a d)")


def conv_and_router(nc, c, acc, x1, logits):
    with ExitStack() as ctx:
        def sb(name, shape, dt=F32):
            return ctx.enter_context(nc.sbuf_tensor(name, shape, dt))
        w = sb("w_conv", [128, 2, KC, D])
        wg = sb("w_router", [128, KC, EXPERTS])
        bias, bias2, bg = sb("conv_bias", [P, D]), sb("conv_bias2", [P, D]), sb("router_bias", [P, EXPERTS])
        cat = sb("conv_cat", [P, 2, 2 * D])
        cat_t = sb("conv_t", [128, 2, 2 * KC, P])
        x1s = sb("x1s", [P, 2, D])
        x1_t = sb("x1_t", [128, 2, KC, P])
        load, chain, cat_ready, turned, t_ready, conv, x1_ready, x1_turned, x1_t_ready, routed, log_ready = (
            c.sem(n) for n in ("conv_loads", "conv_chain", "conv_cat_ready", "conv_turned", "conv_t_ready", "conv_done",
                               "x1_ready", "x1_turned", "x1_t_ready", "routed", "logits_ready"))
        copied = c.sem("conv_copied")
        with nc.Block() as block:
            @block.sync
            def _(sp):
                for k, a in enumerate((c.W_gc, c.W_res)):
                    sp.dma_start(w[:, k], a.rearrange("(c p) o -> p c o", p=128)).then_inc(load, 16)
                sp.dma_start(wg[:, :, :], c.Wg.rearrange("(c p) o -> p c o", p=128)).then_inc(load, 16)
                sp.dma_start(bias[:, :], c.b_gc.partition_broadcast(P)).then_inc(load, 16)
                sp.dma_start(bias2[:, :], c.b_res.partition_broadcast(P)).then_inc(load, 16)
                sp.dma_start(bg[:, :], c.bg.partition_broadcast(P)).then_inc(load, 16)

            @block.vector
            def _(v):
                do = Chain(v, chain)
                v.wait_ge(load, 96)
                do(v.tensor_tensor(bias[:, :], bias[:, :], bias2[:, :], ALU.add))

                def body(t, b, uses):
                    if known(t, 2):
                        v.wait_ge(turned, t - 1)
                    v.tensor_scalar(cat[:, b, 0:D], flat(acc[:, tile_at(t), :]), c.rdeg[:, tile_at(t)], None,
                                    ALU.mult).then_inc(cat_ready, 1)
                    v.wait_ge(conv, t + 1)
                    if known(t, 2):
                        v.wait_ge(x1_turned, t - 1)
                        v.wait_ge(copied, 2 * t - 2)
                    v.tensor_tensor(x1s[:, b, :], c.ps[2 + b][0:P, 0:D], bias[:, :], ALU.add).then_inc(x1_ready, 1)
                    v.wait_ge(routed, t + 1)
                    v.tensor_tensor(flat(logits[:, tile_at(t), :]), c.ps[6 + b][0:P, 0:EXPERTS], bg[:, :],
                                    ALU.add).then_inc(log_ready, 1)
                by_tiles(v, body)

            @block.scalar
            def _(a):
                def body(t, b, uses):
                    if known(t, 2):
                        a.wait_ge(turned, t - 1)
                    a.copy(cat[:, b, D:2 * D], flat(c.nodes[:, tile_at(t), :])).then_inc(copied, 1)
                    a.wait_ge(turned, t + 1)
                    if known(t, 2):
                        a.wait_ge(conv, t - 1)
                    a.copy(cat_t[:, b], c.ps[b][:, 0:2 * KC * P].rearrange("p (c n) -> p c n", n=P)).then_inc(t_ready, 1)
                    a.wait_ge(x1_turned, t + 1)
                    if known(t, 2):
                        a.wait_ge(routed, t - 1)
                    a.copy(x1_t[:, b], c.ps[4 + b][:, 0:KC * P].rearrange("p (c n) -> p c n", n=P)).then_inc(x1_t_ready, 1)
                    a.wait_ge(x1_ready, t + 1)
                    a.copy(flat(x1[:, tile_at(t), :]), x1s[:, b, :]).then_inc(copied, 1)
                by_tiles(a, body)

            @block.tensor
            def _(pe):
                pe.wait_ge(load, 96)

                def body(t, b, uses):
                    pe.wait_ge(cat_ready, t + 1)
                    pe.wait_ge(copied, 2 * t + 1)
                    if known(t, 2):
                        pe.wait_ge(t_ready, t - 1)
                    for k in range(2 * KC):
                        mm = pe.transpose(c.ps[b][:, k * P:(k + 1) * P], cat[:, b, k * 128:(k + 1) * 128],
                                          c.ident[0:P, 0:P])
                    mm.then_inc(turned, 1)
                    pe.wait_ge(t_ready, t + 1)
                    if known(t, 2):
                        pe.wait_ge(x1_ready, t - 1)
                    for k in range(2 * KC):
                        mm = pe.matmul(c.ps[2 + b][0:P, 0:D], cat_t[:, b, k, :], w[:, k // KC, k % KC, :],
                                       start=(k == 0), stop=(k == 2 * KC - 1))
                    mm.then_inc(conv, 1)
                    pe.wait_ge(x1_ready, t + 1)
                    if known(t, 2):
                        pe.wait_ge(x1_t_ready, t - 1)
                    for k in range(KC):
                        mm = pe.transpose(c.ps[4 + b][:, k * P:(k + 1) * P], x1s[:, b, k * 128:(k + 1) * 128],
                                          c.ident[0:P, 0:P])
                    mm.then_inc(x1_turned, 1)
                    pe.wait_ge(x1_t_ready, t + 1)
                    if known(t, 2):
                        pe.wait_ge(log_ready, t - 1)
                    for k in range(KC):
                        mm = pe.matmul(c.ps[6 + b][0:P, 0:EXPERTS], x1_t[:, b, k, :], wg[:, k, :],
                                       start=(k == 0), stop=(k == KC - 1))
                    mm.then_inc(routed, 1)
                by_tiles(pe, body)


def route(nc, c, x1, logits):
    with ExitStack() as ctx:
        def sb(name, shape, dt=F32):
            return ctx.enter_context(nc.sbuf_tensor(name, shape, dt))
        T, X = NODE_TILES, EXPERTS
        wide = [P, T, X]
        iota_m = sb("iota_m", [P, X])
        pick = [sb("pick0", wide), sb("pick1", wide)]
        both, before, work, run = sb("both", wide), sb("before", wide), sb("work", wide), sb("run", [P, T + 1, X])
        val = [sb("val0", [P, T]), sb("val1", [P, T])]
        idx, base, total = sb("idx", [P, T]), sb("base", [P, X]), sb("total", [P, X])
        rank, gap = sb("rank", [P, T]), sb("gap", [P, T])
        pos_f = sb("pos_f", [P, T])
        row_i, row_f = sb("row_ids_i", [P, ROW_TILES], I32), sb("row_ids", [P, ROW_TILES])
        key, key_i = sb("step_key", [P, X]), sb("step_key_i", [P, X], I32)
        lim_i, lim = sb("step_lim_i", [P, STEPS], I32), sb("step_lim", [P, STEPS])
        step_i, tile = sb("step_i", [P, STEPS], I32), sb("step_tile", [P, STEPS])
        grid = sb("grid", [P, STEPS, X])
        chain, act_s, pe_s, iotas, run_ready, pfx, rows_in, pos_ready = (
            c.sem(n) for n in ("route_chain", "route_exp", "route_mm", "route_iotas", "run_ready", "prefix_copied",
                               "rows_stored", "positions_ready"))

        def over_experts(ap):
            return ap.unsqueeze(2).to_broadcast(wide)

        def over_tiles(ap):
            return ap.unsqueeze(1).to_broadcast(wide)

        with nc.Block() as block:
            @block.gpsimd
            def _(pool):
                pool.iota(row_i[:, :], [[P, ROW_TILES]], base=0, channel_multiplier=1).then_inc(iotas, 1)
                pool.iota(key_i[:, :], [[P, X]], base=0, channel_multiplier=0).then_inc(iotas, 1)
                pool.iota(lim_i[:, :], [[P, STEPS]], base=P, channel_multiplier=0).then_inc(iotas, 1)
                pool.iota(step_i[:, :], [[1, STEPS]], base=0, channel_multiplier=0).then_inc(iotas, 1)
                pool.wait_ge(pos_ready, 1)
                for k in range(TOPK):
                    for t in range(T):
                        pool.indirect_dma_start(c.row_table, bass.IndirectOffsetOnAxis(c.pos[k][:, t:t + 1], 0),
                                                x1[:, t, :], None).then_inc(rows_in, 16)
                pool.wait_ge(rows_in, 16 * TOPK * T)

            @block.scalar
            def _(a):
                a.wait_ge(run_ready, 1)
                a.activation(gap[:, :], gap[:, :], ACT.Exp).then_inc(act_s, 1)

                def body(t, b, uses):
                    a.wait_ge(pe_s, t + 1)
                    a.copy(flat(before[:, tile_at(t), :]), c.ps[b][0:P, 0:X]).then_inc(pfx, 1)
                by_tiles(a, body)

            @block.tensor
            def _(pe):
                pe.wait_ge(run_ready, 2)

                def body(t, b, uses):
                    if known(t, 2):
                        pe.wait_ge(pfx, t - 1)
                    pe.matmul(c.ps[b][0:P, 0:X], c.below[0:P, 0:P], flat(both[:, tile_at(t), :]), start=True, stop=False)
                    pe.matmul(c.ps[b][0:P, 0:X], c.ones[0:P, 0:P], flat(run[:, tile_at(t), :]), start=False,
                              stop=True).then_inc(pe_s, 1)
                by_tiles(pe, body)
                pe.matmul(c.ps[2][0:P, 0:X], c.ones[0:P, 0:P], run[:, T, :], start=True, stop=True).then_inc(pe_s, 1)

            @block.vector
            def _(v):
                do = Chain(v, chain)
                do(v.tensor_scalar(iota_m[:, :], c.iota[0:P, 0:X], -float(X), None, ALU.add))
                for k in range(TOPK):
                    do(v.tensor_reduce(val[k][:, :], logits[:, :, :], AX, ALU.max))
                    do(v.tensor_tensor(work[:, :, :], logits[:, :, :], over_experts(val[k][:, :]), ALU.is_equal))
                    do(v.scalar_tensor_tensor(out=work[:, :, :], in0=work[:, :, :], scalar=-float(X),
                                              in1=over_tiles(c.iota[0:P, 0:X]), op0=ALU.mult, op1=ALU.add))
                    do(v.tensor_reduce(idx[:, :], work[:, :, :], AX, ALU.min))
                    do(v.tensor_tensor(pick[k][:, :, :], over_tiles(iota_m[:, :]), over_experts(idx[:, :]), ALU.is_equal))
                    if k == 0:
                        do(v.scalar_tensor_tensor(out=logits[:, :, :], in0=pick[0][:, :, :], scalar=-BIG,
                                                  in1=logits[:, :, :], op0=ALU.mult, op1=ALU.add))
                do(v.tensor_tensor(gap[:, :], val[1][:, :], val[0][:, :], ALU.subtract))
                v.sem_inc(run_ready, 1)
                do(v.tensor_tensor(both[:, :, :], pick[0][:, :, :], pick[1][:, :, :], ALU.add))
                do(v.memset(run[:, 0, :], 0.0))
                at = do.n

                def body(t, b, uses):
                    do.at(at + t)
                    n = t + 1
                    do(v.tensor_tensor(run[:, tile_at(n), :], run[:, tile_at(t), :], both[:, tile_at(t), :], ALU.add))
                by_tiles(v, body)
                do.at(at + T)
                v.sem_inc(run_ready, 1)
                v.wait_ge(act_s, 1)
                do(v.tensor_scalar(rank[:, :], gap[:, :], 1.0, None, ALU.add))
                do(v.reciprocal(c.gate[0][:, :], rank[:, :]))
                do(v.tensor_tensor(c.gate[1][:, :], gap[:, :], c.gate[0][:, :], ALU.mult))
                v.wait_ge(pe_s, T + 1)
                v.wait_ge(pfx, T)
                do(v.tensor_copy(total[:, :], c.ps[2][0:P, 0:X]))
                do(v.tensor_tensor_scan(base[:, :], c.ones[0:P, 0:X], total[:, :], 0.0, ALU.mult, ALU.add))
                do(v.tensor_tensor(base[:, :], base[:, :], total[:, :], ALU.subtract))
                for k in range(TOPK):
                    do(v.tensor_tensor(work[:, :, :], pick[k][:, :, :], before[:, :, :], ALU.mult))
                    do(v.tensor_reduce(rank[:, :], work[:, :, :], AX, ALU.add))
                    do(v.scalar_tensor_tensor(out=c.gate[k][:, :], in0=rank[:, :], scalar=float(CAP),
                                              in1=c.gate[k][:, :], op0=ALU.is_lt, op1=ALU.mult))
                    do(v.tensor_tensor(work[:, :, :], pick[k][:, :, :], over_tiles(base[:, :]), ALU.mult))
                    do(v.tensor_reduce(pos_f[:, :], work[:, :, :], AX, ALU.add))
                    do(v.tensor_tensor(pos_f[:, :], pos_f[:, :], rank[:, :], ALU.add))
                    do(v.tensor_copy(c.pos[k][:, :], pos_f[:, :]))
                v.sem_inc(pos_ready, 1)
                v.wait_ge(iotas, 4)
                for f, i in ((row_f, row_i), (key, key_i), (lim, lim_i), (tile, step_i)):
                    do(v.tensor_copy(f[:, :], i[:, :]))
                g = grid[:, 0:ROW_TILES, :]
                do(v.tensor_tensor(g, row_f[:, :].unsqueeze(2).to_broadcast([P, ROW_TILES, X]),
                                   base[:, :].unsqueeze(1).to_broadcast([P, ROW_TILES, X]), ALU.is_ge))
                do(v.tensor_reduce(c.row_expert[:, :], g, AX, ALU.add))
                do(v.tensor_scalar(c.row_expert[:, :], c.row_expert[:, :], -1.0, None, ALU.add))
                do(v.scalar_tensor_tensor(out=key[:, :], in0=base[:, :], scalar=float(ROW_TILES * P - 1), in1=key[:, :],
                                          op0=ALU.min, op1=ALU.add))
                do(v.tensor_tensor(grid[:, :, :], lim[:, :].unsqueeze(2).to_broadcast([P, STEPS, X]),
                                   key[:, :].unsqueeze(1).to_broadcast([P, STEPS, X]), ALU.is_gt))
                do(v.tensor_reduce(c.step_expert[:, :], grid[:, :, :], AX, ALU.add))
                do(v.tensor_scalar(c.step_expert[:, :], c.step_expert[:, :], -1.0, None, ALU.add))
                do(v.tensor_tensor(tile[:, :], tile[:, :], c.step_expert[:, :], ALU.subtract))
                do(v.tensor_copy(c.step_rows[0:1, 0, :], tile[0:1, :]))
                do(v.tensor_copy(c.step_rows[0:1, 1, :], c.step_expert[0:1, :]))


def experts(nc, c):
    with ExitStack() as ctx:
        def sb(name, shape, dt=F32):
            return ctx.enter_context(nc.sbuf_tensor(name, shape, dt))
        w1, w2 = sb("w1", [128, WRING, KC, HIDDEN]), sb("w2", [128, WRING, HC, D])
        b1, b2 = sb("b1", [128, WRING, HC]), sb("b2", [1, WRING, D])
        xr = sb("xr", [P, WRING, D])
        xt = sb("xr_t", [128, 2, KC, P])
        h = sb("hidden", [128, 2, HC, P])
        mask = sb("row_mask", [P, 2, 1])
        y = sb("expert_rows", [P, ROW_TILES, D])
        loaded = [c.sem(f"weights_in{b}") for b in range(WRING)]
        turned, xt_ready, up, act_s, down, kept, mask_s, clear, stored, seen = (
            c.sem(n) for n in ("rows_turned", "rows_t_ready", "up_done", "gelu_done", "down_done", "rows_kept",
                               "row_mask_ready", "rows_clear", "expert_rows_stored", "expert_seen"))
        with nc.Block() as block:
            @block.sync
            def _(sp):
                def body(s, b, uses):
                    j = sp.value_load(c.step_rows[0:1, 0, tile_at(s)], min_val=0, max_val=ROW_TILES - 1)
                    e = sp.value_load(c.step_rows[0:1, 1, tile_at(s)], min_val=0, max_val=EXPERTS - 1)
                    if known(s, WRING):
                        sp.wait_ge(down, s - WRING + 1)
                    sp.dma_start(xr[:, b, :], c.row_table[ds(j * P, P), :]).then_inc(loaded[b], 16)
                    sp.dma_start(w1[:, b], c.w1[ds(e, 1)].rearrange("a (c p) h -> p (a c) h", p=128)).then_inc(loaded[b], 16)
                    sp.dma_start(b1[:, b, :], c.b1[ds(e, 1)].rearrange("a p c -> (a p) c")).then_inc(loaded[b], 16)
                    sp.dma_start(w2[:, b], c.w2[ds(e, 1)].rearrange("a (c p) h -> p (a c) h", p=128)).then_inc(loaded[b], 16)
                    sp.dma_start(b2[:, b, :], c.b2[ds(e, 1)]).then_inc(loaded[b], 16)
                by_ring(sp, body, STEPS, WRING)
                sp.wait_ge(kept, STEPS)
                sp.dma_start(c.expert_table.rearrange("(j p) d -> p j d", p=P), y[:, :, :]).then_inc(stored, 16)
                sp.wait_ge(stored, 16)

            @block.tensor
            def _(pe):
                def down_layer(s, b):
                    pe.wait_ge(act_s, HC * s + HC)
                    if known(s, 2):
                        pe.wait_ge(kept, s - 1)
                    for m in range(HC):
                        pe.matmul(c.ps[4 + b % 2][0:P, 0:D], h[:, b % 2, m, :], w2[:, b, m, :], start=(m == 0), stop=False)
                    pe.matmul(c.ps[4 + b % 2][0:P, 0:D], c.ones[0:1, 0:P], b2[:, b, :], start=False,
                              stop=True).then_inc(down, 1)

                def body(s, b, uses):
                    pe.wait_ge(loaded[b], 80 * (uses + 1))
                    if known(s, 2):
                        pe.wait_ge(xt_ready, s - 1)
                    for k in range(KC):
                        mm = pe.transpose(c.ps[b % 2][:, k * P:(k + 1) * P], xr[:, b, k * 128:(k + 1) * 128],
                                          c.ident[0:P, 0:P])
                    mm.then_inc(turned, 1)
                    pe.wait_ge(xt_ready, s + 1)
                    if known(s, 2):
                        pe.wait_ge(act_s, HC * s - HC)
                    for m in range(HC):
                        for k in range(KC):
                            mm = pe.matmul(c.ps[2 + b % 2][:, m * P:(m + 1) * P], w1[:, b, k, m * 128:(m + 1) * 128],
                                           xt[:, b % 2, k, :], start=(k == 0), stop=(k == KC - 1))
                    mm.then_inc(up, 1)
                    if known(s, 1):
                        down_layer(s - 1, (b - 1) % WRING)
                by_ring(pe, body, STEPS, WRING)
                down_layer(STEPS - 1, (STEPS - 1) % WRING)

            @block.scalar
            def _(a):
                def body(s, b, uses):
                    a.wait_ge(up, s + 1)
                    if known(s, 2):
                        a.wait_ge(down, s - 1)
                    for m in range(HC):
                        a.activation(h[:, b % 2, m, :], c.ps[2 + b % 2][:, m * P:(m + 1) * P], ACT.Gelu,
                                     bias=b1[:, b, m:m + 1]).then_inc(act_s, 1)
                by_ring(a, body, STEPS, WRING)

            @block.vector
            def _(v):
                v.memset(y[:, :, :], 0.0).then_inc(clear, 1)
                v.wait_ge(clear, 1)

                def keep(s, b):
                    j = v.value_load(c.step_rows[0:1, 0, tile_at(s)], min_val=0, max_val=ROW_TILES - 1)
                    if known(s, 1):
                        v.wait_ge(kept, s)
                    v.tensor_scalar(mask[:, b % 2, :], c.row_expert[:, ds(j, 1)], c.step_expert[:, tile_at(s)], None,
                                    ALU.is_equal).then_inc(mask_s, 1)
                    v.wait_ge(mask_s, s + 1)
                    v.wait_ge(down, s + 1)
                    to = y[:, ds(j, 1), :]
                    v.scalar_tensor_tensor(out=to, in0=c.ps[4 + b % 2][0:P, 0:D].unsqueeze(1), scalar=mask[:, b % 2, :],
                                           in1=to, op0=ALU.mult, op1=ALU.add).then_inc(kept, 1)

                def body(s, b, uses):
                    v.wait_ge(turned, s + 1)
                    if known(s, 2):
                        v.wait_ge(up, s - 1)
                    v.tensor_copy(xt[:, b % 2], c.ps[b % 2][:, 0:KC * P].rearrange("p (c n) -> p c n", n=P)).then_inc(xt_ready, 1)
                    if known(s, 1):
                        keep(s - 1, (b - 1) % WRING)
                by_ring(v, body, STEPS, WRING)
                keep(STEPS - 1, (STEPS - 1) % WRING)


def combine(nc, c, x1):
    with nc.sbuf_tensor("chosen0", [P, NODE_TILES, D], F32) as y0, nc.sbuf_tensor("chosen1", [P, NODE_TILES, D], F32) as y1:
        G = 5
        got = [c.sem(f"chosen_in{g}") for g in range(NODE_TILES // G)]
        added = c.sem("chosen_added")
        with nc.Block() as block:
            @block.gpsimd
            def _(pool):
                for t in range(NODE_TILES):
                    for k, y in enumerate((y0, y1)):
                        pool.indirect_dma_start(y[:, t, :], None, c.expert_table,
                                                bass.IndirectOffsetOnAxis(c.pos[k][:, t:t + 1], 0)).then_inc(got[t // G], 16)

            @block.vector
            def _(v):
                for t in range(NODE_TILES):
                    if t % G == 0:
                        v.wait_ge(got[t // G], 16 * G * TOPK)
                    for k, y in enumerate((y0, y1)):
                        if t or k:
                            v.wait_ge(added, 2 * t + k)
                        v.scalar_tensor_tensor(out=x1[:, t, :], in0=y[:, t, :], scalar=c.gate[k][:, t:t + 1],
                                               in1=x1[:, t, :], op0=ALU.mult, op1=ALU.add).then_inc(added, 1)


def batch_norm(nc, c, name, y, gamma, beta):
    with ExitStack() as ctx:
        def sb(n, shape, dt=F32):
            return ctx.enter_context(nc.sbuf_tensor(name + n, shape, dt))
        g, be = sb("_gamma", [P, D]), sb("_beta", [P, D])
        mean, rstd = sb("_mean", [P, D]), sb("_rstd", [P, D])
        sq = sb("_sq", [P, NODE_TILES, D])
        load, chain, mm, act_s = (c.sem(name + n) for n in ("_loads", "_chain", "_sums", "_act"))
        wide = [P, NODE_TILES, D]

        def over_tiles(ap):
            return ap.unsqueeze(1).to_broadcast(wide)
        with nc.Block() as block:
            @block.sync
            def _(sp):
                sp.dma_start(g[:, :], gamma.partition_broadcast(P)).then_inc(load, 16)
                sp.dma_start(be[:, :], beta.partition_broadcast(P)).then_inc(load, 16)

            @block.tensor
            def _(pe):
                for k, src in enumerate((y, sq)):
                    if k:
                        pe.wait_ge(act_s, 1)
                    for t in range(NODE_TILES):
                        m = pe.matmul(c.ps[k][0:P, 0:D], c.ones[0:P, 0:P], src[:, t, :], start=(t == 0),
                                      stop=(t == NODE_TILES - 1))
                    m.then_inc(mm, 1)

            @block.scalar
            def _(a):
                a.wait_ge(chain, 2)
                a.activation(sq[:, :, :], y[:, :, :], ACT.Square).then_inc(act_s, 1)
                a.wait_ge(chain, 3)
                a.activation(rstd[:, :], rstd[:, :], ACT.Sqrt).then_inc(act_s, 1)

            @block.vector
            def _(v):
                do = Chain(v, chain)
                v.wait_ge(mm, 1)
                do(v.tensor_scalar(mean[:, :], c.ps[0][0:P, 0:D], 1.0 / N, None, ALU.mult))
                do(v.tensor_tensor(y[:, :, :], y[:, :, :], over_tiles(mean[:, :]), ALU.subtract))
                v.wait_ge(mm, 2)
                do(v.tensor_scalar(rstd[:, :], c.ps[1][0:P, 0:D], 1.0 / N, BN_EPS, ALU.mult, ALU.add))
                v.wait_ge(act_s, 2)
                do(v.reciprocal(rstd[:, :], rstd[:, :]))
                v.wait_ge(load, 32)
                do(v.tensor_tensor(rstd[:, :], rstd[:, :], g[:, :], ALU.mult))
                do(v.tensor_tensor(y[:, :, :], y[:, :, :], over_tiles(rstd[:, :]), ALU.mult))
                do(v.tensor_tensor(y[:, :, :], y[:, :, :], over_tiles(be[:, :]), ALU.add))
                do(v.tensor_tensor(y[:, :, :], y[:, :, :], c.nodes[:, :, :], ALU.add))


def linear(nc, c, acc, y):
    with ExitStack() as ctx:
        def sb(name, shape, dt=F32):
            return ctx.enter_context(nc.sbuf_tensor(name, shape, dt))
        w, bias = sb("w_lin", [128, KC, D]), sb("lin_bias", [P, D])
        hs, ht = sb("lin_h", [P, 2, D]), sb("lin_ht", [128, 2, KC, P])
        load, ready, turned, t_ready, mixed, out = (
            c.sem(n) for n in ("lin_loads", "lin_h_ready", "lin_turned", "lin_t_ready", "lin_mixed", "lin_out"))
        with nc.Block() as block:
            @block.sync
            def _(sp):
                sp.dma_start(w[:, :, :], c.w_linT.rearrange("(c p) o -> p c o", p=128)).then_inc(load, 16)
                sp.dma_start(bias[:, :], c.b_lin.partition_broadcast(P)).then_inc(load, 16)

            @block.vector
            def _(v):
                v.wait_ge(load, 32)

                def last(t, b):
                    v.wait_ge(mixed, t + 1)
                    v.tensor_tensor(flat(y[:, tile_at(t), :]), c.ps[2 + b][0:P, 0:D], bias[:, :], ALU.add).then_inc(out, 1)

                def body(t, b, uses):
                    if known(t, 2):
                        v.wait_ge(turned, t - 1)
                    v.tensor_tensor(hs[:, b, :], flat(acc[:, tile_at(t), :]), flat(c.nodes[:, tile_at(t), :]),
                                    ALU.add).then_inc(ready, 1)
                    if known(t, 1):
                        last(t - 1, 1 - b)
                by_tiles(v, body)
                last(NODE_TILES - 1, (NODE_TILES - 1) % 2)

            @block.scalar
            def _(a):
                def body(t, b, uses):
                    a.wait_ge(turned, t + 1)
                    if known(t, 2):
                        a.wait_ge(mixed, t - 1)
                    a.copy(ht[:, b], c.ps[b][:, 0:KC * P].rearrange("p (c n) -> p c n", n=P)).then_inc(t_ready, 1)
                by_tiles(a, body)

            @block.tensor
            def _(pe):
                pe.wait_ge(load, 32)

                def body(t, b, uses):
                    pe.wait_ge(ready, t + 1)
                    if known(t, 2):
                        pe.wait_ge(t_ready, t - 1)
                    for k in range(KC):
                        mm = pe.transpose(c.ps[b][:, k * P:(k + 1) * P], hs[:, b, k * 128:(k + 1) * 128], c.ident[0:P, 0:P])
                    mm.then_inc(turned, 1)
                    pe.wait_ge(t_ready, t + 1)
                    if known(t, 2):
                        pe.wait_ge(out, t - 1)
                    for k in range(KC):
                        mm = pe.matmul(c.ps[2 + b][0:P, 0:D], ht[:, b, k, :], w[:, k, :], start=(k == 0), stop=(k == KC - 1))
                    mm.then_inc(mixed, 1)
                by_tiles(pe, body)


def relation_pass(nc, c, name, table, acc):
    ATTRS = 32
    with ExitStack() as ctx:
        def sb(n, shape, dt=F32):
            return ctx.enter_context(nc.sbuf_tensor(name + n, shape, dt))
        got = sb("_got", [P, RING, D])
        rows = sb("_rows", [P, RING], I32)
        hot = sb("_hot", [P, RING, P])
        attr = sb("_attr", [ATTRS + 1, RING, P])
        ew = sb("_ew", [ATTRS + 1, D])
        prod = sb("_prod", [P, 2, D])
        msg = sb("_msg", [P, 2, REL3, D])
        filled = [c.sem(f"{name}_in{r}") for r in range(RING)]
        attr_in = [c.sem(f"{name}_attr_in{r}") for r in range(RING)]
        (load, copied, let_go, hot_ready, scaled, prod_done, split, summed, added, clear, seen) = (
            c.sem(name + n) for n in ("_loads", "_rows_copied", "_pool_seen", "_hot_ready", "_edge_scale", "_prod_done",
                                      "_split", "_summed", "_added", "_clear", "_act_seen"))
        with nc.Block() as block:
            @block.gpsimd
            def _(pool):
                gather_rows(pool, c, rows, got, prod_done, copied, table, D, filled, let_go)

            @block.sync
            def _(sp):
                sp.dma_start(ew[0:ATTRS, :], c.edge_w).then_inc(load, 16)
                sp.dma_start(ew[ATTRS:ATTRS + 1, :], c.edge_b).then_inc(load, 16)

                def body(s, i):
                    for r in range(RING):
                        j = sp.value_load(col(c.edge_row, s + r), min_val=0, max_val=EDGE_TILES - 1)
                        if known(s, 1):
                            sp.wait_ge(scaled, s + r - RING + 1)
                        sp.dma_start(attr[0:ATTRS, r, :], c.attrT[ds(j, 1)].rearrange("a k e -> (a k) e"))                            .then_inc(attr_in[r], 16)
                by_slots(sp, body)

            @block.scalar
            def _(a):
                def body(s, i):
                    for h in range(2):
                        copy_rows_half(a, s, i, h, c, c.src_idx, rows, prod_done, copied)
                    for r in range(RING):
                        a.wait_ge(prod_done, s + r + 1)
                        if known(s, 1) or r >= 2:
                            a.wait_ge(summed, s + r - 1)
                        a.sem_inc(seen, 1)
                        for k in range(REL3):
                            flag = c.rel_cols[:, s + r, k:k + 1] if isinstance(s, int) else                                 c.rel_cols[:, ds(s + r, 1), k]
                            a.activation(msg[:, r % 2, k, :], prod[:, r % 2, :], ACT.Relu, scale=flag).then_inc(split, 1)
                by_slots(a, body)

            @block.tensor
            def _(pe):
                def scale(s, r, i):
                    pe.wait_ge(attr_in[r], 16 * (i + 1))
                    if known(s, 1) or r >= 2:
                        pe.wait_ge(prod_done, s + r - 1)
                    pe.matmul(c.ps[4 + r % 2][0:P, 0:D], attr[:, r, :], ew[:, :], start=True, stop=True).then_inc(scaled, 1)

                def body(s, i):
                    scale(s, 0, i)
                    scale(s, 1, i)
                    for r in range(RING):
                        pe.wait_ge(split, REL3 * (s + r + 1))
                        pe.wait_ge(hot_ready, s + r + 1)
                        if known(s, 1) or r >= 2:
                            pe.wait_ge(added, s + r - 1)
                        m = msg[:, r % 2].rearrange("p k d -> p (k d)")
                        pe.matmul(c.pair[r % 2][0:P, 0:2 * D], hot[:, r, :], m[:, 0:2 * D], start=True, stop=True)
                        pe.matmul(c.pair[r % 2][0:P, 2 * D:3 * D], hot[:, r, :], m[:, 2 * D:3 * D], start=True,
                                  stop=True).then_inc(summed, 1)
                        if r + 2 < RING:
                            scale(s, r + 2, i)
                pe.wait_ge(load, 32)
                pe.wait_ge(clear, 2)
                by_slots(pe, body)

            @block.vector
            def _(v):
                v.memset(attr[ATTRS:ATTRS + 1, :, :], 1.0).then_inc(clear, 1)
                v.memset(acc[:, :, :, :], 0.0).then_inc(clear, 1)
                v.wait_ge(clear, 2)

                def add(s, r):
                    t = v.value_load(col(c.tile_row, s + r), min_val=0, max_val=NODE_TILES - 1)
                    v.wait_ge(summed, s + r + 1)
                    if known(s, 1) or r >= 1:
                        v.wait_ge(added, s + r)
                    to = acc[:, ds(t, 1)].rearrange("p a k d -> p (a k d)")
                    v.tensor_tensor(to, to, c.pair[r % 2][0:P, 0:REL3 * D], ALU.add).then_inc(added, 1)

                def body(s, i):
                    for r in range(RING):
                        if known(s, 1):
                            v.wait_ge(summed, s + r - RING + 1)
                        v.tensor_scalar(hot[:, r, :], c.iota[0:P, 0:P], col(c.dloc, s + r), None,
                                        ALU.is_equal).then_inc(hot_ready, 1)
                    for r in range(RING):
                        v.wait_ge(scaled, s + r + 1)
                        v.wait_ge(filled[r], 16 * (i + 1))
                        if known(s, 1) or r >= 2:
                            v.wait_ge(split, REL3 * (s + r - 1))
                        v.tensor_tensor(prod[:, r % 2, :], got[:, r, :], c.ps[4 + r % 2][0:P, 0:D],
                                        ALU.mult).then_inc(prod_done, 1)
                        if r:
                            add(s, r - 1)
                    add(s, RING - 1)
                by_slots(v, body)


def relation_mix(nc, c, name, layer, acc, x_table):
    K = (REL3 + 1) * KC
    with ExitStack() as ctx:
        def sb(n, shape, dt=F32):
            return ctx.enter_context(nc.sbuf_tensor(name + n, shape, dt))
        w, bias = sb("_w", [128, REL3 + 1, KC, D]), sb("_bias", [P, D])
        cat, cat_t = sb("_cat", [P, 2, REL3 + 1, D]), sb("_cat_t", [128, 2, K, P])
        pre = sb("_pre", [P, 2, D])
        load, ready, turned, t_ready, mixed, pre_s, act_s, out, stored = (
            c.sem(name + n) for n in ("_loads", "_cat_ready", "_turned", "_t_ready", "_mixed", "_pre_ready", "_copied",
                                      "_out", "_stored"))
        with nc.Block() as block:
            @block.sync
            def _(sp):
                sp.dma_start(w[:, 0:REL3], c.weights[layer].rearrange("r (c p) o -> p r c o", p=128)).then_inc(load, 16)
                sp.dma_start(w[:, REL3], c.roots[layer].rearrange("(c p) o -> p c o", p=128)).then_inc(load, 16)
                sp.dma_start(bias[:, :], c.biases[layer].partition_broadcast(P)).then_inc(load, 16)
                if x_table is not None:
                    sp.wait_ge(out, NODE_TILES)
                    sp.dma_start(x_table.rearrange("(t p) d -> p t d", p=P), c.nodes[:, :, :]).then_inc(stored, 16)
                    sp.wait_ge(stored, 16)

            @block.vector
            def _(v):
                v.wait_ge(load, 48)

                def last(t, b):
                    v.wait_ge(mixed, t + 1)
                    v.tensor_tensor(pre[:, b, :], c.ps[4 + b][0:P, 0:D], bias[:, :], ALU.add).then_inc(pre_s, 1)
                    v.wait_ge(pre_s, t + 1)
                    x = flat(c.nodes[:, tile_at(t), :])
                    v.scalar_tensor_tensor(out=x, in0=pre[:, b, :], scalar=0.0, in1=x, op0=ALU.max,
                                           op1=ALU.add).then_inc(out, 1)

                def body(t, b, uses):
                    if known(t, 2):
                        v.wait_ge(turned, t - 1)
                    v.tensor_tensor(cat[:, b, 0:REL3, :], acc[:, tile_at(t)].rearrange("p a k d -> p (a k) d"),
                                    flat(c.cnt[:, tile_at(t), 1:1 + REL3]).unsqueeze(2).to_broadcast([P, REL3, D]),
                                    ALU.mult).then_inc(ready, 1)
                    if known(t, 1):
                        last(t - 1, 1 - b)
                by_tiles(v, body)
                last(NODE_TILES - 1, (NODE_TILES - 1) % 2)

            @block.scalar
            def _(a):
                def body(t, b, uses):
                    if known(t, 2):
                        a.wait_ge(turned, t - 1)
                    a.copy(cat[:, b, REL3, :], flat(c.nodes[:, tile_at(t), :])).then_inc(act_s, 1)
                    a.wait_ge(turned, t + 1)
                    if known(t, 2):
                        a.wait_ge(mixed, t - 1)
                    a.copy(cat_t[:, b].rearrange("p (g k) n -> p g (k n)", g=2),
                           c.pair[b][:, :].rearrange("p (g k) -> p g k", g=2)[:, :, 0:K // 2 * P]).then_inc(t_ready, 1)
                by_tiles(a, body)

            @block.tensor
            def _(pe):
                pe.wait_ge(load, 48)

                def body(t, b, uses):
                    pe.wait_ge(ready, t + 1)
                    pe.wait_ge(act_s, t + 1)
                    if known(t, 2):
                        pe.wait_ge(t_ready, t - 1)
                    for k in range(K):
                        at = 512 * (k // (K // 2)) + k % (K // 2) * P
                        mm = pe.transpose(c.pair[b][:, at:at + P], cat[:, b, k // KC, k % KC * 128:(k % KC + 1) * 128],
                                          c.ident[0:P, 0:P])
                    mm.then_inc(turned, 1)
                    pe.wait_ge(t_ready, t + 1)
                    if known(t, 2):
                        pe.wait_ge(pre_s, t - 1)
                    for k in range(K):
                        mm = pe.matmul(c.ps[4 + b][0:P, 0:D], cat_t[:, b, k, :], w[:, k // KC, k % KC, :],
                                       start=(k == 0), stop=(k == K - 1))
                    mm.then_inc(mixed, 1)
                by_tiles(pe, body)


def program(nc, c):
    outer = ExitStack()
    with outer:
        c.in_use = []

        def sem(name):
            c.in_use.append(nc.alloc_semaphore(name))
            return c.in_use[-1]
        c.sem = sem
        c.pair = [outer.enter_context(nc.psum_tensor(f"banks{k}", [128, 1024], F32)) for k in range(4)]
        c.ps = [c.pair[k // 2][:, k % 2 * 512:(k % 2 + 1) * 512] for k in range(8)]
        c.iota = outer.enter_context(nc.sbuf_tensor("iota", [128, 128], F32))
        c.part = outer.enter_context(nc.sbuf_tensor("part", [128, 1], F32))
        c.ident = outer.enter_context(nc.sbuf_tensor("ident", [128, 128], F32))
        c.ident16 = outer.enter_context(nc.sbuf_tensor("ident16", [128, 128], BF16))
        c.ones = outer.enter_context(nc.sbuf_tensor("ones", [128, 128], F32))
        c.below = outer.enter_context(nc.sbuf_tensor("below", [128, 128], F32))
        c.tile_row = outer.enter_context(nc.sbuf_tensor("tile_row", [1, SLOTS], I32))
        c.edge_row = outer.enter_context(nc.sbuf_tensor("edge_row", [1, SLOTS], I32))
        c.dloc = outer.enter_context(nc.sbuf_tensor("dloc", [P, SLOTS], F32))
        c.src_idx = outer.enter_context(nc.sbuf_tensor("src_idx", [P, SLOTS], I32))
        c.cnt = outer.enter_context(nc.sbuf_tensor("cnt", [P, NODE_TILES, 1 + REL3], F32))
        c.rdeg = outer.enter_context(nc.sbuf_tensor("rdeg", [P, NODE_TILES], F32))
        c.nodes = outer.enter_context(nc.sbuf_tensor("nodes", [P, NODE_TILES, D], F32))
        c.nodes_b = outer.enter_context(nc.sbuf_tensor("nodes_b", [P, NODE_TILES, D], F32))
        c.key_table = nc.dram_tensor("key_table", (RELS * N, D), F32, kind="Internal").ap()
        c.msg_table = nc.dram_tensor("msg_table", (RELS * N, D), F32, kind="Internal").ap()
        c.seq_dram = nc.dram_tensor("seq_dram", (HEADS + 2, SLOTS, P), F32, kind="Internal").ap()
        c.max_dram = nc.dram_tensor("max_dram", (HEADS, SLOTS, P), F32, kind="Internal").ap()

        c.x_table = [nc.dram_tensor(f"x_table{k}", (N, D), F32, kind="Internal").ap() for k in range(5)]
        c.row_table = nc.dram_tensor("row_table", (N * TOPK, D), F32, kind="Internal").ap()
        c.expert_table = nc.dram_tensor("expert_table", (N * TOPK, D), F32, kind="Internal").ap()
        c.rout = outer.enter_context(nc.sbuf_tensor("rout", [P, NODE_TILES], F32))
        c.rel_cols = outer.enter_context(nc.sbuf_tensor("rel_cols", [P, SLOTS, REL3], F32))

        constants(nc, c)
        out_degrees(nc, c)
        with ExitStack() as layer0:
            c.kv_idx = layer0.enter_context(nc.sbuf_tensor("kv_idx", [P, SLOTS], I32))
            c.valid = layer0.enter_context(nc.sbuf_tensor("valid", [P, SLOTS], F32))
            c.starts = layer0.enter_context(nc.sbuf_tensor("starts", [P, SLOTS], F32))
            c.ends = layer0.enter_context(nc.sbuf_tensor("ends", [P, SLOTS], F32))
            c.edge_cols = layer0.enter_context(nc.sbuf_tensor("edge_cols", [P, SLOTS, EXTRA], F32))
            c.type_row = layer0.enter_context(nc.sbuf_tensor("type_row", [128, N], I32))
            slot_tables(nc, c)
            project(nc, c)
            c.score = layer0.enter_context(nc.sbuf_tensor("score", [P, SLOTS, HEADS], F32))
            attention_scores(nc, c)
            segment_softmax(nc, c)
            c.acc = layer0.enter_context(nc.sbuf_tensor("acc0", [P, NODE_TILES, D + EXTRA], F32))
            weighted_messages(nc, c)
            attention_output(nc, c)
        row_norm(nc, c, "norm0", c.nodes_b, c.x_table[0], scale=c.rout)
        clear_semaphores(nc, c)

        with ExitStack() as layer1:
            x1 = c.nodes_b
            logits = layer1.enter_context(nc.sbuf_tensor("logits", [P, NODE_TILES, EXPERTS], F32))
            with nc.sbuf_tensor("acc1", [P, NODE_TILES, D], F32) as acc:
                graph_sum(nc, c, "sum1", c.x_table[0], acc)
                conv_and_router(nc, c, acc, x1, logits)
            c.gate = [layer1.enter_context(nc.sbuf_tensor(f"gate{k}", [P, NODE_TILES], F32)) for k in range(TOPK)]
            c.pos = [layer1.enter_context(nc.sbuf_tensor(f"pos{k}", [P, NODE_TILES], I32)) for k in range(TOPK)]
            c.row_expert = layer1.enter_context(nc.sbuf_tensor("row_expert", [P, ROW_TILES], F32))
            c.step_expert = layer1.enter_context(nc.sbuf_tensor("step_expert", [P, STEPS], F32))
            c.step_rows = layer1.enter_context(nc.sbuf_tensor("step_rows", [1, 2, STEPS], I32))
            route(nc, c, x1, logits)
            experts(nc, c)
            combine(nc, c, x1)
            batch_norm(nc, c, "bn1", x1, c.gamma, c.beta)
        row_norm(nc, c, "norm1", c.nodes_b, c.x_table[1])
        clear_semaphores(nc, c)

        with nc.sbuf_tensor("acc2", [P, NODE_TILES, D], F32) as acc:
            graph_sum(nc, c, "sum2", c.x_table[1], acc)
            linear(nc, c, acc, c.nodes_b)
        batch_norm(nc, c, "bn2", c.nodes_b, c.bn_w, c.bn_b)
        row_norm(nc, c, "norm2", c.nodes_b, c.x_table[2])

        clear_semaphores(nc, c)

        keep_input(nc, c)
        for layer in range(3):
            with nc.sbuf_tensor(f"acc3_{layer}", [P, NODE_TILES, REL3, D], F32) as acc:
                relation_pass(nc, c, f"rel{layer}", c.x_table[2 + layer], acc)
                relation_mix(nc, c, f"mix{layer}", layer, acc, c.x_table[3 + layer] if layer < 2 else None)
        add_input(nc, c)
        row_norm(nc, c, "norm3", c.nodes_b, c.out)


def clear_semaphores(nc, c):
    nc.all_engine_barrier()
    nc.clear_and_free_semaphores(c.in_use)
    c.in_use.clear()
    nc.all_engine_barrier()


def keep_input(nc, c):
    done = c.sem("input_kept")
    with nc.Block() as block:
        @block.vector
        def _(v):
            v.tensor_copy(c.nodes_b[:, :, :], c.nodes[:, :, :]).then_inc(done, 1)


def add_input(nc, c):
    done = c.sem("input_added")
    with nc.Block() as block:
        @block.vector
        def _(v):
            v.tensor_tensor(c.nodes_b[:, :, :], c.nodes_b[:, :, :], c.nodes[:, :, :], ALU.add).then_inc(done, 1)


_INS = {
    "x": ("x", lambda a: a), "xT": ("x", lambda a: a.T), "src": ("src", lambda a: a), "dst": ("dst", lambda a: a),
    "t3": ("edge_type_3", lambda a: a), "t8": ("edge_type_8", lambda a: a),
    "node_type": ("node_type_4", lambda a: a), "node_type_cols": ("node_type_4", lambda a: a.reshape(NODE_TILES, P).T),
    "wq": ("L0_gnn_q_linears", lambda a: a), "wk": ("L0_gnn_k_linears", lambda a: a),
    "wv": ("L0_gnn_v_linears", lambda a: a), "wa": ("L0_gnn_a_linears", lambda a: a),
    "attT": ("L0_gnn_relation_att", lambda a: a.transpose(0, 1, 3, 2)), "msg": ("L0_gnn_relation_msg", lambda a: a),
    "pri": ("L0_gnn_relation_pri", lambda a: a), "skip": ("L0_gnn_skip", lambda a: a),
    "W_gc": ("L1_gnn_W_gc", lambda a: a), "W_res": ("L1_gnn_W_res", lambda a: a), "b_gc": ("L1_gnn_b_gc", lambda a: a),
    "b_res": ("L1_gnn_b_res", lambda a: a), "Wg": ("L1_gnn_Wg", lambda a: a), "bg": ("L1_gnn_bg", lambda a: a),
    "w1": ("L1_gnn_w1", lambda a: a), "b1": ("L1_gnn_b1", lambda a: a.reshape(EXPERTS, HC, 128).transpose(0, 2, 1)),
    "w2": ("L1_gnn_w2", lambda a: a), "b2": ("L1_gnn_b2", lambda a: a), "gamma": ("L1_gnn_gamma", lambda a: a),
    "beta": ("L1_gnn_beta", lambda a: a), "w_linT": ("L2_gnn_W", lambda a: a.T), "b_lin": ("L2_gnn_b", lambda a: a),
    "bn_w": ("L2_gnn_bn_w", lambda a: a), "bn_b": ("L2_gnn_bn_b", lambda a: a),
    "weights": ("L3_gnn_weights", lambda a: a), "roots": ("L3_gnn_roots", lambda a: a),
    "biases": ("L3_gnn_biases", lambda a: a), "edge_w": ("L3_gnn_edge_w", lambda a: a),
    "edge_b": ("L3_gnn_edge_b", lambda a: a.reshape(1, D)),
    "attrT": ("edge_attr_32", lambda a: a.reshape(EDGE_TILES, P, 32).transpose(0, 2, 1)),
}


def kernel(**inputs):
    import numpy as _np
    import concourse.bacc as _bacc
    from concourse import mybir as _mybir
    from concourse.bass_utils import run_bass_kernel_spmd as _run

    nc = _bacc.Bacc("TRN2", target_bir_lowering=False, num_devices=1)
    c = Core()
    arrays = {}
    for name, (arg, lay) in _INS.items():
        a = _np.ascontiguousarray(lay(_np.asarray(inputs[arg])))
        arrays[f"in_{name}"] = a
        c.__dict__[name] = nc.dram_tensor(f"in_{name}", a.shape, _mybir.dt.from_np(a.dtype), kind="ExternalInput").ap()
    c.out = nc.dram_tensor("out_x", (N, D), F32, kind="ExternalOutput").ap()
    program(nc, c)
    r = _run(nc, [arrays], core_ids=[0])
    return r.results[0]["out_x"]
```

```python
from contextlib import ExitStack

import concourse.bass as bass
from concourse import mybir

F32 = mybir.dt.float32
BF16 = mybir.dt.bfloat16
I32 = mybir.dt.int32
I16 = mybir.dt.int16
ALU = mybir.AluOpType
ACT = mybir.ActivationFunctionType
AX = mybir.AxisListType.X

N, E, D = 3125, 53125, 256
P = 125
NODE_TILES = N // P
EDGE_TILES = E // P
RING = 10
SLOTS = -(-(EDGE_TILES + NODE_TILES - 1) // RING) * RING
ROUNDS = SLOTS // RING
GROUP = 2
BUFS = RING // 2
AHEAD = 2
WIN, WINS = 42, -(-N // 42)
ROW16 = 16
NEAR = 8
IOTA = max(128, 3 * WIN)
WSLOTS = -(-(EDGE_TILES + WINS - 1) // RING) * RING
JC, JP = 5, EDGE_TILES // 5
KC = D // 128
HEADS, DK = 4, 64
NTYPES, RELS, REL3 = 4, 8, 3
ATTRS = 32
EXTRA = 8
SCAN_C = 25
SCAN_S = SLOTS // SCAN_C
SLOT_C, SLOT_P = 5, SLOTS // 5
BIG = 1e30
LN_EPS = 1e-5


def ds(i, n):
    return bass.ds(i, n)


class Chain:

    def __init__(self, eng, sem):
        self.eng, self.sem, self.base, self.n = eng, sem, 0, 0

    def at(self, base):
        self.base, self.n = base, 0

    def __call__(self, ins):
        self.n += 1
        ins.then_inc(self.sem, 1)
        self.eng.wait_ge(self.sem, self.base + self.n)


def known(t, at_least):
    return not isinstance(t, int) or t >= at_least


def by_tiles(eng, body):
    for t in range(3):
        body(t, t % 2, t // 2)
    with eng.Fori(1, NODE_TILES // 2) as k:
        body(2 * k + 1, 1, k)
        body(2 * k + 2, 0, k + 1)


def by_slots(eng, body, slots=SLOTS):
    body(0, 0)
    with eng.Fori(1, slots // RING - 1) as i:
        body(i * RING, i)
    body(slots - RING, slots // RING - 1)


def before_end(s, r, ahead, slots=SLOTS):
    return not isinstance(s, int) or s + r + ahead < slots


def col(table, s, n=1):
    return table[:, s:s + n] if isinstance(s, int) else table[:, ds(s, n)]


class Rows:

    def __init__(self, eng, name, table, limit):
        self.eng, self.table, self.limit = eng, table, limit
        self.regs = [eng.alloc_register(f"{name}{r}") for r in range(RING)]
        self.values = [None] * RING

    def load(self, i, lo, hi):
        at = self.table[0:1, i:i + 1, lo:hi] if isinstance(i, int) else self.table[0:1, ds(i, 1), lo:hi]
        self.eng.load(self.regs[lo:hi], at)
        for r in range(lo, hi):
            self.values[r] = self.eng.snap(self.regs[r], min_val=0, max_val=self.limit)

    def at(self, i, r):
        if r in (0, NEAR):
            self.load(i, r, NEAR if r == 0 else RING)
        return self.values[r]

    def free(self):
        for reg in self.regs:
            self.eng.free_register(reg)


class Core:
    pass


def constants(nc, c):
    with nc.sbuf_tensor("iota_i", [128, IOTA], I32) as iota_i, nc.sbuf_tensor("part_i", [128, 1], I32) as part_i:
        made, dve = c.sem("iota_made"), c.sem("const_chain")
        with nc.Block() as block:
            @block.gpsimd
            def _(pool):
                pool.iota(iota_i[:, :], [[1, IOTA]], base=0, channel_multiplier=0).then_inc(made, 1)
                pool.iota(part_i[:, :], [[0, 1]], base=0, channel_multiplier=1).then_inc(made, 1)

            @block.vector
            def _(v):
                do = Chain(v, dve)
                do(v.memset(c.ones[:, :], 1.0))
                v.wait_ge(made, 2)
                do(v.tensor_copy(c.iota[:, :], iota_i[:, :]))
                do(v.tensor_copy(c.part[:, :], part_i[:, :]))
                do(v.tensor_scalar(c.ident[:, :], c.iota[:, 0:128], c.part[:, :], None, ALU.is_equal))
                do(v.tensor_copy(c.ident16[:, :], c.ident[:, :]))
                do(v.tensor_scalar(c.below[:, :], c.iota[:, 0:128], c.part[:, :], None, ALU.is_gt))


def slot_tables(nc, c):
    with ExitStack() as ctx:
        def sb(name, shape, dt=F32):
            return ctx.enter_context(nc.sbuf_tensor(name, shape, dt))
        names = ["dst", "src", "t3", "t8"]
        raw = {n: sb("raw_" + n, [JP, JC, P], I32) for n in names + ["before", "after"]}
        flt = {n: sb("flt_" + n, [JP, JC, P]) for n in names + ["before", "after"]}
        tmp = sb("clipped", [1, WSLOTS])
        border_i, border = sb("border_i", [JP, WINS], I32), sb("border", [JP, WINS])
        past = sb("past", [JP, JC, WINS])
        key = sb("key", [WINS, 1])
        slot_i, slot = sb("slot_i", [128, WSLOTS], I32), sb("slot", [128, WSLOTS])
        passed = sb("passed", [WINS, WSLOTS])
        tile = sb("tile", [128, WSLOTS])
        edge_tile = sb("edge_tile", [128, WSLOTS])
        row_i = sb("row_i", [128, JC], I32)
        row_f = sb("row_f", [128, JC])
        pick = sb("pick", [JP, JC, WSLOTS])
        dst_s, val = sb("dst_s", [P, WSLOTS]), sb("val_s", [P, WSLOTS])
        load, pool_done, dve = c.sem("edge_loads"), c.sem("slot_iotas"), c.sem("slot_chain")
        blank, ask, mm_done, picked = (c.sem(n) for n in ("neighbours_blank", "table_asked", "table_mm", "picked"))
        kinds = [(P, NODE_TILES, SLOTS, ["dst", "src", "t3", "t8", "before", "after"]),
                 (WIN, WINS, WSLOTS, ["dst", "src", "t3"])]

        def edges(a):
            return a.rearrange("(c p e) -> p c e", c=JC, p=JP)

        with nc.Block() as block:
            @block.sync
            def _(sp):
                for n, a in (("dst", c.dst), ("src", c.src), ("t3", c.t3), ("t8", c.t8)):
                    sp.dma_start(raw[n][:, :, :], edges(a)).then_inc(load, 16)
                sp.wait_ge(blank, 2)
                flat = c.dst.rearrange("(a e) -> a e", a=1)
                b, a = raw["before"], raw["after"]
                sp.dma_start(b[0:1, 0, 1:P], flat[:, 0:P - 1]).then_inc(load, 16)
                sp.dma_start(a[JP - 1:JP, JC - 1, 0:P - 1], flat[:, E - P + 1:E]).then_inc(load, 16)
                for k in range(JC):
                    e0 = k * JP * P
                    r0 = 1 if k == 0 else 0
                    sp.dma_start(b[r0:JP, k, :], c.dst[e0 + r0 * P - 1:e0 + JP * P - 1]
                                 .rearrange("(p e) -> p e", e=P)).then_inc(load, 16)
                    r1 = JP - 1 if k == JC - 1 else JP
                    sp.dma_start(a[0:r1, k, :], c.dst[e0 + 1:e0 + r1 * P + 1]
                                 .rearrange("(p e) -> p e", e=P)).then_inc(load, 16)

            @block.gpsimd
            def _(pool):
                pool.iota(slot_i[:, :], [[1, WSLOTS]], base=0, channel_multiplier=0).then_inc(pool_done, 1)
                pool.iota(row_i[:, :], [[JP, JC]], base=0, channel_multiplier=1).then_inc(pool_done, 1)
                pool.iota(border_i[:, :], [[1, WINS]], base=0, channel_multiplier=0).then_inc(pool_done, 1)

            @block.vector
            def _(v):
                do = Chain(v, dve)
                v.memset(raw["before"][:, :, :], -1).then_inc(blank, 1)
                v.memset(raw["after"][:, :, :], -1).then_inc(blank, 1)
                v.wait_ge(pool_done, 3)
                do(v.tensor_copy(slot[:, :], slot_i[:, :]))
                do(v.tensor_copy(row_f[:, :], row_i[:, :]))
                v.wait_ge(load, 16 * (6 + 2 * JC))
                for n in raw:
                    do(v.tensor_copy(flt[n][:, :, :], raw[n][:, :, :]))
                for n in ("before", "after"):
                    do(v.tensor_tensor(flt[n][:, :, :], flt["dst"][:, :, :], flt[n][:, :, :], ALU.is_equal))
                    do(v.tensor_scalar(flt[n][:, :, :], flt[n][:, :, :], -1.0, 1.0, ALU.mult, ALU.add))
                n_picked = 0
                for turn, (width, tiles, slots, tables) in enumerate(kinds):
                    do(v.tensor_scalar(border[:, 0:tiles], border_i[:, 0:tiles], float(width), None, ALU.mult))
                    do(v.tensor_tensor(past[:, :, 0:tiles], flt["dst"][:, :, P - 1:P].to_broadcast([JP, JC, tiles]),
                                       border[:, 0:tiles].unsqueeze(1).to_broadcast([JP, JC, tiles]), ALU.is_lt))
                    v.sem_inc(ask, 1)
                    v.wait_ge(mm_done, 2 * turn + 1)
                    do(v.scalar_tensor_tensor(out=key[0:tiles, :], in0=c.ps[6][0:tiles, 0:1], scalar=float(EDGE_TILES - 1),
                                              in1=c.part[0:tiles, :], op0=ALU.min, op1=ALU.add))
                    do(v.tensor_scalar(passed[0:tiles, 0:slots], slot[0:tiles, 0:slots], key[0:tiles, :], None, ALU.is_ge))
                    v.sem_inc(ask, 1)
                    v.wait_ge(mm_done, 2 * turn + 2)
                    do(v.tensor_scalar(tile[:, 0:slots], c.ps[7][:, 0:slots], -1.0, None, ALU.add))
                    do(v.tensor_tensor(edge_tile[:, 0:slots], slot[:, 0:slots], tile[:, 0:slots], ALU.subtract))
                    for k in range(JC):
                        do(v.tensor_scalar(pick[:, k, 0:slots], edge_tile[0:JP, 0:slots], row_f[0:JP, k:k + 1], None,
                                           ALU.is_equal))
                    v.sem_inc(ask, 1)
                    tile_row, edge_row = ((c.tile_row, c.edge_row), (c.win_row, c.win_edge_row))[turn]
                    step = 1.0 if turn == 0 else float(WIN)
                    by_round = [t[0:1, 0:slots].rearrange("a (i r) -> a i r", r=RING) for t in (tile, edge_tile)]
                    do(v.tensor_scalar(tile_row[0:1, :, 0:RING], by_round[0], step, None, ALU.mult))
                    if turn == 1:
                        do(v.tensor_scalar(edge_row[0:1, :, 0:RING], by_round[1], float(EDGE_TILES - 1), None, ALU.min))

                    def taken(name):
                        v.wait_ge(picked, n_picked + tables.index(name) + 1)
                        return c.ps[tables.index(name)][0:P, 0:slots]
                    t_of = tile[0:P, 0:slots]
                    if turn == 0:
                        do(v.tensor_copy(dst_s[:, 0:slots], taken("dst")))
                        do(v.scalar_tensor_tensor(out=c.dloc[:, :], in0=t_of, scalar=-float(P), in1=dst_s[:, 0:slots],
                                                  op0=ALU.mult, op1=ALU.add))
                        do(v.tensor_copy(val[:, 0:slots], taken("src")))
                        do(v.tensor_copy(c.src_idx[:, :], val[:, 0:slots]))
                        do(v.scalar_tensor_tensor(out=val[:, 0:slots], in0=taken("t8"), scalar=float(N),
                                                  in1=val[:, 0:slots], op0=ALU.mult, op1=ALU.add))
                        do(v.tensor_copy(c.kv_idx[:, :], val[:, 0:slots]))
                        do(v.tensor_copy(val[:, 0:slots], taken("t3")))
                        for r in range(REL3):
                            do(v.tensor_scalar(c.edge_cols[:, :, HEADS + 1 + r], val[:, 0:slots], float(r), None,
                                               ALU.is_equal))
                        do(v.memset(c.edge_cols[:, :, HEADS], 1.0))
                        do(v.tensor_scalar(c.valid[:, :], c.dloc[:, :], float(P - 1), None, ALU.is_le))
                        do(v.scalar_tensor_tensor(out=c.valid[:, :], in0=c.dloc[:, :], scalar=0.0, in1=c.valid[:, :],
                                                  op0=ALU.is_ge, op1=ALU.mult))
                        for n, flag in (("before", c.starts), ("after", c.ends)):
                            do(v.tensor_tensor(flag[:, :], taken(n), c.valid[:, :], ALU.mult))
                            do(v.tensor_scalar(flag[:, :], flag[:, :], -BIG, None, ALU.mult))
                    else:
                        do(v.tensor_copy(dst_s[:, :], taken("dst")))
                        do(v.scalar_tensor_tensor(out=dst_s[:, :], in0=t_of, scalar=-float(WIN), in1=dst_s[:, :],
                                                  op0=ALU.mult, op1=ALU.add))
                        do(v.tensor_scalar(val[:, :], dst_s[:, :], float(WIN - 1), None, ALU.is_le))
                        do(v.scalar_tensor_tensor(out=val[:, :], in0=dst_s[:, :], scalar=0.0, in1=val[:, :],
                                                  op0=ALU.is_ge, op1=ALU.mult))
                        do(v.scalar_tensor_tensor(out=dst_s[:, :], in0=taken("t3"), scalar=float(WIN), in1=dst_s[:, :],
                                                  op0=ALU.mult, op1=ALU.add))
                        do(v.scalar_tensor_tensor(out=dst_s[:, :], in0=dst_s[:, :], scalar=1.0, in1=val[:, :],
                                                  op0=ALU.add, op1=ALU.mult))
                        do(v.tensor_scalar(c.win_key[:, :], dst_s[:, :], -1.0, None, ALU.add))
                        do(v.tensor_copy(c.win_src[:, :], taken("src")))
                    n_picked += len(tables)
                    v.sem_inc(ask, 1)

            @block.tensor
            def _(pe):
                for turn, (width, tiles, slots, tables) in enumerate(kinds):
                    pe.wait_ge(ask, 4 * turn + 1)
                    for k in range(JC):
                        mm = pe.matmul(c.ps[6][0:tiles, 0:1], past[:, k, 0:tiles], c.ones[0:JP, 0:1], start=(k == 0),
                                       stop=(k == JC - 1))
                    mm.then_inc(mm_done, 1)
                    pe.wait_ge(ask, 4 * turn + 2)
                    pe.matmul(c.ps[7][:, 0:slots], c.ones[0:tiles, :], passed[0:tiles, 0:slots], start=True,
                              stop=True).then_inc(mm_done, 1)
                    pe.wait_ge(ask, 4 * turn + 3)
                    for n, name in enumerate(tables):
                        for k in range(JC):
                            mm = pe.matmul(c.ps[n][0:P, 0:slots], flt[name][:, k, :], pick[:, k, 0:slots],
                                           start=(k == 0), stop=(k == JC - 1))
                        mm.then_inc(picked, 1)


def project(nc, c):
    with ExitStack() as ctx:
        def sb(name, shape, dt=F32):
            return ctx.enter_context(nc.sbuf_tensor(name, shape, dt))
        w = {n: sb("w_" + n, [128, NTYPES, KC, D]) for n in "qkv"}
        rel = {n: sb("rel_" + n, [128, RELS, KC, 128]) for n in ("att", "msg")}
        pri = sb("pri", [128, RELS, HEADS])
        xt = sb("xt", [128, KC, N])
        xm = sb("xm", [128, 2, NTYPES, KC, P])
        kvt = sb("kvt", [128, 2, 2, KC, P])
        stage = sb("stage", [P, 2, RELS, 2 * D])
        load, cleared, dve, xm_ready, proj, proj_out, rel_mm, rel_act, rel_dve, rel_w = (
            c.sem(n) for n in ("proj_loads", "rel_cleared", "proj_chain", "masked_x", "projected", "proj_copied",
                               "related", "related_by_act", "related_by_dve", "rel_weights"))
        stored = [c.sem("kv_stored0"), c.sem("kv_stored1")]

        with nc.Block() as block:
            @block.sync
            def _(sp):
                sp.dma_start(xt[:, :, :], c.xT.rearrange("(c p) n -> p c n", p=128)).then_inc(load, 16)
                sp.dma_start(c.type_row[:, :], c.node_type.partition_broadcast(128)).then_inc(load, 16)
                sp.dma_start(pri[:, :, :], c.pri.partition_broadcast(128)).then_inc(load, 16)
                for n, a in (("q", c.wq), ("k", c.wk), ("v", c.wv)):
                    sp.dma_start(w[n][:, :, :, :], a.rearrange("t (c p) o -> p t c o", p=128)).then_inc(load, 16)
                sp.wait_ge(cleared, 2)
                for n, a in (("att", c.attT), ("msg", c.msg)):
                    for h in range(HEADS):
                        lo = h % 2 * DK
                        sp.dma_start(rel[n][lo:lo + DK, :, h // 2, lo:lo + DK],
                                     a[:, h].rearrange("r e d -> e r d")).then_inc(load, 16)

                def body(t, b, uses):
                    sp.wait_ge(rel_act, 4 * t + 4)
                    sp.wait_ge(rel_dve, 4 * t + 4)
                    for k, table in enumerate((c.key_table, c.msg_table)):
                        to = table.rearrange("(r n) d -> n r d", r=RELS)
                        to = to[t * P:(t + 1) * P] if isinstance(t, int) else to[ds(t * P, P)]
                        sp.dma_start(to, stage[:, b, :, k * D:(k + 1) * D]).then_inc(stored[b], 16)
                by_tiles(sp, body)
                sp.wait_ge(stored[0], 32 * 13)
                sp.wait_ge(stored[1], 32 * 12)

            @block.vector
            def _(v):
                do = Chain(v, dve)
                for n in rel:
                    v.memset(rel[n][:, :, :, :], 0.0).then_inc(cleared, 1)
                v.wait_ge(load, 16 * 14)
                do(v.tensor_scalar(pri[:, :, :], pri[:, :, :], DK ** -0.5, None, ALU.mult))
                for h in range(HEADS):
                    lo = h % 2 * DK
                    blk = rel["att"][:, :, h // 2, lo:lo + DK]
                    do(v.tensor_tensor(blk, blk, pri[:, :, h:h + 1].to_broadcast([128, RELS, DK]), ALU.mult))
                v.sem_inc(rel_w, 1)

                def body(t, b, uses):
                    if known(t, 2):
                        v.wait_ge(proj, t - 1)
                    for y in range(NTYPES):
                        at = slice(t * P, (t + 1) * P) if isinstance(t, int) else ds(t * P, P)
                        m = v.scalar_tensor_tensor(
                            out=xm[:, b, y], in0=c.type_row[:, at].unsqueeze(1).to_broadcast([128, KC, P]),
                            scalar=float(y), in1=xt[:, :, at], op0=ALU.is_equal, op1=ALU.mult)
                    m.then_inc(xm_ready, 1)
                    for r in range(1, RELS, 2):
                        v.wait_ge(rel_mm, RELS * t + r + 1)
                        if r == 1 and known(t, 2):
                            v.wait_ge(stored[b], 32 * uses)
                        v.tensor_copy(stage[:, b, r, :], c.ps[3 + r % 4][0:P, :]).then_inc(rel_dve, 1)
                by_tiles(v, body)

            @block.scalar
            def _(a):
                def body(t, b, uses):
                    a.wait_ge(proj, t + 1)
                    tile = slice(t, t + 1) if isinstance(t, int) else ds(t, 1)
                    a.copy(c.nodes_b[:, tile, :], c.ps[0][0:P, 0:D].unsqueeze(1)).then_inc(proj_out, 1)
                    if known(t, 2):
                        a.wait_ge(rel_mm, RELS * (t - 1))
                    for k in range(2):
                        a.copy(kvt[:, b, k], c.ps[1 + k][:, 0:KC * P].rearrange("p (c n) -> p c n", c=KC))\
                            .then_inc(proj_out, 1)
                    for r in range(0, RELS, 2):
                        a.wait_ge(rel_mm, RELS * t + r + 1)
                        if r == 0 and known(t, 2):
                            a.wait_ge(stored[b], 32 * uses)
                        a.copy(stage[:, b, r, :], c.ps[3 + r % 4][0:P, :]).then_inc(rel_act, 1)
                by_tiles(a, body)

            @block.tensor
            def _(pe):
                def body(t, b, uses):
                    pe.wait_ge(xm_ready, t + 1)
                    if known(t, 1):
                        pe.wait_ge(proj_out, 3 * t)
                    steps = [(y, k) for y in range(NTYPES) for k in range(KC)]
                    for i, (y, k) in enumerate(steps):
                        pe.matmul(c.ps[0][0:P, 0:D], xm[:, b, y, k, :], w["q"][:, y, k, :], start=(i == 0),
                                  stop=(i == len(steps) - 1))
                    for n, name in enumerate("kv"):
                        for o in range(KC):
                            for i, (y, k) in enumerate(steps):
                                mm = pe.matmul(c.ps[1 + n][:, o * P:(o + 1) * P],
                                               w[name][:, y, k, o * 128:(o + 1) * 128], xm[:, b, y, k, :],
                                               start=(i == 0), stop=(i == len(steps) - 1))
                    mm.then_inc(proj, 1)
                    pe.wait_ge(proj_out, 3 * t + 3)
                    if isinstance(t, int) and t == 0:
                        pe.wait_ge(rel_w, 1)
                    for r in range(RELS):
                        if known(t, 1) or r >= 4:
                            pe.wait_ge((rel_act, rel_dve)[r % 2], 4 * t + r // 2 - 1)
                        for n, name in enumerate(("att", "msg")):
                            for o in range(KC):
                                mm = pe.matmul(c.ps[3 + r % 4][0:P, n * D + o * 128:n * D + (o + 1) * 128],
                                               kvt[:, b, n, o, :], rel[name][:, r, o, :], start=True, stop=True)
                        mm.then_inc(rel_mm, 1)
                pe.wait_ge(load, 16 * 14)
                by_tiles(pe, body)


def gather_rows(pool, rows, ring, ring_used, copied, table, filled, let_go, slots=SLOTS):
    def body(s, i):
        for r in range(RING):
            if r % GROUP == 0:
                pool.wait_ge(copied, RING // GROUP * i + r // GROUP + 1)
                pool.sem_inc(let_go, 1)
            if known(s, 1):
                pool.wait_ge(ring_used, s + r - RING + 1)
                pool.sem_inc(let_go, 1)
            pool.indirect_dma_start(ring[:, r, :], None, table,
                                    bass.IndirectOffsetOnAxis(rows[:, r:r + 1], 0)).then_inc(filled[r], 16)
    by_slots(pool, body, slots)


def copy_rows(a, s, i, r, table, rows, filled, copied):
    if known(s, 1):
        for k in range(GROUP):
            a.wait_ge(filled[r + k], 16 * i)
    a.copy(rows[:, r:r + GROUP], col(table, s + r, GROUP)).then_inc(copied, 1)


def copy_first_rows(a, table, rows, filled, copied):
    for r in range(0, RING, GROUP):
        copy_rows(a, 0, 0, r, table, rows, filled, copied)


def copy_next_rows(a, s, i, r, table, rows, filled, copied, slots=SLOTS):
    if r % GROUP == GROUP - 1 and before_end(s, r, RING, slots):
        copy_rows(a, s + RING, i + 1, r - GROUP + 1, table, rows, filled, copied)


def copy_all_rows(a, table, rows, filled, copied, slots=SLOTS):
    def body(s, i):
        for r in range(0, RING, GROUP):
            copy_rows(a, s, i, r, table, rows, filled, copied)
    by_slots(a, body, slots)


def one_hot(v, c, hot, s, r, hot_ready, key=None, columns=P, ahead=0):
    v.tensor_scalar(hot[:, (r + ahead) % RING, :], c.iota[0:P, 0:columns],
                    col(c.dloc if key is None else key, s + r + ahead), None, ALU.is_equal).then_inc(hot_ready, 1)


def attention_scores(nc, c):
    with ExitStack() as ctx:
        def sb(name, shape, dt=F32):
            return ctx.enter_context(nc.sbuf_tensor(name, shape, dt))
        keys = sb("keys", [P, RING, D])
        rows = sb("rows_a", [P, RING], I32)
        hot = sb("hot16", [P, RING, P], BF16)
        hot_t = sb("hot_t", [P, 2, P])
        prod = sb("prod", [P, BUFS, D])
        filled = [c.sem(f"keys_in{r}") for r in range(RING)]
        copied, let_go, hot_ready, turned, hot_t_ready, q_ready, prod_done, scored = (
            c.sem(n) for n in ("rows_copied_a", "pool_seen_a", "hot_ready_a", "turned_a", "hot_t_ready", "q_ready",
                               "prod_done", "scored"))
        with nc.Block() as block:
            @block.gpsimd
            def _(pool):
                gather_rows(pool, rows, keys, prod_done, copied, c.key_table, filled, let_go)

            @block.scalar
            def _(a):
                def body(s, i):
                    for r in range(RING):
                        if r % GROUP == 0:
                            copy_rows(a, s, i, r, c.kv_idx, rows, filled, copied)
                        a.wait_ge(turned, s + r + 1)
                        if known(s, 1) or r >= 2:
                            a.wait_ge(q_ready, s + r - 1)
                        a.copy(hot_t[:, r % 2, :], c.ps[r % 2][:, :].bitcast(BF16)[0:P, 0:P]).then_inc(hot_t_ready, 1)
                by_slots(a, body)

            @block.tensor
            def _(pe):
                tiles = Rows(pe, "q_tile", c.tile_row, NODE_TILES - 1)

                def turn(s, r, ahead=0):
                    n = r + ahead
                    pe.wait_ge(hot_ready, s + n + 1)
                    if known(s, 1) or n >= 2:
                        pe.wait_ge(hot_t_ready, s + n - 1)
                    pe.transpose(c.ps[n % 2][:, :].bitcast(BF16)[0:P, 0:P], hot[:, n % RING, :],
                                 c.ident16[0:P, 0:P]).then_inc(turned, 1)

                def body(s, i):
                    for r in range(RING):
                        t = tiles.at(i, r)
                        pe.wait_ge(hot_t_ready, s + r + 1)
                        if known(s, 1) or r >= BUFS:
                            pe.wait_ge(prod_done, s + r - BUFS + 1)
                        pe.matmul(c.ps[2 + r % BUFS][0:P, 0:D], hot_t[:, r % 2, :],
                                  c.nodes_b[:, ds(t, 1), :].rearrange("p a d -> p (a d)"), start=True,
                                  stop=True).then_inc(q_ready, 1)
                        if before_end(s, r, AHEAD):
                            turn(s, r, AHEAD)
                for r in range(AHEAD):
                    turn(0, r)
                by_slots(pe, body)
                tiles.free()

            @block.vector
            def _(v):
                def score(s, r):
                    v.wait_ge(prod_done, s + r + 1)
                    to = c.score[:, s + r, :] if isinstance(s, int) else \
                        c.score[:, ds(s + r, 1), :].rearrange("p a h -> p (a h)")
                    v.tensor_reduce(to, prod[:, r % BUFS, :].rearrange("p (h d) -> p h d", h=HEADS), AX,
                                    ALU.add).then_inc(scored, 1)

                def body(s, i):
                    for r in range(RING):
                        v.wait_ge(q_ready, s + r + 1)
                        v.wait_ge(filled[r], 16 * (i + 1))
                        if known(s, 1) or r >= BUFS:
                            v.wait_ge(scored, s + r - BUFS + 1)
                        v.tensor_tensor(prod[:, r % BUFS, :], keys[:, r, :], c.ps[2 + r % BUFS][0:P, 0:D],
                                        ALU.mult).then_inc(prod_done, 1)
                        if before_end(s, r, RING):
                            one_hot(v, c, hot, s, r, hot_ready, ahead=RING)
                        score(s, r)
                for r in range(RING):
                    one_hot(v, c, hot, 0, r, hot_ready)
                by_slots(v, body)


def segment_softmax(nc, c):
    with ExitStack() as ctx:
        def sb(name, shape, dt=F32):
            return ctx.enter_context(nc.sbuf_tensor(name, shape, dt))
        CH = HEADS * SCAN_C
        L = SCAN_S * P
        turned = sb("turned", [SLOT_P, HEADS + 2, SLOT_C, P])
        seq, fwd, bwd = sb("seq", [CH, L]), sb("fwd", [CH, L]), sb("bwd", [CH, L])
        reset = {n: sb("reset_" + n, [CH, L]) for n in ("start", "end")}
        ends2 = sb("ends2", [CH, 2])
        row = sb("row", [1, 2, CH])
        carry_row = sb("carry_row", [1, CH + 2])
        carry = sb("carry", [CH, 1])
        dve, pe_s, mm_done, out_t, dma_o, dma_i, ready = (
            c.sem(n) for n in ("softmax_chain", "softmax_turned", "softmax_mm", "seq_copied", "seq_stored",
                               "seq_loaded", "seq_ready"))
        n_turn = (HEADS + 2) * SLOT_C

        with nc.Block() as block:
            @block.vector
            def _(v):
                do = Chain(v, dve)
                valid = c.valid[:, :].unsqueeze(2).to_broadcast([P, SLOTS, HEADS])
                do(v.tensor_tensor(c.score[:, :, :], c.score[:, :, :], valid, ALU.mult))
                do(v.tensor_scalar(c.valid[:, :], c.valid[:, :], BIG, -BIG, ALU.mult, ALU.add))
                do(v.tensor_tensor(c.score[:, :, :], c.score[:, :, :], valid, ALU.add))
                v.sem_inc(ready, 1)
                for n in range(n_turn):
                    v.wait_ge(pe_s, n + 1)
                    v.tensor_copy(turned[:, n // SLOT_C, n % SLOT_C, :],
                                  c.ps[n % 8][0:SLOT_P, 0:P]).then_inc(out_t, 1)

                def scan(src, out, flags, step, at_last):
                    view = (lambda a: a[:, ::step])
                    do(v.tensor_tensor_scan(view(out), view(flags), view(src), -BIG, ALU.add, ALU.max))
                    do(v.tensor_copy(ends2[:, 0:1], out[:, at_last:at_last + 1]))
                    do(v.tensor_reduce(ends2[:, 1:2], flags[:, :], AX, ALU.min))
                    v.sem_inc(ready, 1)
                    turn = 0 if step == 1 else 1
                    v.wait_ge(mm_done, 3 * turn + 2)
                    for k in range(2):
                        do(v.tensor_copy(row[0:1, k, :], c.ps[k][0:1, 0:CH]))
                    do(v.memset(carry_row[0:1, :], -BIG))
                    mid = carry_row[0:1, 1:CH + 1]
                    do(v.tensor_tensor_scan(mid[:, ::step], row[0:1, 1, ::step], row[0:1, 0, ::step], -BIG,
                                            ALU.add, ALU.max))
                    v.sem_inc(ready, 1)
                    v.wait_ge(mm_done, 3 * turn + 3)
                    do(v.tensor_copy(carry[:, :], c.ps[2][0:CH, 0:1]))
                    do(v.tensor_tensor_scan(view(out), view(flags), view(src), carry[:, :], ALU.add, ALU.max))
                v.wait_ge(dma_i, 16 * (1 + 2 * HEADS))
                scan(seq, fwd, reset["start"], 1, L - 1)
                scan(fwd, bwd, reset["end"], -1, 0)
                v.sem_inc(ready, 1)
                for n in range(HEADS * SLOT_C):
                    h, k = n // SLOT_C, n % SLOT_C
                    v.wait_ge(pe_s, n_turn + n + 1)
                    at = c.score[:, k * SLOT_P:(k + 1) * SLOT_P, h]
                    v.tensor_tensor(at, at, c.ps[n % 8][0:P, 0:SLOT_P], ALU.subtract).then_inc(out_t, 1)

            @block.tensor
            def _(pe):
                pe.wait_ge(ready, 1)
                for n in range(n_turn):
                    a, k = n // SLOT_C, n % SLOT_C
                    if n >= 8:
                        pe.wait_ge(out_t, n - 7)
                    src = c.score[:, k * SLOT_P:(k + 1) * SLOT_P, a] if a < HEADS else \
                        (c.starts, c.ends)[a - HEADS][:, k * SLOT_P:(k + 1) * SLOT_P]
                    pe.transpose(c.ps[n % 8][0:SLOT_P, 0:P], src, c.ident[0:P, 0:P]).then_inc(pe_s, 1)
                pe.wait_ge(out_t, n_turn)
                for turn in range(2):
                    step = 1 if turn == 0 else -1
                    pe.wait_ge(ready, 2 + 2 * turn)
                    for k in range(2):
                        pe.transpose(c.ps[k][0:1, 0:CH], ends2[:, k:k + 1], c.ident[0:CH, 0:CH]).then_inc(mm_done, 1)
                    pe.wait_ge(ready, 3 + 2 * turn)
                    at = 1 - step
                    pe.transpose(c.ps[2][0:CH, 0:1], carry_row[0:1, at:at + CH],
                                 c.ident[0:1, 0:1]).then_inc(mm_done, 1)
                pe.wait_ge(ready, 6)
                pe.wait_ge(dma_i, 16 * (1 + 2 * HEADS + 1))
                for n in range(HEADS * SLOT_C):
                    if n >= 8:
                        pe.wait_ge(out_t, n_turn + n - 7)
                    pe.transpose(c.ps[n % 8][0:P, 0:SLOT_P], turned[:, n // SLOT_C, n % SLOT_C, :],
                                 c.ident[0:SLOT_P, 0:SLOT_P]).then_inc(pe_s, 1)

            @block.sync
            def _(sp):
                sp.wait_ge(out_t, n_turn)
                for a in range(HEADS + 2):
                    sp.dma_start(c.seq_dram[a].rearrange("(k p) e -> p k e", p=SLOT_P),
                                 turned[:, a]).then_inc(dma_o, 16)
                sp.wait_ge(dma_o, 16 * (HEADS + 2))
                chunks = "(c s) e -> c (s e)"
                sp.dma_start(seq[:, :], c.seq_dram[0:HEADS].rearrange("h (c s) e -> (h c) (s e)", s=SCAN_S))\
                    .then_inc(dma_i, 16)
                for h in range(HEADS):
                    for k, n in enumerate(("start", "end")):
                        sp.dma_start(reset[n][h * SCAN_C:(h + 1) * SCAN_C, :],
                                     c.seq_dram[HEADS + k].rearrange(chunks, s=SCAN_S)).then_inc(dma_i, 16)
                sp.wait_ge(ready, 6)
                sp.dma_start(c.max_dram.rearrange("h (c s) e -> (h c) (s e)", s=SCAN_S), bwd[:, :]).then_inc(dma_o, 16)
                sp.wait_ge(dma_o, 16 * (HEADS + 3))
                sp.dma_start(turned[:, 0:HEADS].rearrange("p h k e -> p (h k) e"),
                             c.max_dram.rearrange("h (k p) e -> p (h k) e", p=SLOT_P)).then_inc(dma_i, 16)

            @block.scalar
            def _(a):
                a.wait_ge(out_t, n_turn + HEADS * SLOT_C)
                a.activation(c.edge_cols[:, :, 0:HEADS], c.score[:, :, :], ACT.Exp).then_inc(dma_o, 1)


def add_sum(v, s, n, i, places, summed, added, to_of, part):
    t = places.at(i, n)
    v.wait_ge(summed, s + n + 1)
    if known(s, 1) or n >= 1:
        v.wait_ge(added, s + n)
    to = to_of(t)
    v.tensor_tensor(to, to, part, ALU.add).then_inc(added, 1)


def weighted_messages(nc, c):
    W = D + EXTRA
    LAG = 2
    with ExitStack() as ctx:
        def sb(name, shape, dt=F32):
            return ctx.enter_context(nc.sbuf_tensor(name, shape, dt))
        got = sb("got_b", [P, RING, D])
        rows = sb("rows_b", [P, RING], I32)
        hot = sb("hot_b", [P, RING, P])
        msg = sb("msg_b", [P, BUFS, D])
        filled = [c.sem(f"msgs_in{r}") for r in range(RING)]
        copied, let_go, hot_ready, weighted, summed, added = (
            c.sem(n) for n in ("rows_copied_b", "pool_seen_b", "hot_ready_b", "weighted", "summed_b", "added_b"))
        clear = c.sem("acc_clear_b")
        with nc.Block() as block:
            @block.gpsimd
            def _(pool):
                gather_rows(pool, rows, got, weighted, copied, c.msg_table, filled, let_go)

            @block.scalar
            def _(a):
                copy_all_rows(a, c.kv_idx, rows, filled, copied)

            @block.tensor
            def _(pe):
                def body(s, i):
                    for r in range(RING):
                        pe.wait_ge(weighted, s + r + 1)
                        pe.wait_ge(hot_ready, s + r + 1)
                        if known(s, 1) or r >= BUFS:
                            pe.wait_ge(added, s + r - BUFS + 1)
                        pe.matmul(c.ps[r % BUFS][0:P, 0:D], hot[:, r, :], msg[:, r % BUFS, :], start=True, stop=True)
                        cols = c.edge_cols[:, s + r, :] if isinstance(s, int) else \
                            c.edge_cols[:, ds(s + r, 1), :].rearrange("p a h -> p (a h)")
                        pe.matmul(c.ps[r % BUFS][0:P, D:W], hot[:, r, :], cols, start=True, stop=True)\
                            .then_inc(summed, 1)
                by_slots(pe, body)

            @block.vector
            def _(v):
                v.memset(c.acc[:, :, :], 0.0).then_inc(clear, 1)
                v.wait_ge(clear, 1)

                places = Rows(v, "msg_tile", c.tile_row, NODE_TILES - 1)

                def add(s, n, i):
                    add_sum(v, s, n, i, places, summed, added, lambda t: c.acc[:, ds(t, 1), 0:W],
                            c.ps[n % BUFS][0:P, 0:W].unsqueeze(1))
                    if before_end(s, n, RING):
                        one_hot(v, c, hot, s, n, hot_ready, ahead=RING)

                def body(s, i):
                    for r in range(RING):
                        v.wait_ge(filled[r], 16 * (i + 1))
                        if known(s, 1) or r >= BUFS:
                            v.wait_ge(summed, s + r - BUFS + 1)
                        cols = c.edge_cols[:, s + r, 0:HEADS] if isinstance(s, int) else \
                            c.edge_cols[:, ds(s + r, 1), 0:HEADS].rearrange("p a h -> p (a h)")
                        v.tensor_tensor(msg[:, r % BUFS, :].rearrange("p (h d) -> p h d", h=HEADS),
                                        got[:, r, :].rearrange("p (h d) -> p h d", h=HEADS),
                                        cols.unsqueeze(2).to_broadcast([P, HEADS, DK]), ALU.mult)\
                            .then_inc(weighted, 1)
                        if known(s, 1) or r >= LAG:
                            add(s - RING, r - LAG + RING, i - 1) if r < LAG else add(s, r - LAG, i)
                for r in range(RING):
                    one_hot(v, c, hot, 0, r, hot_ready)
                by_slots(v, body)
                for r in range(RING - LAG, RING):
                    add(SLOTS - RING, r, ROUNDS - 1)
                places.free()


def attention_output(nc, c):
    with ExitStack() as ctx:
        def sb(name, shape, dt=F32):
            return ctx.enter_context(nc.sbuf_tensor(name, shape, dt))
        wa = sb("wa", [128, NTYPES, KC, D])
        am = sb("am", [128, 2, NTYPES, KC, P])
        agg = sb("agg", [P, 2, D])
        rden = sb("rden", [P, NODE_TILES, HEADS])
        skip, gate_e = sb("skip", [P, NTYPES]), sb("gate_e", [P, NTYPES])
        ntype_i, ntype = sb("ntype_i", [P, NODE_TILES], I32), sb("ntype", [P, NODE_TILES])
        gate, tmp = sb("gate", [P, NODE_TILES]), sb("gate_tmp", [P, NODE_TILES])
        load, dve, act_s, agg_ready, turned, masked, mixed, out_done = (
            c.sem(n) for n in ("att_loads", "att_chain", "att_act", "agg_ready", "agg_turned", "agg_masked",
                               "agg_mixed", "att_out"))
        with nc.Block() as block:
            @block.sync
            def _(sp):
                sp.dma_start(wa[:, :, :, :], c.wa.rearrange("t (c p) o -> p t c o", p=128)).then_inc(load, 16)
                sp.dma_start(skip[:, :], c.skip.partition_broadcast(P)).then_inc(load, 16)
                sp.dma_start(ntype_i[:, :], c.node_type_cols).then_inc(load, 16)
                sp.dma_start(c.nodes[:, :, :], c.x.rearrange("(t p) d -> p t d", p=P)).then_inc(load, 16)

            @block.scalar
            def _(a):
                a.wait_ge(load, 64)
                a.activation(gate_e[:, :], skip[:, :], ACT.Exp, scale=-1.0).then_inc(act_s, 1)
                a.wait_ge(dve, 2)
                a.activation(c.rdeg[:, :], c.cnt[:, :, 0], ACT.Sqrt).then_inc(act_s, 1)

            @block.vector
            def _(v):
                do = Chain(v, dve)
                do(v.tensor_scalar(c.cnt[:, :, :], c.acc[:, :, D + HEADS:D + EXTRA], 1.0, None, ALU.max))
                do(v.tensor_scalar(rden[:, :, :], c.acc[:, :, D:D + HEADS], 1e-30, None, ALU.max))
                do(v.reciprocal(rden[:, :, :], rden[:, :, :]))
                v.wait_ge(act_s, 2)
                do(v.reciprocal(c.rdeg[:, :], c.rdeg[:, :]))
                do(v.reciprocal(c.cnt[:, :, :], c.cnt[:, :, :]))
                do(v.tensor_scalar(gate_e[:, :], gate_e[:, :], 1.0, None, ALU.add))
                do(v.reciprocal(gate_e[:, :], gate_e[:, :]))
                do(v.tensor_copy(ntype[:, :], ntype_i[:, :]))
                do(v.memset(gate[:, :], 0.0))
                for y in range(NTYPES):
                    do(v.tensor_scalar(tmp[:, :], ntype[:, :], float(y), gate_e[:, y:y + 1], ALU.is_equal, ALU.mult))
                    do(v.tensor_tensor(gate[:, :], gate[:, :], tmp[:, :], ALU.add))

                def body(t, b, uses):
                    tile = slice(t, t + 1) if isinstance(t, int) else ds(t, 1)
                    at = slice(t * P, (t + 1) * P) if isinstance(t, int) else ds(t * P, P)
                    if known(t, 2):
                        v.wait_ge(turned, t - 1)
                    v.tensor_tensor(agg[:, b, :].rearrange("p (h d) -> p h d", h=HEADS),
                                    c.acc[:, tile, 0:D].rearrange("p a (h d) -> p (a h) d", h=HEADS),
                                    rden[:, tile, :].rearrange("p a h -> p (a h)").unsqueeze(2)
                                    .to_broadcast([P, HEADS, DK]), ALU.mult).then_inc(agg_ready, 1)
                    v.wait_ge(turned, t + 1)
                    if known(t, 2):
                        v.wait_ge(mixed, t - 1)
                    for y in range(NTYPES):
                        m = v.scalar_tensor_tensor(
                            out=am[:, b, y], in0=c.type_row[:, at].unsqueeze(1).to_broadcast([128, KC, P]),
                            scalar=float(y), in1=c.ps[b][:, 0:KC * P].rearrange("p (c n) -> p c n", c=KC),
                            op0=ALU.is_equal, op1=ALU.mult)
                    m.then_inc(masked, 1)
                    v.wait_ge(mixed, t + 1)
                    v.scalar_tensor_tensor(out=c.nodes_b[:, tile, :], in0=c.ps[2 + b][0:P, 0:D].unsqueeze(1),
                                           scalar=gate[:, tile], in1=c.nodes[:, tile, :], op0=ALU.mult,
                                           op1=ALU.add).then_inc(out_done, 1)
                by_tiles(v, body)

            @block.tensor
            def _(pe):
                pe.wait_ge(load, 64)

                def body(t, b, uses):
                    pe.wait_ge(agg_ready, t + 1)
                    if known(t, 2):
                        pe.wait_ge(masked, t - 1)
                    for k in range(KC):
                        mm = pe.transpose(c.ps[b][:, k * P:(k + 1) * P], agg[:, b, k * 128:(k + 1) * 128],
                                          c.ident[0:P, 0:P])
                    mm.then_inc(turned, 1)
                    pe.wait_ge(masked, t + 1)
                    if known(t, 2):
                        pe.wait_ge(out_done, t - 1)
                    steps = [(y, k) for y in range(NTYPES) for k in range(KC)]
                    for i, (y, k) in enumerate(steps):
                        mm = pe.matmul(c.ps[2 + b][0:P, 0:D], am[:, b, y, k, :], wa[:, y, k, :], start=(i == 0),
                                       stop=(i == len(steps) - 1))
                    mm.then_inc(mixed, 1)
                by_tiles(pe, body)


def row_norm(nc, c, name, src, to_dram, scale=None, final=False):
    with ExitStack() as ctx:
        def sb(n, shape, dt=F32):
            return ctx.enter_context(nc.sbuf_tensor(name + n, shape, dt))
        parts, mv = sb("_parts", [P, 2, 6]), sb("_mv", [P, 2, 2])
        mean, rstd = sb("_mean", [P, NODE_TILES]), sb("_rstd", [P, NODE_TILES])
        chain, seen, act_s, rows, stored = (c.sem(name + n) for n in ("_chain", "_seen", "_sqrt", "_rows", "_stored"))
        scaled = sb("_scaled", [P, NODE_TILES, D]) if scale is not None else c.nodes
        with nc.Block() as block:
            @block.vector
            def _(v):
                do = Chain(v, chain)

                def body(t, b, uses):
                    do.at(4 * t)
                    tile = slice(t, t + 1) if isinstance(t, int) else ds(t, 1)
                    do(v.bn_stats(parts[:, b, :], src[:, tile, :].rearrange("p a d -> p (a d)")))
                    v.sem_inc(seen, 1)
                    do(v.bn_aggr(mv[:, b, :], parts[:, b, :]))
                    do(v.tensor_copy(mean[:, tile], mv[:, b, 0:1]))
                    do(v.tensor_copy(rstd[:, tile], mv[:, b, 1:2]))
                by_tiles(v, body)
                do.at(4 * NODE_TILES)
                do(v.tensor_scalar(rstd[:, :], rstd[:, :], LN_EPS, None, ALU.add))
                v.wait_ge(act_s, 1)
                do(v.reciprocal(rstd[:, :], rstd[:, :]))

                def apply(t, b, uses):
                    tile = slice(t, t + 1) if isinstance(t, int) else ds(t, 1)
                    v.tensor_scalar(c.nodes[:, tile, :], src[:, tile, :], mean[:, tile], rstd[:, tile],
                                    ALU.subtract, ALU.mult).then_inc(rows, 1)
                    if scale is not None:
                        v.wait_ge(rows, 2 * t + 1)
                        v.tensor_scalar(scaled[:, tile, :], c.nodes[:, tile, :], scale[:, tile], None,
                                        ALU.mult).then_inc(rows, 1)
                by_tiles(v, apply)

            @block.scalar
            def _(a):
                a.wait_ge(chain, 4 * NODE_TILES + 1)
                a.activation(rstd[:, :], rstd[:, :], ACT.Sqrt).then_inc(act_s, 1)

            @block.sync
            def _(sp):
                sp.wait_ge(rows, NODE_TILES * (1 if scale is None else 2))
                sp.dma_start(to_dram.rearrange("(t p) d -> p t d", p=P), scaled[:, :, :]).then_inc(stored, 16)
                sp.wait_ge(stored, 16)


EXPERTS, HIDDEN, TOPK, CAP = 64, 512, 2, 1024
HC = HIDDEN // 128
ROW_TILES = N * TOPK // P
STEPS = ROW_TILES + EXPERTS - 1
WRING = 4
BN_EPS = 1e-5


def by_ring(eng, body, count, ring):
    for s in range(ring + 1):
        body(s, s % ring, s // ring)
    with eng.Fori(1, count // ring) as k:
        for i in range(ring):
            body(ring * k + 1 + i, (1 + i) % ring, k + (1 + i) // ring)


def out_degrees(nc, c):
    G = 5
    with ExitStack() as ctx:
        def sb(name, shape, dt=F32):
            return ctx.enter_context(nc.sbuf_tensor(name, shape, dt))
        src_i, lo, hi = sb("src_i", [P, EDGE_TILES], I32), sb("src_lo", [P, EDGE_TILES]), sb("src_hi", [P, EDGE_TILES])
        hot_lo, hot_hi = sb("hot_lo", [P, 2, G, P], BF16), sb("hot_hi", [P, 2, G, NODE_TILES], BF16)
        load, chain, hot_ready, counted, act_s = (
            c.sem(n) for n in ("src_load", "hist_chain", "hist_hot", "hist_counted", "hist_sqrt"))
        with nc.Block() as block:
            @block.sync
            def _(sp):
                sp.dma_start(src_i[:, :], c.src.rearrange("(p k) -> p k", p=P)).then_inc(load, 16)

            @block.vector
            def _(v):
                do = Chain(v, chain)
                v.wait_ge(load, 16)
                do(v.tensor_copy(lo[:, :], src_i[:, :]))
                do(v.memset(hi[:, :], 0.0))
                for t in range(1, NODE_TILES):
                    do(v.scalar_tensor_tensor(out=hi[:, :], in0=lo[:, :], scalar=float(P * t), in1=hi[:, :],
                                              op0=ALU.is_ge, op1=ALU.add))
                do(v.scalar_tensor_tensor(out=lo[:, :], in0=hi[:, :], scalar=-float(P), in1=lo[:, :],
                                          op0=ALU.mult, op1=ALU.add))

                def body(g, b, uses):
                    at = slice(g * G, (g + 1) * G) if isinstance(g, int) else ds(g * G, G)
                    if known(g, 2):
                        v.wait_ge(counted, g - 1)
                    for hot, digit, n in ((hot_lo, lo, P), (hot_hi, hi, NODE_TILES)):
                        v.tensor_tensor(hot[:, b], c.iota[0:P, 0:n].unsqueeze(1).to_broadcast([P, G, n]),
                                        digit[:, at].unsqueeze(2).to_broadcast([P, G, n]),
                                        ALU.is_equal).then_inc(hot_ready, 1)
                by_ring(v, body, EDGE_TILES // G, 2)
                v.wait_ge(counted, EDGE_TILES // G)
                do(v.tensor_scalar(c.rout[:, :], c.ps[0][0:P, 0:NODE_TILES], 1.0, None, ALU.max))
                v.wait_ge(act_s, 1)
                do(v.reciprocal(c.rout[:, :], c.rout[:, :]))

            @block.scalar
            def _(a):
                a.wait_ge(chain, NODE_TILES + 3)
                a.activation(c.rout[:, :], c.rout[:, :], ACT.Sqrt).then_inc(act_s, 1)

            @block.tensor
            def _(pe):
                last = EDGE_TILES // G - 1

                def body(g, b, uses):
                    pe.wait_ge(hot_ready, 2 * g + 2)
                    for k in range(G):
                        mm = pe.matmul(c.ps[0][0:P, 0:NODE_TILES], hot_lo[:, b, k, :], hot_hi[:, b, k, :],
                                       start=(isinstance(g, int) and g == 0 and k == 0), stop=True,
                                       skip_group_check=True)
                    mm.then_inc(counted, 1)
                by_ring(pe, body, EDGE_TILES // G, 2)


def graph_sum(nc, c, name, table, acc):
    with ExitStack() as ctx:
        def sb(n, shape, dt=F32):
            return ctx.enter_context(nc.sbuf_tensor(name + n, shape, dt))
        got = sb("_got", [P, RING, D])
        rows = sb("_rows", [P, RING], I32)
        hot = sb("_hot", [P, RING, P])
        filled = [c.sem(f"{name}_in{r}") for r in range(RING)]
        copied, let_go, hot_ready, summed, added, clear = (
            c.sem(name + n) for n in ("_rows_copied", "_pool_seen", "_hot_ready", "_summed", "_added", "_clear"))
        with nc.Block() as block:
            @block.gpsimd
            def _(pool):
                gather_rows(pool, rows, got, summed, copied, table, filled, let_go)

            @block.scalar
            def _(a):
                copy_all_rows(a, c.src_idx, rows, filled, copied)

            @block.tensor
            def _(pe):
                def body(s, i):
                    for r in range(RING):
                        pe.wait_ge(filled[r], 16 * (i + 1))
                        pe.wait_ge(hot_ready, s + r + 1)
                        if known(s, 1) or r >= BUFS:
                            pe.wait_ge(added, s + r - BUFS + 1)
                        pe.matmul(c.ps[r % BUFS][0:P, 0:D], hot[:, r, :], got[:, r, :], start=True,
                                  stop=True).then_inc(summed, 1)
                by_slots(pe, body)

            @block.vector
            def _(v):
                v.memset(acc[:, :, :], 0.0).then_inc(clear, 1)
                v.wait_ge(clear, 1)

                places = Rows(v, name + "_tile", c.tile_row, NODE_TILES - 1)

                def body(s, i):
                    for r in range(RING):
                        add_sum(v, s, r, i, places, summed, added, lambda t: acc[:, ds(t, 1), :],
                                c.ps[r % BUFS][0:P, 0:D].unsqueeze(1))
                        if before_end(s, r, RING):
                            one_hot(v, c, hot, s, r, hot_ready, ahead=RING)
                for r in range(RING):
                    one_hot(v, c, hot, 0, r, hot_ready)
                by_slots(v, body)
                places.free()


def tile_at(t, n=1):
    return slice(t, t + n) if isinstance(t, int) else ds(t, n)


def flat(ap):
    return ap.rearrange("p a d -> p (a d)")


def conv_and_router(nc, c, acc, x1, logits):
    with ExitStack() as ctx:
        def sb(name, shape, dt=F32):
            return ctx.enter_context(nc.sbuf_tensor(name, shape, dt))
        w = sb("w_conv", [128, 2, KC, D])
        wg = sb("w_router", [128, KC, EXPERTS])
        bias, bias2, bg = sb("conv_bias", [P, D]), sb("conv_bias2", [P, D]), sb("router_bias", [P, EXPERTS])
        cat = sb("conv_cat", [P, 2, 2 * D])
        cat_t = sb("conv_t", [128, 2, 2 * KC, P])
        x1s = sb("x1s", [P, 2, D])
        x1_t = sb("x1_t", [128, 2, KC, P])
        load, chain, cat_ready, turned, t_ready, conv, x1_ready, x1_turned, x1_t_ready, routed, log_ready = (
            c.sem(n) for n in ("conv_loads", "conv_chain", "conv_cat_ready", "conv_turned", "conv_t_ready", "conv_done",
                               "x1_ready", "x1_turned", "x1_t_ready", "routed", "logits_ready"))
        copied = c.sem("conv_copied")
        with nc.Block() as block:
            @block.sync
            def _(sp):
                for k, a in enumerate((c.W_gc, c.W_res)):
                    sp.dma_start(w[:, k], a.rearrange("(c p) o -> p c o", p=128)).then_inc(load, 16)
                sp.dma_start(wg[:, :, :], c.Wg.rearrange("(c p) o -> p c o", p=128)).then_inc(load, 16)
                sp.dma_start(bias[:, :], c.b_gc.partition_broadcast(P)).then_inc(load, 16)
                sp.dma_start(bias2[:, :], c.b_res.partition_broadcast(P)).then_inc(load, 16)
                sp.dma_start(bg[:, :], c.bg.partition_broadcast(P)).then_inc(load, 16)

            @block.vector
            def _(v):
                do = Chain(v, chain)
                v.wait_ge(load, 96)
                do(v.tensor_tensor(bias[:, :], bias[:, :], bias2[:, :], ALU.add))

                def body(t, b, uses):
                    if known(t, 2):
                        v.wait_ge(turned, t - 1)
                    v.tensor_scalar(cat[:, b, 0:D], flat(acc[:, tile_at(t), :]), c.rdeg[:, tile_at(t)], None,
                                    ALU.mult).then_inc(cat_ready, 1)
                    v.wait_ge(conv, t + 1)
                    if known(t, 2):
                        v.wait_ge(x1_turned, t - 1)
                        v.wait_ge(copied, 2 * t - 2)
                    v.tensor_tensor(x1s[:, b, :], c.ps[2 + b][0:P, 0:D], bias[:, :], ALU.add).then_inc(x1_ready, 1)
                    v.wait_ge(routed, t + 1)
                    v.tensor_tensor(flat(logits[:, tile_at(t), :]), c.ps[6 + b][0:P, 0:EXPERTS], bg[:, :],
                                    ALU.add).then_inc(log_ready, 1)
                by_tiles(v, body)

            @block.scalar
            def _(a):
                def body(t, b, uses):
                    if known(t, 2):
                        a.wait_ge(turned, t - 1)
                    a.copy(cat[:, b, D:2 * D], flat(c.nodes[:, tile_at(t), :])).then_inc(copied, 1)
                    a.wait_ge(turned, t + 1)
                    if known(t, 2):
                        a.wait_ge(conv, t - 1)
                    a.copy(cat_t[:, b], c.ps[b][:, 0:2 * KC * P].rearrange("p (c n) -> p c n", n=P)).then_inc(t_ready, 1)
                    a.wait_ge(x1_turned, t + 1)
                    if known(t, 2):
                        a.wait_ge(routed, t - 1)
                    a.copy(x1_t[:, b], c.ps[4 + b][:, 0:KC * P].rearrange("p (c n) -> p c n", n=P)).then_inc(x1_t_ready, 1)
                    a.wait_ge(x1_ready, t + 1)
                    a.copy(flat(x1[:, tile_at(t), :]), x1s[:, b, :]).then_inc(copied, 1)
                by_tiles(a, body)

            @block.tensor
            def _(pe):
                pe.wait_ge(load, 96)

                def body(t, b, uses):
                    pe.wait_ge(cat_ready, t + 1)
                    pe.wait_ge(copied, 2 * t + 1)
                    if known(t, 2):
                        pe.wait_ge(t_ready, t - 1)
                    for k in range(2 * KC):
                        mm = pe.transpose(c.ps[b][:, k * P:(k + 1) * P], cat[:, b, k * 128:(k + 1) * 128],
                                          c.ident[0:P, 0:P])
                    mm.then_inc(turned, 1)
                    pe.wait_ge(t_ready, t + 1)
                    if known(t, 2):
                        pe.wait_ge(x1_ready, t - 1)
                    for k in range(2 * KC):
                        mm = pe.matmul(c.ps[2 + b][0:P, 0:D], cat_t[:, b, k, :], w[:, k // KC, k % KC, :],
                                       start=(k == 0), stop=(k == 2 * KC - 1))
                    mm.then_inc(conv, 1)
                    pe.wait_ge(x1_ready, t + 1)
                    if known(t, 2):
                        pe.wait_ge(x1_t_ready, t - 1)
                    for k in range(KC):
                        mm = pe.transpose(c.ps[4 + b][:, k * P:(k + 1) * P], x1s[:, b, k * 128:(k + 1) * 128],
                                          c.ident[0:P, 0:P])
                    mm.then_inc(x1_turned, 1)
                    pe.wait_ge(x1_t_ready, t + 1)
                    if known(t, 2):
                        pe.wait_ge(log_ready, t - 1)
                    for k in range(KC):
                        mm = pe.matmul(c.ps[6 + b][0:P, 0:EXPERTS], x1_t[:, b, k, :], wg[:, k, :],
                                       start=(k == 0), stop=(k == KC - 1))
                    mm.then_inc(routed, 1)
                by_tiles(pe, body)


def route(nc, c, x1, logits):
    with ExitStack() as ctx:
        def sb(name, shape, dt=F32):
            return ctx.enter_context(nc.sbuf_tensor(name, shape, dt))
        T, X = NODE_TILES, EXPERTS
        wide = [P, T, X]
        iota_m = sb("iota_m", [P, X])
        pick = [sb("pick0", wide), sb("pick1", wide)]
        both, before, work, run = sb("both", wide), sb("before", wide), sb("work", wide), sb("run", [P, T + 1, X])
        val = [sb("val0", [P, T]), sb("val1", [P, T])]
        idx, base, total = sb("idx", [P, T]), sb("base", [P, X]), sb("total", [P, X])
        rank, gap = sb("rank", [P, T]), sb("gap", [P, T])
        pos_f = sb("pos_f", [P, T])
        row_i, row_f = sb("row_ids_i", [P, ROW_TILES], I32), sb("row_ids", [P, ROW_TILES])
        key, key_i = sb("step_key", [P, X]), sb("step_key_i", [P, X], I32)
        lim_i, lim = sb("step_lim_i", [P, STEPS], I32), sb("step_lim", [P, STEPS])
        step_i, tile = sb("step_i", [P, STEPS], I32), sb("step_tile", [P, STEPS])
        grid = sb("grid", [P, STEPS, X])
        chain, act_s, pe_s, iotas, run_ready, pfx, rows_in, pos_ready = (
            c.sem(n) for n in ("route_chain", "route_exp", "route_mm", "route_iotas", "run_ready", "prefix_copied",
                               "rows_stored", "positions_ready"))

        def over_experts(ap):
            return ap.unsqueeze(2).to_broadcast(wide)

        def over_tiles(ap):
            return ap.unsqueeze(1).to_broadcast(wide)

        with nc.Block() as block:
            @block.gpsimd
            def _(pool):
                pool.iota(row_i[:, :], [[P, ROW_TILES]], base=0, channel_multiplier=1).then_inc(iotas, 1)
                pool.iota(key_i[:, :], [[P, X]], base=0, channel_multiplier=0).then_inc(iotas, 1)
                pool.iota(lim_i[:, :], [[P, STEPS]], base=P, channel_multiplier=0).then_inc(iotas, 1)
                pool.iota(step_i[:, :], [[1, STEPS]], base=0, channel_multiplier=0).then_inc(iotas, 1)
                pool.wait_ge(pos_ready, 1)
                for k in range(TOPK):
                    for t in range(T):
                        pool.indirect_dma_start(c.row_table, bass.IndirectOffsetOnAxis(c.pos[k][:, t:t + 1], 0),
                                                x1[:, t, :], None).then_inc(rows_in, 16)
                pool.wait_ge(rows_in, 16 * TOPK * T)

            @block.scalar
            def _(a):
                a.wait_ge(run_ready, 1)
                a.activation(gap[:, :], gap[:, :], ACT.Exp).then_inc(act_s, 1)

                def body(t, b, uses):
                    a.wait_ge(pe_s, t + 1)
                    a.copy(flat(before[:, tile_at(t), :]), c.ps[b][0:P, 0:X]).then_inc(pfx, 1)
                by_tiles(a, body)

            @block.tensor
            def _(pe):
                pe.wait_ge(run_ready, 2)

                def body(t, b, uses):
                    if known(t, 2):
                        pe.wait_ge(pfx, t - 1)
                    pe.matmul(c.ps[b][0:P, 0:X], c.below[0:P, 0:P], flat(both[:, tile_at(t), :]), start=True, stop=False)
                    pe.matmul(c.ps[b][0:P, 0:X], c.ones[0:P, 0:P], flat(run[:, tile_at(t), :]), start=False,
                              stop=True).then_inc(pe_s, 1)
                by_tiles(pe, body)
                pe.matmul(c.ps[2][0:P, 0:X], c.ones[0:P, 0:P], run[:, T, :], start=True, stop=True).then_inc(pe_s, 1)

            @block.vector
            def _(v):
                do = Chain(v, chain)
                do(v.tensor_scalar(iota_m[:, :], c.iota[0:P, 0:X], -float(X), None, ALU.add))
                for k in range(TOPK):
                    do(v.tensor_reduce(val[k][:, :], logits[:, :, :], AX, ALU.max))
                    do(v.tensor_tensor(work[:, :, :], logits[:, :, :], over_experts(val[k][:, :]), ALU.is_equal))
                    do(v.scalar_tensor_tensor(out=work[:, :, :], in0=work[:, :, :], scalar=-float(X),
                                              in1=over_tiles(c.iota[0:P, 0:X]), op0=ALU.mult, op1=ALU.add))
                    do(v.tensor_reduce(idx[:, :], work[:, :, :], AX, ALU.min))
                    do(v.tensor_tensor(pick[k][:, :, :], over_tiles(iota_m[:, :]), over_experts(idx[:, :]), ALU.is_equal))
                    if k == 0:
                        do(v.scalar_tensor_tensor(out=logits[:, :, :], in0=pick[0][:, :, :], scalar=-BIG,
                                                  in1=logits[:, :, :], op0=ALU.mult, op1=ALU.add))
                do(v.tensor_tensor(gap[:, :], val[1][:, :], val[0][:, :], ALU.subtract))
                v.sem_inc(run_ready, 1)
                do(v.tensor_tensor(both[:, :, :], pick[0][:, :, :], pick[1][:, :, :], ALU.add))
                do(v.memset(run[:, 0, :], 0.0))
                at = do.n

                def body(t, b, uses):
                    do.at(at + t)
                    n = t + 1
                    do(v.tensor_tensor(run[:, tile_at(n), :], run[:, tile_at(t), :], both[:, tile_at(t), :], ALU.add))
                by_tiles(v, body)
                do.at(at + T)
                v.sem_inc(run_ready, 1)
                v.wait_ge(act_s, 1)
                do(v.tensor_scalar(rank[:, :], gap[:, :], 1.0, None, ALU.add))
                do(v.reciprocal(c.gate[0][:, :], rank[:, :]))
                do(v.tensor_tensor(c.gate[1][:, :], gap[:, :], c.gate[0][:, :], ALU.mult))
                v.wait_ge(pe_s, T + 1)
                v.wait_ge(pfx, T)
                do(v.tensor_copy(total[:, :], c.ps[2][0:P, 0:X]))
                do(v.tensor_tensor_scan(base[:, :], c.ones[0:P, 0:X], total[:, :], 0.0, ALU.mult, ALU.add))
                do(v.tensor_tensor(base[:, :], base[:, :], total[:, :], ALU.subtract))
                for k in range(TOPK):
                    do(v.tensor_tensor(work[:, :, :], pick[k][:, :, :], before[:, :, :], ALU.mult))
                    do(v.tensor_reduce(rank[:, :], work[:, :, :], AX, ALU.add))
                    do(v.scalar_tensor_tensor(out=c.gate[k][:, :], in0=rank[:, :], scalar=float(CAP),
                                              in1=c.gate[k][:, :], op0=ALU.is_lt, op1=ALU.mult))
                    do(v.tensor_tensor(work[:, :, :], pick[k][:, :, :], over_tiles(base[:, :]), ALU.mult))
                    do(v.tensor_reduce(pos_f[:, :], work[:, :, :], AX, ALU.add))
                    do(v.tensor_tensor(pos_f[:, :], pos_f[:, :], rank[:, :], ALU.add))
                    do(v.tensor_copy(c.pos[k][:, :], pos_f[:, :]))
                v.sem_inc(pos_ready, 1)
                v.wait_ge(iotas, 4)
                for f, i in ((row_f, row_i), (key, key_i), (lim, lim_i), (tile, step_i)):
                    do(v.tensor_copy(f[:, :], i[:, :]))
                g = grid[:, 0:ROW_TILES, :]
                do(v.tensor_tensor(g, row_f[:, :].unsqueeze(2).to_broadcast([P, ROW_TILES, X]),
                                   base[:, :].unsqueeze(1).to_broadcast([P, ROW_TILES, X]), ALU.is_ge))
                do(v.tensor_reduce(c.row_expert[:, :], g, AX, ALU.add))
                do(v.tensor_scalar(c.row_expert[:, :], c.row_expert[:, :], -1.0, None, ALU.add))
                do(v.scalar_tensor_tensor(out=key[:, :], in0=base[:, :], scalar=float(ROW_TILES * P - 1), in1=key[:, :],
                                          op0=ALU.min, op1=ALU.add))
                do(v.tensor_tensor(grid[:, :, :], lim[:, :].unsqueeze(2).to_broadcast([P, STEPS, X]),
                                   key[:, :].unsqueeze(1).to_broadcast([P, STEPS, X]), ALU.is_gt))
                do(v.tensor_reduce(c.step_expert[:, :], grid[:, :, :], AX, ALU.add))
                do(v.tensor_scalar(c.step_expert[:, :], c.step_expert[:, :], -1.0, None, ALU.add))
                do(v.tensor_tensor(tile[:, :], tile[:, :], c.step_expert[:, :], ALU.subtract))
                do(v.tensor_copy(c.step_rows[0:1, 0, :], tile[0:1, :]))
                do(v.tensor_copy(c.step_rows[0:1, 1, :], c.step_expert[0:1, :]))


def experts(nc, c):
    with ExitStack() as ctx:
        def sb(name, shape, dt=F32):
            return ctx.enter_context(nc.sbuf_tensor(name, shape, dt))
        w1, w2 = sb("w1", [128, WRING, KC, HIDDEN]), sb("w2", [128, WRING, HC, D])
        b1, b2 = sb("b1", [128, WRING, HC]), sb("b2", [1, WRING, D])
        xr = sb("xr", [P, WRING, D])
        xt = sb("xr_t", [128, 2, KC, P])
        h = sb("hidden", [128, 2, HC, P])
        mask = sb("row_mask", [P, 2, 1])
        y = sb("expert_rows", [P, ROW_TILES, D])
        loaded = [c.sem(f"weights_in{b}") for b in range(WRING)]
        turned, xt_ready, up, act_s, down, kept, mask_s, clear, stored, seen = (
            c.sem(n) for n in ("rows_turned", "rows_t_ready", "up_done", "gelu_done", "down_done", "rows_kept",
                               "row_mask_ready", "rows_clear", "expert_rows_stored", "expert_seen"))
        with nc.Block() as block:
            @block.sync
            def _(sp):
                def body(s, b, uses):
                    j = sp.value_load(c.step_rows[0:1, 0, tile_at(s)], min_val=0, max_val=ROW_TILES - 1)
                    e = sp.value_load(c.step_rows[0:1, 1, tile_at(s)], min_val=0, max_val=EXPERTS - 1)
                    if known(s, WRING):
                        sp.wait_ge(down, s - WRING + 1)
                    sp.dma_start(xr[:, b, :], c.row_table[ds(j * P, P), :]).then_inc(loaded[b], 16)
                    sp.dma_start(w1[:, b], c.w1[ds(e, 1)].rearrange("a (c p) h -> p (a c) h", p=128)).then_inc(loaded[b], 16)
                    sp.dma_start(b1[:, b, :], c.b1[ds(e, 1)].rearrange("a p c -> (a p) c")).then_inc(loaded[b], 16)
                    sp.dma_start(w2[:, b], c.w2[ds(e, 1)].rearrange("a (c p) h -> p (a c) h", p=128)).then_inc(loaded[b], 16)
                    sp.dma_start(b2[:, b, :], c.b2[ds(e, 1)]).then_inc(loaded[b], 16)
                by_ring(sp, body, STEPS, WRING)
                sp.wait_ge(kept, STEPS)
                sp.dma_start(c.expert_table.rearrange("(j p) d -> p j d", p=P), y[:, :, :]).then_inc(stored, 16)
                sp.wait_ge(stored, 16)

            @block.tensor
            def _(pe):
                def down_layer(s, b):
                    pe.wait_ge(act_s, HC * s + HC)
                    if known(s, 2):
                        pe.wait_ge(kept, s - 1)
                    for m in range(HC):
                        pe.matmul(c.ps[4 + b % 2][0:P, 0:D], h[:, b % 2, m, :], w2[:, b, m, :], start=(m == 0), stop=False)
                    pe.matmul(c.ps[4 + b % 2][0:P, 0:D], c.ones[0:1, 0:P], b2[:, b, :], start=False,
                              stop=True).then_inc(down, 1)

                def body(s, b, uses):
                    pe.wait_ge(loaded[b], 80 * (uses + 1))
                    if known(s, 2):
                        pe.wait_ge(xt_ready, s - 1)
                    for k in range(KC):
                        mm = pe.transpose(c.ps[b % 2][:, k * P:(k + 1) * P], xr[:, b, k * 128:(k + 1) * 128],
                                          c.ident[0:P, 0:P])
                    mm.then_inc(turned, 1)
                    pe.wait_ge(xt_ready, s + 1)
                    if known(s, 2):
                        pe.wait_ge(act_s, HC * s - HC)
                    for m in range(HC):
                        for k in range(KC):
                            mm = pe.matmul(c.ps[2 + b % 2][:, m * P:(m + 1) * P], w1[:, b, k, m * 128:(m + 1) * 128],
                                           xt[:, b % 2, k, :], start=(k == 0), stop=(k == KC - 1))
                    mm.then_inc(up, 1)
                    if known(s, 1):
                        down_layer(s - 1, (b - 1) % WRING)
                by_ring(pe, body, STEPS, WRING)
                down_layer(STEPS - 1, (STEPS - 1) % WRING)

            @block.scalar
            def _(a):
                def body(s, b, uses):
                    a.wait_ge(up, s + 1)
                    if known(s, 2):
                        a.wait_ge(down, s - 1)
                    for m in range(HC):
                        a.activation(h[:, b % 2, m, :], c.ps[2 + b % 2][:, m * P:(m + 1) * P], ACT.Gelu,
                                     bias=b1[:, b, m:m + 1]).then_inc(act_s, 1)
                by_ring(a, body, STEPS, WRING)

            @block.vector
            def _(v):
                v.memset(y[:, :, :], 0.0).then_inc(clear, 1)
                v.wait_ge(clear, 1)

                def keep(s, b):
                    j = v.value_load(c.step_rows[0:1, 0, tile_at(s)], min_val=0, max_val=ROW_TILES - 1)
                    if known(s, 1):
                        v.wait_ge(kept, s)
                    v.tensor_scalar(mask[:, b % 2, :], c.row_expert[:, ds(j, 1)], c.step_expert[:, tile_at(s)], None,
                                    ALU.is_equal).then_inc(mask_s, 1)
                    v.wait_ge(mask_s, s + 1)
                    v.wait_ge(down, s + 1)
                    to = y[:, ds(j, 1), :]
                    v.scalar_tensor_tensor(out=to, in0=c.ps[4 + b % 2][0:P, 0:D].unsqueeze(1), scalar=mask[:, b % 2, :],
                                           in1=to, op0=ALU.mult, op1=ALU.add).then_inc(kept, 1)

                def body(s, b, uses):
                    v.wait_ge(turned, s + 1)
                    if known(s, 2):
                        v.wait_ge(up, s - 1)
                    v.tensor_copy(xt[:, b % 2], c.ps[b % 2][:, 0:KC * P].rearrange("p (c n) -> p c n", n=P)).then_inc(xt_ready, 1)
                    if known(s, 1):
                        keep(s - 1, (b - 1) % WRING)
                by_ring(v, body, STEPS, WRING)
                keep(STEPS - 1, (STEPS - 1) % WRING)


def combine(nc, c, x1):
    with nc.sbuf_tensor("chosen0", [P, NODE_TILES, D], F32) as y0, nc.sbuf_tensor("chosen1", [P, NODE_TILES, D], F32) as y1:
        G = 5
        got = [c.sem(f"chosen_in{g}") for g in range(NODE_TILES // G)]
        added = c.sem("chosen_added")
        with nc.Block() as block:
            @block.gpsimd
            def _(pool):
                for t in range(NODE_TILES):
                    for k, y in enumerate((y0, y1)):
                        pool.indirect_dma_start(y[:, t, :], None, c.expert_table,
                                                bass.IndirectOffsetOnAxis(c.pos[k][:, t:t + 1], 0)).then_inc(got[t // G], 16)

            @block.vector
            def _(v):
                for t in range(NODE_TILES):
                    if t % G == 0:
                        v.wait_ge(got[t // G], 16 * G * TOPK)
                    for k, y in enumerate((y0, y1)):
                        if t or k:
                            v.wait_ge(added, 2 * t + k)
                        v.scalar_tensor_tensor(out=x1[:, t, :], in0=y[:, t, :], scalar=c.gate[k][:, t:t + 1],
                                               in1=x1[:, t, :], op0=ALU.mult, op1=ALU.add).then_inc(added, 1)


def batch_norm(nc, c, name, y, gamma, beta):
    with ExitStack() as ctx:
        def sb(n, shape, dt=F32):
            return ctx.enter_context(nc.sbuf_tensor(name + n, shape, dt))
        g, be = sb("_gamma", [P, D]), sb("_beta", [P, D])
        mean, rstd = sb("_mean", [P, D]), sb("_rstd", [P, D])
        sq = sb("_sq", [P, NODE_TILES, D])
        load, chain, mm, act_s = (c.sem(name + n) for n in ("_loads", "_chain", "_sums", "_act"))
        wide = [P, NODE_TILES, D]

        def over_tiles(ap):
            return ap.unsqueeze(1).to_broadcast(wide)
        with nc.Block() as block:
            @block.sync
            def _(sp):
                sp.dma_start(g[:, :], gamma.partition_broadcast(P)).then_inc(load, 16)
                sp.dma_start(be[:, :], beta.partition_broadcast(P)).then_inc(load, 16)

            @block.tensor
            def _(pe):
                for k, src in enumerate((y, sq)):
                    if k:
                        pe.wait_ge(act_s, 1)
                    for t in range(NODE_TILES):
                        m = pe.matmul(c.ps[k][0:P, 0:D], c.ones[0:P, 0:P], src[:, t, :], start=(t == 0),
                                      stop=(t == NODE_TILES - 1))
                    m.then_inc(mm, 1)

            @block.scalar
            def _(a):
                a.wait_ge(chain, 2)
                a.activation(sq[:, :, :], y[:, :, :], ACT.Square).then_inc(act_s, 1)
                a.wait_ge(chain, 3)
                a.activation(rstd[:, :], rstd[:, :], ACT.Sqrt).then_inc(act_s, 1)

            @block.vector
            def _(v):
                do = Chain(v, chain)
                v.wait_ge(mm, 1)
                do(v.tensor_scalar(mean[:, :], c.ps[0][0:P, 0:D], 1.0 / N, None, ALU.mult))
                do(v.tensor_tensor(y[:, :, :], y[:, :, :], over_tiles(mean[:, :]), ALU.subtract))
                v.wait_ge(mm, 2)
                do(v.tensor_scalar(rstd[:, :], c.ps[1][0:P, 0:D], 1.0 / N, BN_EPS, ALU.mult, ALU.add))
                v.wait_ge(act_s, 2)
                do(v.reciprocal(rstd[:, :], rstd[:, :]))
                v.wait_ge(load, 32)
                do(v.tensor_tensor(rstd[:, :], rstd[:, :], g[:, :], ALU.mult))
                do(v.tensor_tensor(y[:, :, :], y[:, :, :], over_tiles(rstd[:, :]), ALU.mult))
                do(v.tensor_tensor(y[:, :, :], y[:, :, :], over_tiles(be[:, :]), ALU.add))
                do(v.tensor_tensor(y[:, :, :], y[:, :, :], c.nodes[:, :, :], ALU.add))


def linear(nc, c, acc, y):
    with ExitStack() as ctx:
        def sb(name, shape, dt=F32):
            return ctx.enter_context(nc.sbuf_tensor(name, shape, dt))
        w, bias = sb("w_lin", [128, KC, D]), sb("lin_bias", [P, D])
        hs, ht = sb("lin_h", [P, 2, D]), sb("lin_ht", [128, 2, KC, P])
        load, ready, turned, t_ready, mixed, out = (
            c.sem(n) for n in ("lin_loads", "lin_h_ready", "lin_turned", "lin_t_ready", "lin_mixed", "lin_out"))
        with nc.Block() as block:
            @block.sync
            def _(sp):
                sp.dma_start(w[:, :, :], c.w_linT.rearrange("(c p) o -> p c o", p=128)).then_inc(load, 16)
                sp.dma_start(bias[:, :], c.b_lin.partition_broadcast(P)).then_inc(load, 16)

            @block.vector
            def _(v):
                v.wait_ge(load, 32)

                def last(t, b):
                    v.wait_ge(mixed, t + 1)
                    v.tensor_tensor(flat(y[:, tile_at(t), :]), c.ps[2 + b][0:P, 0:D], bias[:, :], ALU.add).then_inc(out, 1)

                def body(t, b, uses):
                    if known(t, 2):
                        v.wait_ge(turned, t - 1)
                    v.tensor_tensor(hs[:, b, :], flat(acc[:, tile_at(t), :]), flat(c.nodes[:, tile_at(t), :]),
                                    ALU.add).then_inc(ready, 1)
                    if known(t, 1):
                        last(t - 1, 1 - b)
                by_tiles(v, body)
                last(NODE_TILES - 1, (NODE_TILES - 1) % 2)

            @block.scalar
            def _(a):
                def body(t, b, uses):
                    a.wait_ge(turned, t + 1)
                    if known(t, 2):
                        a.wait_ge(mixed, t - 1)
                    a.copy(ht[:, b], c.ps[b][:, 0:KC * P].rearrange("p (c n) -> p c n", n=P)).then_inc(t_ready, 1)
                by_tiles(a, body)

            @block.tensor
            def _(pe):
                pe.wait_ge(load, 32)

                def body(t, b, uses):
                    pe.wait_ge(ready, t + 1)
                    if known(t, 2):
                        pe.wait_ge(t_ready, t - 1)
                    for k in range(KC):
                        mm = pe.transpose(c.ps[b][:, k * P:(k + 1) * P], hs[:, b, k * 128:(k + 1) * 128], c.ident[0:P, 0:P])
                    mm.then_inc(turned, 1)
                    pe.wait_ge(t_ready, t + 1)
                    if known(t, 2):
                        pe.wait_ge(out, t - 1)
                    for k in range(KC):
                        mm = pe.matmul(c.ps[2 + b][0:P, 0:D], ht[:, b, k, :], w[:, k, :], start=(k == 0), stop=(k == KC - 1))
                    mm.then_inc(mixed, 1)
                by_tiles(pe, body)


PARTS = 3


def split_edge_product(nc, c):
    G, H = 5, 2
    T, K = EDGE_TILES // G, ATTRS // H
    steps = [(g, h) for g in range(G) for h in range(H)]
    with ExitStack() as ctx:
        def sb(name, shape, dt=F32):
            return ctx.enter_context(nc.sbuf_tensor(name, shape, dt))
        a = sb("attr_in", [T, 2, K, P])
        parts = sb("attr_split", [T, 2, PARTS, K, 2, P], BF16)
        w, w_parts = sb("edge_w_in", [ATTRS + 1, D]), sb("edge_w_split", [ATTRS + 1, PARTS, D], BF16)
        loaded = [c.sem(f"attr_loaded{b}") for b in range(2)]
        stored = [c.sem(f"attr_stored{b}") for b in range(2)]
        w_load, w_chain, w_done, w_put, high, rest, mid, low, high_copy, high_copy2, mid_copy = (
            c.sem(n) for n in ("edge_w_loads", "edge_w_chain", "edge_w_done", "edge_w_put", "attr_high", "attr_rest",
                               "attr_mid", "attr_low", "attr_high_copy", "attr_high_copy2", "attr_mid_copy"))
        with nc.Block() as block:
            @block.sync
            def _(sp):
                def fetch(n):
                    g, h = steps[n]
                    sp.dma_start(a[:, n % 2], c.attrT[g * T:(g + 1) * T, h * K:(h + 1) * K, :])\
                        .then_inc(loaded[n % 2], 16)
                sp.dma_start(w[0:ATTRS, :], c.edge_w).then_inc(w_load, 16)
                sp.dma_start(w[ATTRS:ATTRS + 1, :], c.edge_b).then_inc(w_load, 16)
                fetch(0)
                fetch(1)
                for n, (g, h) in enumerate(steps):
                    sp.wait_ge(low, n + 1)
                    if n + 2 < len(steps):
                        fetch(n + 2)
                    for copy in (high_copy, high_copy2, mid_copy):
                        sp.wait_ge(copy, n + 1)
                    sp.dma_start(c.attr_parts[g * T:(g + 1) * T].rearrange("j (q k) b e -> j q (k b e)", q=PARTS)
                                 [:, :, h * K * 2 * P:(h + 1) * K * 2 * P],
                                 parts[:, n % 2].rearrange("j q k b e -> j q (k b e)")).then_inc(stored[n % 2], 16)
                sp.wait_ge(w_done, 1)
                for row, b, part in ((0, 0, 0), (1, 0, 1), (2, 0, 2), (0, 1, 0), (1, 1, 1), (2, 1, 0)):
                    sp.dma_start(c.ew_parts[row * ATTRS:(row + 1) * ATTRS, b, :], w_parts[0:ATTRS, part, :])\
                        .then_inc(w_put, 16)
                for q in range(PARTS):
                    row = PARTS * ATTRS + q
                    sp.dma_start(c.ew_parts[row:row + 1, 0, :], w_parts[ATTRS:ATTRS + 1, q, :]).then_inc(w_put, 16)
                sp.wait_ge(w_put, 16 * (2 * PARTS + PARTS))
                for b in range(2):
                    sp.wait_ge(stored[b], 16 * (len(steps) // 2))

            @block.scalar
            def _(act):
                for n in range(len(steps) + 1):
                    if n < len(steps):
                        act.wait_ge(loaded[n % 2], 16 * (n // 2 + 1))
                        if n >= 2:
                            act.wait_ge(stored[n % 2], 16 * (n // 2))
                        act.copy(parts[:, n % 2, 0, :, 0, :], a[:, n % 2]).then_inc(high, 1)
                        act.wait_ge(high, n + 1)
                        act.copy(parts[:, n % 2, 1, :, 0, :], parts[:, n % 2, 0, :, 0, :]).then_inc(high_copy, 1)
                    if n >= 1:
                        act.wait_ge(rest, n)
                        act.copy(parts[:, (n - 1) % 2, 0, :, 1, :], a[:, (n - 1) % 2]).then_inc(mid, 1)

            @block.gpsimd
            def _(pool):
                for n in range(len(steps)):
                    pool.wait_ge(high, n + 1)
                    pool.tensor_copy(parts[:, n % 2, 2, :, 0, :], parts[:, n % 2, 0, :, 0, :]).then_inc(high_copy2, 1)

            @block.vector
            def _(v):
                do = Chain(v, w_chain)
                v.wait_ge(w_load, 32)
                do(v.tensor_copy(w_parts[:, 0, :], w[:, :]))
                do(v.tensor_tensor(w[:, :], w[:, :], w_parts[:, 0, :], ALU.subtract))
                do(v.tensor_copy(w_parts[:, 1, :], w[:, :]))
                do(v.tensor_tensor(w_parts[:, 2, :], w[:, :], w_parts[:, 1, :], ALU.subtract))
                v.sem_inc(w_done, 1)
                for n in range(len(steps) + 1):
                    if n < len(steps):
                        v.wait_ge(high, n + 1)
                        v.tensor_tensor(a[:, n % 2], a[:, n % 2], parts[:, n % 2, 0, :, 0, :], ALU.subtract)\
                            .then_inc(rest, 1)
                    if n >= 1:
                        b = (n - 1) % 2
                        v.wait_ge(mid, n)
                        v.tensor_tensor(parts[:, b, 2, :, 1, :], a[:, b], parts[:, b, 0, :, 1, :], ALU.subtract)\
                            .then_inc(low, 1)
                        v.tensor_copy(parts[:, b, 1, :, 1, :], parts[:, b, 0, :, 1, :]).then_inc(mid_copy, 1)


def relation_pass(nc, c, name, table, acc):
    COLS, LAG, EW = REL3 * WIN, 2, BUFS
    K = PARTS * ATTRS
    with ExitStack() as ctx:
        def sb(n, shape, dt=F32):
            return ctx.enter_context(nc.sbuf_tensor(name + n, shape, dt))
        got = sb("_got", [P, RING, D])
        rows = sb("_rows", [P, RING], I32)
        hot = sb("_hot", [P, RING, COLS])
        attr = sb("_attr", [K + PARTS, RING, 2, P], BF16)
        prod = sb("_prod", [P, BUFS, D])
        msg = sb("_msg", [P, BUFS, D])
        filled = [c.sem(f"{name}_in{r}") for r in range(RING)]
        attr_in = [c.sem(f"{name}_attr_in{r}") for r in range(RING)]
        (copied, let_go, hot_ready, scaled, prod_done, msg_ready, summed, added, clear) = (
            c.sem(name + n) for n in ("_rows_copied", "_pool_seen", "_hot_ready", "_edge_scale", "_prod_done",
                                      "_msg_ready", "_summed", "_added", "_clear"))
        with nc.Block() as block:
            @block.gpsimd
            def _(pool):
                gather_rows(pool, rows, got, prod_done, copied, table, filled, let_go, WSLOTS)

            @block.sync
            def _(sp):
                tiles = Rows(sp, name + "_edge_tile", c.win_edge_row, EDGE_TILES - 1)

                def body(s, i):
                    for r in range(RING):
                        j = tiles.at(i, r)
                        if known(s, 1):
                            sp.wait_ge(scaled, s + r - RING + 1)
                        sp.dma_start(attr[0:K, r], c.attr_parts[ds(j, 1)].rearrange("a k b e -> (a k) b e"))\
                            .then_inc(attr_in[r], 16)
                by_slots(sp, body, WSLOTS)
                tiles.free()

            @block.scalar
            def _(a):
                def body(s, i):
                    for r in range(RING):
                        a.wait_ge(prod_done, s + r + 1)
                        if known(s, 1) or r >= BUFS:
                            a.wait_ge(summed, s + r - BUFS + 1)
                        a.activation(msg[:, r % BUFS, :], prod[:, r % BUFS, :], ACT.Relu).then_inc(msg_ready, 1)
                        copy_next_rows(a, s, i, r, c.win_src, rows, filled, copied, WSLOTS)
                copy_first_rows(a, c.win_src, rows, filled, copied)
                by_slots(a, body, WSLOTS)

            @block.tensor
            def _(pe):
                def scale(s, r, i, ahead=0):
                    n = r + ahead
                    pe.wait_ge(attr_in[n % RING], 16 * (i + n // RING + 1))
                    if known(s, 1) or n >= EW:
                        pe.wait_ge(prod_done, s + n - EW + 1)
                    pe.matmul(c.ps[n % EW][0:P, 0:D], attr[:, n % RING, 0, :], c.ew_parts[:, 0, :], start=True,
                              stop=False)
                    pe.matmul(c.ps[n % EW][0:P, 0:D], attr[0:K, n % RING, 1, :], c.ew_parts[0:K, 1, :], start=False,
                              stop=True).then_inc(scaled, 1)

                def body(s, i):
                    for r in range(RING):
                        if before_end(s, r, EW - 1, WSLOTS):
                            scale(s, r, i, EW - 1)
                        pe.wait_ge(msg_ready, s + r + 1)
                        pe.wait_ge(hot_ready, s + r + 1)
                        if known(s, 1) or r >= 2:
                            pe.wait_ge(added, s + r - 1)
                        for k in range(KC):
                            mm = pe.matmul(c.ps[6 + r % 2][:, k * COLS:(k + 1) * COLS],
                                           msg[:, r % BUFS, k * 128:(k + 1) * 128], hot[:, r, :], start=True, stop=True)
                        mm.then_inc(summed, 1)
                pe.wait_ge(clear, 2)
                for r in range(EW - 1):
                    scale(0, r, 0)
                by_slots(pe, body, WSLOTS)

            @block.vector
            def _(v):
                v.memset(attr[K:K + PARTS, :, 0, :], 1.0).then_inc(clear, 1)
                v.memset(acc[:, :, :], 0.0).then_inc(clear, 1)
                v.wait_ge(clear, 2)

                places = Rows(v, name + "_win", c.win_row, WIN * (WINS - 1))

                def add(s, n, i):
                    add_sum(v, s, n, i, places, summed, added, lambda t: acc[:, :, ds(t, WIN)],
                            c.ps[6 + n % 2][:, 0:KC * COLS].rearrange("p (g n) -> p g n", n=WIN))
                    if before_end(s, n, RING, WSLOTS):
                        one_hot(v, c, hot, s, n, hot_ready, c.win_key, COLS, RING)

                def body(s, i):
                    for r in range(RING):
                        v.wait_ge(scaled, s + r + 1)
                        v.wait_ge(filled[r], 16 * (i + 1))
                        if known(s, 1) or r >= BUFS:
                            v.wait_ge(msg_ready, s + r - BUFS + 1)
                        v.tensor_tensor(prod[:, r % BUFS, :], got[:, r, :], c.ps[r % EW][0:P, 0:D],
                                        ALU.mult).then_inc(prod_done, 1)
                        if known(s, 1) or r >= LAG:
                            add(s - RING, r - LAG + RING, i - 1) if r < LAG else add(s, r - LAG, i)
                for r in range(RING):
                    one_hot(v, c, hot, 0, r, hot_ready, c.win_key, COLS)
                by_slots(v, body, WSLOTS)
                for r in range(RING - LAG, RING):
                    add(WSLOTS - RING, r, WSLOTS // RING - 1)
                places.free()


def relation_mix(nc, c, name, layer, acc, x_table):
    R = REL3 + 1
    with ExitStack() as ctx:
        def sb(n, shape, dt=F32):
            return ctx.enter_context(nc.sbuf_tensor(name + n, shape, dt))
        w, bias = sb("_w", [128, R, KC, D]), sb("_bias", [P, D])
        agg, xs, xt = sb("_agg", [128, 2, KC * REL3, P]), sb("_x", [P, 2, D]), sb("_xt", [128, 2, KC, P])
        out_s = sb("_sum", [P, 2, D])
        load, agg_ready, turned, t_ready, mixed, chain, out, stored = (
            c.sem(name + n) for n in ("_loads", "_agg_ready", "_turned", "_t_ready", "_mixed", "_sum_chain", "_out",
                                      "_stored"))
        with nc.Block() as block:
            @block.sync
            def _(sp):
                sp.dma_start(w[:, 0:REL3], c.weights[layer].rearrange("r (c p) o -> p r c o", p=128)).then_inc(load, 16)
                sp.dma_start(w[:, REL3], c.roots[layer].rearrange("(c p) o -> p c o", p=128)).then_inc(load, 16)
                sp.dma_start(bias[:, :], c.biases[layer].partition_broadcast(P)).then_inc(load, 16)
                if x_table is not None:
                    sp.wait_ge(out, NODE_TILES)
                    sp.dma_start(x_table.rearrange("(t p) d -> p t d", p=P), c.nodes[:, :, :]).then_inc(stored, 16)
                    sp.wait_ge(stored, 16)

            @block.scalar
            def _(a):
                def body(t, b, uses):
                    at = slice(t * P, (t + 1) * P) if isinstance(t, int) else ds(t * P, P)
                    if known(t, 2):
                        a.wait_ge(mixed, t - 1)
                    a.copy(xs[:, b, :], flat(c.nodes[:, tile_at(t), :])).then_inc(agg_ready, 1)
                    a.copy(agg[:, b], acc[:, :, at]).then_inc(agg_ready, 1)
                by_tiles(a, body)

            @block.tensor
            def _(pe):
                def turn(t, b):
                    pe.wait_ge(agg_ready, 2 * t + 1)
                    if known(t, 2):
                        pe.wait_ge(t_ready, t - 1)
                    for k in range(KC):
                        mm = pe.transpose(c.ps[4 + b][:, k * P:(k + 1) * P], xs[:, b, k * 128:(k + 1) * 128],
                                          c.ident[0:P, 0:P])
                    mm.then_inc(turned, 1)

                def body(t, b, uses):
                    turn(t, b)
                    pe.wait_ge(agg_ready, 2 * t + 2)
                    if known(t, 2):
                        pe.wait_ge(out, t - 1)
                    for r in range(R):
                        if r == REL3:
                            pe.wait_ge(t_ready, t + 1)
                        for k in range(KC):
                            lhs = agg[:, b, k * REL3 + r, :] if r < REL3 else xt[:, b, k, :]
                            mm = pe.matmul(c.pair[b][0:P, r * D:(r + 1) * D], lhs, w[:, r, k, :], start=(k == 0),
                                           stop=(k == KC - 1), skip_group_check=True)
                    mm.then_inc(mixed, 1)
                pe.wait_ge(load, 48)
                by_tiles(pe, body)

            @block.vector
            def _(v):
                v.wait_ge(load, 48)
                do = Chain(v, chain)

                def turn(t, b):
                    v.wait_ge(turned, t + 1)
                    v.tensor_copy(xt[:, b], c.ps[4 + b][:, 0:KC * P].rearrange("p (c n) -> p c n", n=P))\
                        .then_inc(t_ready, 1)

                def last(t, b):
                    do.at(R * t)
                    v.wait_ge(mixed, t + 1)
                    part = bias[:, :]
                    for r in range(REL3):
                        do(v.scalar_tensor_tensor(out=out_s[:, b, :], in0=c.pair[b][0:P, r * D:(r + 1) * D],
                                                  scalar=flat(c.cnt[:, tile_at(t), 1 + r:2 + r]), in1=part,
                                                  op0=ALU.mult, op1=ALU.add))
                        part = out_s[:, b, :]
                    do(v.tensor_tensor(part, part, c.pair[b][0:P, REL3 * D:R * D], ALU.add))
                    x = flat(c.nodes[:, tile_at(t), :])
                    v.scalar_tensor_tensor(out=x, in0=part, scalar=0.0, in1=x, op0=ALU.max,
                                           op1=ALU.add).then_inc(out, 1)

                def body(t, b, uses):
                    if known(t, 2):
                        v.wait_ge(mixed, t - 1)
                    turn(t, b)
                    if known(t, 1):
                        last(t - 1, 1 - b)
                by_tiles(v, body)
                last(NODE_TILES - 1, (NODE_TILES - 1) % 2)


def program(nc, c):
    outer = ExitStack()
    with outer:
        c.in_use = []

        def sem(name):
            c.in_use.append(nc.alloc_semaphore(name))
            return c.in_use[-1]
        c.sem = sem
        c.pair = [outer.enter_context(nc.psum_tensor(f"banks{k}", [128, 1024], F32)) for k in range(4)]
        c.ps = [c.pair[k // 2][:, k % 2 * 512:(k % 2 + 1) * 512] for k in range(8)]
        c.iota = outer.enter_context(nc.sbuf_tensor("iota", [128, IOTA], F32))
        c.part = outer.enter_context(nc.sbuf_tensor("part", [128, 1], F32))
        c.ident = outer.enter_context(nc.sbuf_tensor("ident", [128, 128], F32))
        c.ident16 = outer.enter_context(nc.sbuf_tensor("ident16", [128, 128], BF16))
        c.ones = outer.enter_context(nc.sbuf_tensor("ones", [128, 128], F32))
        c.below = outer.enter_context(nc.sbuf_tensor("below", [128, 128], F32))
        c.tile_row = outer.enter_context(nc.sbuf_tensor("tile_row", [1, ROUNDS, ROW16], I16))
        c.edge_row = None
        c.win_row = outer.enter_context(nc.sbuf_tensor("win_row", [1, WSLOTS // RING, ROW16], I16))
        c.win_edge_row = outer.enter_context(nc.sbuf_tensor("win_edge_row", [1, WSLOTS // RING, ROW16], I16))
        c.win_key = outer.enter_context(nc.sbuf_tensor("win_key", [P, WSLOTS], F32))
        c.win_src = outer.enter_context(nc.sbuf_tensor("win_src", [P, WSLOTS], I32))
        c.dloc = outer.enter_context(nc.sbuf_tensor("dloc", [P, SLOTS], F32))
        c.src_idx = outer.enter_context(nc.sbuf_tensor("src_idx", [P, SLOTS], I32))
        c.cnt = outer.enter_context(nc.sbuf_tensor("cnt", [P, NODE_TILES, 1 + REL3], F32))
        c.rdeg = outer.enter_context(nc.sbuf_tensor("rdeg", [P, NODE_TILES], F32))
        c.nodes = outer.enter_context(nc.sbuf_tensor("nodes", [P, NODE_TILES, D], F32))
        c.nodes_b = outer.enter_context(nc.sbuf_tensor("nodes_b", [P, NODE_TILES, D], F32))
        c.key_table = nc.dram_tensor("key_table", (RELS * N, D), F32, kind="Internal").ap()
        c.msg_table = nc.dram_tensor("msg_table", (RELS * N, D), F32, kind="Internal").ap()
        c.seq_dram = nc.dram_tensor("seq_dram", (HEADS + 2, SLOTS, P), F32, kind="Internal").ap()
        c.max_dram = nc.dram_tensor("max_dram", (HEADS, SLOTS, P), F32, kind="Internal").ap()

        c.x_table = [nc.dram_tensor(f"x_table{k}", (N, D), F32, kind="Internal").ap() for k in range(5)]
        c.row_table = nc.dram_tensor("row_table", (N * TOPK, D), F32, kind="Internal").ap()
        c.expert_table = nc.dram_tensor("expert_table", (N * TOPK, D), F32, kind="Internal").ap()
        c.attr_parts = nc.dram_tensor("attr_parts", (EDGE_TILES, PARTS * ATTRS, 2, P), BF16, kind="Internal").ap()
        c.rout = outer.enter_context(nc.sbuf_tensor("rout", [P, NODE_TILES], F32))

        constants(nc, c)
        out_degrees(nc, c)
        with ExitStack() as layer0:
            c.kv_idx = layer0.enter_context(nc.sbuf_tensor("kv_idx", [P, SLOTS], I32))
            c.valid = layer0.enter_context(nc.sbuf_tensor("valid", [P, SLOTS], F32))
            c.starts = layer0.enter_context(nc.sbuf_tensor("starts", [P, SLOTS], F32))
            c.ends = layer0.enter_context(nc.sbuf_tensor("ends", [P, SLOTS], F32))
            c.edge_cols = layer0.enter_context(nc.sbuf_tensor("edge_cols", [P, SLOTS, EXTRA], F32))
            c.type_row = layer0.enter_context(nc.sbuf_tensor("type_row", [128, N], I32))
            slot_tables(nc, c)
            project(nc, c)
            c.score = layer0.enter_context(nc.sbuf_tensor("score", [P, SLOTS, HEADS], F32))
            attention_scores(nc, c)
            segment_softmax(nc, c)
            c.acc = layer0.enter_context(nc.sbuf_tensor("acc0", [P, NODE_TILES, D + EXTRA], F32))
            weighted_messages(nc, c)
            attention_output(nc, c)
        row_norm(nc, c, "norm0", c.nodes_b, c.x_table[0], scale=c.rout)
        clear_semaphores(nc, c)

        with ExitStack() as layer1:
            x1 = c.nodes_b
            logits = layer1.enter_context(nc.sbuf_tensor("logits", [P, NODE_TILES, EXPERTS], F32))
            with nc.sbuf_tensor("acc1", [P, NODE_TILES, D], F32) as acc:
                graph_sum(nc, c, "sum1", c.x_table[0], acc)
                conv_and_router(nc, c, acc, x1, logits)
            c.gate = [layer1.enter_context(nc.sbuf_tensor(f"gate{k}", [P, NODE_TILES], F32)) for k in range(TOPK)]
            c.pos = [layer1.enter_context(nc.sbuf_tensor(f"pos{k}", [P, NODE_TILES], I32)) for k in range(TOPK)]
            c.row_expert = layer1.enter_context(nc.sbuf_tensor("row_expert", [P, ROW_TILES], F32))
            c.step_expert = layer1.enter_context(nc.sbuf_tensor("step_expert", [P, STEPS], F32))
            c.step_rows = layer1.enter_context(nc.sbuf_tensor("step_rows", [1, 2, STEPS], I32))
            route(nc, c, x1, logits)
            experts(nc, c)
            combine(nc, c, x1)
            batch_norm(nc, c, "bn1", x1, c.gamma, c.beta)
        row_norm(nc, c, "norm1", c.nodes_b, c.x_table[1])
        clear_semaphores(nc, c)

        with nc.sbuf_tensor("acc2", [P, NODE_TILES, D], F32) as acc:
            graph_sum(nc, c, "sum2", c.x_table[1], acc)
            linear(nc, c, acc, c.nodes_b)
        batch_norm(nc, c, "bn2", c.nodes_b, c.bn_w, c.bn_b)
        row_norm(nc, c, "norm2", c.nodes_b, c.x_table[2])

        clear_semaphores(nc, c)

        keep_input(nc, c)
        c.ew_parts = outer.enter_context(nc.sbuf_tensor("ew_parts", [PARTS * (ATTRS + 1), 2, D], BF16))
        split_edge_product(nc, c)
        for layer in range(3):
            with nc.sbuf_tensor(f"acc3_{layer}", [128, KC * REL3, WIN * WINS], F32) as acc:
                relation_pass(nc, c, f"rel{layer}", c.x_table[2 + layer], acc)
                relation_mix(nc, c, f"mix{layer}", layer, acc, c.x_table[3 + layer] if layer < 2 else None)
        add_input(nc, c)
        row_norm(nc, c, "norm3", c.nodes_b, c.out)


def clear_semaphores(nc, c):
    nc.all_engine_barrier()
    nc.clear_and_free_semaphores(c.in_use)
    c.in_use.clear()
    nc.all_engine_barrier()


def keep_input(nc, c):
    done = c.sem("input_kept")
    with nc.Block() as block:
        @block.vector
        def _(v):
            v.tensor_copy(c.nodes_b[:, :, :], c.nodes[:, :, :]).then_inc(done, 1)


def add_input(nc, c):
    done = c.sem("input_added")
    with nc.Block() as block:
        @block.vector
        def _(v):
            v.tensor_tensor(c.nodes_b[:, :, :], c.nodes_b[:, :, :], c.nodes[:, :, :], ALU.add).then_inc(done, 1)


_INS = {
    "x": ("x", lambda a: a), "xT": ("x", lambda a: a.T), "src": ("src", lambda a: a), "dst": ("dst", lambda a: a),
    "t3": ("edge_type_3", lambda a: a), "t8": ("edge_type_8", lambda a: a),
    "node_type": ("node_type_4", lambda a: a), "node_type_cols": ("node_type_4", lambda a: a.reshape(NODE_TILES, P).T),
    "wq": ("L0_gnn_q_linears", lambda a: a), "wk": ("L0_gnn_k_linears", lambda a: a),
    "wv": ("L0_gnn_v_linears", lambda a: a), "wa": ("L0_gnn_a_linears", lambda a: a),
    "attT": ("L0_gnn_relation_att", lambda a: a.transpose(0, 1, 3, 2)), "msg": ("L0_gnn_relation_msg", lambda a: a),
    "pri": ("L0_gnn_relation_pri", lambda a: a), "skip": ("L0_gnn_skip", lambda a: a),
    "W_gc": ("L1_gnn_W_gc", lambda a: a), "W_res": ("L1_gnn_W_res", lambda a: a), "b_gc": ("L1_gnn_b_gc", lambda a: a),
    "b_res": ("L1_gnn_b_res", lambda a: a), "Wg": ("L1_gnn_Wg", lambda a: a), "bg": ("L1_gnn_bg", lambda a: a),
    "w1": ("L1_gnn_w1", lambda a: a), "b1": ("L1_gnn_b1", lambda a: a.reshape(EXPERTS, HC, 128).transpose(0, 2, 1)),
    "w2": ("L1_gnn_w2", lambda a: a), "b2": ("L1_gnn_b2", lambda a: a), "gamma": ("L1_gnn_gamma", lambda a: a),
    "beta": ("L1_gnn_beta", lambda a: a), "w_linT": ("L2_gnn_W", lambda a: a.T), "b_lin": ("L2_gnn_b", lambda a: a),
    "bn_w": ("L2_gnn_bn_w", lambda a: a), "bn_b": ("L2_gnn_bn_b", lambda a: a),
    "weights": ("L3_gnn_weights", lambda a: a), "roots": ("L3_gnn_roots", lambda a: a),
    "biases": ("L3_gnn_biases", lambda a: a), "edge_w": ("L3_gnn_edge_w", lambda a: a),
    "edge_b": ("L3_gnn_edge_b", lambda a: a.reshape(1, D)),
    "attrT": ("edge_attr_32", lambda a: a.reshape(EDGE_TILES, P, 32).transpose(0, 2, 1)),
}


def kernel(**inputs):
    import numpy as _np
    import concourse.bacc as _bacc
    from concourse import mybir as _mybir
    from concourse.bass_utils import run_bass_kernel_spmd as _run

    nc = _bacc.Bacc("TRN2", target_bir_lowering=False, num_devices=1)
    c = Core()
    arrays = {}
    for name, (arg, lay) in _INS.items():
        a = _np.ascontiguousarray(lay(_np.asarray(inputs[arg])))
        arrays[f"in_{name}"] = a
        c.__dict__[name] = nc.dram_tensor(f"in_{name}", a.shape, _mybir.dt.from_np(a.dtype), kind="ExternalInput").ap()
    c.out = nc.dram_tensor("out_x", (N, D), F32, kind="ExternalOutput").ap()
    program(nc, c)
    r = _run(nc, [arrays], core_ids=[0])
    return r.results[0]["out_x"]
```

```python
from contextlib import ExitStack

import concourse.bass as bass
from concourse import mybir

F32 = mybir.dt.float32
BF16 = mybir.dt.bfloat16
I32 = mybir.dt.int32
I16 = mybir.dt.int16
ALU = mybir.AluOpType
ACT = mybir.ActivationFunctionType
AX = mybir.AxisListType.X

N, E, D = 3125, 53125, 256
P = 125
NODE_TILES = N // P
EDGE_TILES = E // P
RING = 10
SLOTS = -(-(EDGE_TILES + NODE_TILES - 1) // RING) * RING
ROUNDS = SLOTS // RING
GROUP = 2
BUFS = RING // 2
AHEAD = 2
WIN, WINS = 50, -(-N // 50)
ROW16 = 16
NEAR = 8
IOTA = max(128, 3 * WIN)
WSLOTS = -(-(EDGE_TILES + WINS - 1) // RING) * RING
JC, JP = 5, EDGE_TILES // 5
KC = D // 128
HEADS, DK = 4, 64
NTYPES, RELS, REL3 = 4, 8, 3
ATTRS = 32
EXTRA = 8
SCAN_C = 25
SCAN_S = SLOTS // SCAN_C
SLOT_C, SLOT_P = 5, SLOTS // 5
BIG = 1e30
LN_EPS = 1e-5


def ds(i, n):
    return bass.ds(i, n)


class Chain:

    def __init__(self, eng, sem):
        self.eng, self.sem, self.base, self.n = eng, sem, 0, 0

    def at(self, base):
        self.base, self.n = base, 0

    def __call__(self, ins):
        self.n += 1
        ins.then_inc(self.sem, 1)
        self.eng.wait_ge(self.sem, self.base + self.n)


def known(t, at_least):
    return not isinstance(t, int) or t >= at_least


def by_tiles(eng, body):
    for t in range(3):
        body(t, t % 2, t // 2)
    with eng.Fori(1, NODE_TILES // 2) as k:
        body(2 * k + 1, 1, k)
        body(2 * k + 2, 0, k + 1)


def in_steps(eng, *steps):
    most = max(lag for lag, _ in steps)
    first = most + 2 + (NODE_TILES - most) % 2

    def turn(t):
        for lag, step in steps:
            if 0 <= t - lag < NODE_TILES:
                step(t - lag, (t - lag) % 2, (t - lag) // 2)
    for t in range(first):
        turn(t)
    with eng.Fori(0, (NODE_TILES - first) // 2) as k:
        for half in range(2):
            for lag, step in steps:
                at = first + half - lag
                step(2 * k + at, at % 2, k + at // 2)
    for t in range(NODE_TILES, NODE_TILES + most):
        turn(t)


def by_slots(eng, body, slots=SLOTS):
    body(0, 0)
    with eng.Fori(1, slots // RING - 1) as i:
        body(i * RING, i)
    body(slots - RING, slots // RING - 1)


def before_end(s, r, ahead, slots=SLOTS):
    return not isinstance(s, int) or s + r + ahead < slots


def col(table, s, n=1):
    return table[:, s:s + n] if isinstance(s, int) else table[:, ds(s, n)]


def tile_at(t, n=1):
    return slice(t, t + n) if isinstance(t, int) else ds(t, n)


def flat(ap):
    return ap.rearrange("p a d -> p (a d)")


class Rows:

    def __init__(self, eng, name, table, limit):
        self.eng, self.table, self.limit = eng, table, limit
        self.regs = [eng.alloc_register(f"{name}{r}") for r in range(RING)]
        self.values = [None] * RING

    def load(self, i, lo, hi):
        at = self.table[0:1, i:i + 1, lo:hi] if isinstance(i, int) else self.table[0:1, ds(i, 1), lo:hi]
        self.eng.load(self.regs[lo:hi], at)
        for r in range(lo, hi):
            self.values[r] = self.eng.snap(self.regs[r], min_val=0, max_val=self.limit)

    def at(self, i, r):
        if r in (0, NEAR):
            self.load(i, r, NEAR if r == 0 else RING)
        return self.values[r]

    def free(self):
        for reg in self.regs:
            self.eng.free_register(reg)


class Core:
    pass


def constants(nc, c):
    with nc.sbuf_tensor("iota_i", [128, IOTA], I32) as iota_i, nc.sbuf_tensor("part_i", [128, 1], I32) as part_i:
        made, dve = c.sem("iota_made"), c.sem("const_chain")
        with nc.Block() as block:
            @block.gpsimd
            def _(pool):
                pool.iota(iota_i[:, :], [[1, IOTA]], base=0, channel_multiplier=0).then_inc(made, 1)
                pool.iota(part_i[:, :], [[0, 1]], base=0, channel_multiplier=1).then_inc(made, 1)

            @block.vector
            def _(v):
                do = Chain(v, dve)
                do(v.memset(c.ones[:, :], 1.0))
                v.wait_ge(made, 2)
                do(v.tensor_copy(c.iota[:, :], iota_i[:, :]))
                do(v.tensor_copy(c.part[:, :], part_i[:, :]))
                do(v.tensor_scalar(c.ident[:, :], c.iota[:, 0:128], c.part[:, :], None, ALU.is_equal))
                do(v.tensor_copy(c.ident16[:, :], c.ident[:, :]))
                do(v.tensor_scalar(c.below[:, :], c.iota[:, 0:128], c.part[:, :], None, ALU.is_gt))


def slot_tables(nc, c):
    with ExitStack() as ctx:
        def sb(name, shape, dt=F32):
            return ctx.enter_context(nc.sbuf_tensor(name, shape, dt))
        names = ["dst", "src", "t3", "t8"]
        raw = {n: sb("raw_" + n, [JP, JC, P], I32) for n in names + ["before", "after"]}
        flt = {n: sb("flt_" + n, [JP, JC, P]) for n in names + ["before", "after"]}
        tmp = sb("clipped", [1, WSLOTS])
        border_i, border = sb("border_i", [JP, WINS], I32), sb("border", [JP, WINS])
        past = sb("past", [JP, JC, WINS])
        key = sb("key", [WINS, 1])
        slot_i, slot = sb("slot_i", [128, WSLOTS], I32), sb("slot", [128, WSLOTS])
        passed = sb("passed", [WINS, WSLOTS])
        tile = sb("tile", [128, WSLOTS])
        edge_tile = sb("edge_tile", [128, WSLOTS])
        row_i = sb("row_i", [128, JC], I32)
        row_f = sb("row_f", [128, JC])
        pick = sb("pick", [JP, JC, WSLOTS])
        dst_s, val = sb("dst_s", [P, WSLOTS]), sb("val_s", [P, WSLOTS])
        load, pool_done, dve = c.sem("edge_loads"), c.sem("slot_iotas"), c.sem("slot_chain")
        blank, ask, mm_done, picked = (c.sem(n) for n in ("neighbours_blank", "table_asked", "table_mm", "picked"))
        kinds = [(P, NODE_TILES, SLOTS, ["dst", "src", "t3", "t8", "before", "after"]),
                 (WIN, WINS, WSLOTS, ["dst", "src", "t3"])]

        def edges(a):
            return a.rearrange("(c p e) -> p c e", c=JC, p=JP)

        with nc.Block() as block:
            @block.sync
            def _(sp):
                for n, a in (("dst", c.dst), ("src", c.src), ("t3", c.t3), ("t8", c.t8)):
                    sp.dma_start(raw[n][:, :, :], edges(a)).then_inc(load, 16)
                sp.wait_ge(blank, 2)
                flat = c.dst.rearrange("(a e) -> a e", a=1)
                b, a = raw["before"], raw["after"]
                sp.dma_start(b[0:1, 0, 1:P], flat[:, 0:P - 1]).then_inc(load, 16)
                sp.dma_start(a[JP - 1:JP, JC - 1, 0:P - 1], flat[:, E - P + 1:E]).then_inc(load, 16)
                for k in range(JC):
                    e0 = k * JP * P
                    r0 = 1 if k == 0 else 0
                    sp.dma_start(b[r0:JP, k, :], c.dst[e0 + r0 * P - 1:e0 + JP * P - 1]
                                 .rearrange("(p e) -> p e", e=P)).then_inc(load, 16)
                    r1 = JP - 1 if k == JC - 1 else JP
                    sp.dma_start(a[0:r1, k, :], c.dst[e0 + 1:e0 + r1 * P + 1]
                                 .rearrange("(p e) -> p e", e=P)).then_inc(load, 16)

            @block.gpsimd
            def _(pool):
                pool.iota(slot_i[:, :], [[1, WSLOTS]], base=0, channel_multiplier=0).then_inc(pool_done, 1)
                pool.iota(row_i[:, :], [[JP, JC]], base=0, channel_multiplier=1).then_inc(pool_done, 1)
                pool.iota(border_i[:, :], [[1, WINS]], base=0, channel_multiplier=0).then_inc(pool_done, 1)

            @block.vector
            def _(v):
                do = Chain(v, dve)
                v.memset(raw["before"][:, :, :], -1).then_inc(blank, 1)
                v.memset(raw["after"][:, :, :], -1).then_inc(blank, 1)
                v.wait_ge(pool_done, 3)
                do(v.tensor_copy(slot[:, :], slot_i[:, :]))
                do(v.tensor_copy(row_f[:, :], row_i[:, :]))
                v.wait_ge(load, 16 * (6 + 2 * JC))
                for n in raw:
                    do(v.tensor_copy(flt[n][:, :, :], raw[n][:, :, :]))
                for n in ("before", "after"):
                    do(v.tensor_tensor(flt[n][:, :, :], flt["dst"][:, :, :], flt[n][:, :, :], ALU.is_equal))
                    do(v.tensor_scalar(flt[n][:, :, :], flt[n][:, :, :], -1.0, 1.0, ALU.mult, ALU.add))
                n_picked = 0
                for turn, (width, tiles, slots, tables) in enumerate(kinds):
                    do(v.tensor_scalar(border[:, 0:tiles], border_i[:, 0:tiles], float(width), None, ALU.mult))
                    do(v.tensor_tensor(past[:, :, 0:tiles], flt["dst"][:, :, P - 1:P].to_broadcast([JP, JC, tiles]),
                                       border[:, 0:tiles].unsqueeze(1).to_broadcast([JP, JC, tiles]), ALU.is_lt))
                    v.sem_inc(ask, 1)
                    v.wait_ge(mm_done, 2 * turn + 1)
                    do(v.scalar_tensor_tensor(out=key[0:tiles, :], in0=c.ps[6][0:tiles, 0:1], scalar=float(EDGE_TILES - 1),
                                              in1=c.part[0:tiles, :], op0=ALU.min, op1=ALU.add))
                    do(v.tensor_scalar(passed[0:tiles, 0:slots], slot[0:tiles, 0:slots], key[0:tiles, :], None, ALU.is_ge))
                    v.sem_inc(ask, 1)
                    v.wait_ge(mm_done, 2 * turn + 2)
                    do(v.tensor_scalar(tile[:, 0:slots], c.ps[7][:, 0:slots], -1.0, None, ALU.add))
                    do(v.tensor_tensor(edge_tile[:, 0:slots], slot[:, 0:slots], tile[:, 0:slots], ALU.subtract))
                    for k in range(JC):
                        do(v.tensor_scalar(pick[:, k, 0:slots], edge_tile[0:JP, 0:slots], row_f[0:JP, k:k + 1], None,
                                           ALU.is_equal))
                    v.sem_inc(ask, 1)
                    tile_row = (c.tile_row, c.win_row)[turn]
                    step = 1.0 if turn == 0 else float(WIN)
                    by_round = [t[0:1, 0:slots].rearrange("a (i r) -> a i r", r=RING) for t in (tile, edge_tile)]
                    do(v.tensor_scalar(tile_row[0:1, :, 0:RING], by_round[0], step, None, ALU.mult))
                    if turn == 1:
                        do(v.tensor_scalar(c.win_edge_row[0:1, :, 0:RING], by_round[1], float(EDGE_TILES - 1), None, ALU.min))

                    def taken(name):
                        v.wait_ge(picked, n_picked + tables.index(name) + 1)
                        return c.ps[tables.index(name)][0:P, 0:slots]
                    t_of = tile[0:P, 0:slots]
                    if turn == 0:
                        do(v.tensor_copy(dst_s[:, 0:slots], taken("dst")))
                        do(v.scalar_tensor_tensor(out=c.dloc[:, :], in0=t_of, scalar=-float(P), in1=dst_s[:, 0:slots],
                                                  op0=ALU.mult, op1=ALU.add))
                        do(v.tensor_copy(val[:, 0:slots], taken("src")))
                        do(v.tensor_copy(c.src_idx[:, :], val[:, 0:slots]))
                        do(v.scalar_tensor_tensor(out=val[:, 0:slots], in0=taken("t8"), scalar=float(N),
                                                  in1=val[:, 0:slots], op0=ALU.mult, op1=ALU.add))
                        do(v.tensor_copy(c.kv_idx[:, :], val[:, 0:slots]))
                        do(v.tensor_copy(val[:, 0:slots], taken("t3")))
                        for r in range(REL3):
                            do(v.tensor_scalar(c.edge_cols[:, :, HEADS + 1 + r], val[:, 0:slots], float(r), None,
                                               ALU.is_equal))
                        do(v.memset(c.edge_cols[:, :, HEADS], 1.0))
                        do(v.tensor_scalar(c.valid[:, :], c.dloc[:, :], float(P - 1), None, ALU.is_le))
                        do(v.scalar_tensor_tensor(out=c.valid[:, :], in0=c.dloc[:, :], scalar=0.0, in1=c.valid[:, :],
                                                  op0=ALU.is_ge, op1=ALU.mult))
                        for n, flag in (("before", c.starts), ("after", c.ends)):
                            do(v.tensor_tensor(flag[:, :], taken(n), c.valid[:, :], ALU.mult))
                            do(v.tensor_scalar(flag[:, :], flag[:, :], -BIG, None, ALU.mult))
                    else:
                        do(v.tensor_copy(dst_s[:, :], taken("dst")))
                        do(v.scalar_tensor_tensor(out=dst_s[:, :], in0=t_of, scalar=-float(WIN), in1=dst_s[:, :],
                                                  op0=ALU.mult, op1=ALU.add))
                        do(v.tensor_scalar(val[:, :], dst_s[:, :], float(WIN - 1), None, ALU.is_le))
                        do(v.scalar_tensor_tensor(out=val[:, :], in0=dst_s[:, :], scalar=0.0, in1=val[:, :],
                                                  op0=ALU.is_ge, op1=ALU.mult))
                        do(v.scalar_tensor_tensor(out=dst_s[:, :], in0=taken("t3"), scalar=float(WIN), in1=dst_s[:, :],
                                                  op0=ALU.mult, op1=ALU.add))
                        do(v.scalar_tensor_tensor(out=dst_s[:, :], in0=dst_s[:, :], scalar=1.0, in1=val[:, :],
                                                  op0=ALU.add, op1=ALU.mult))
                        do(v.tensor_scalar(c.win_key[:, :], dst_s[:, :], -1.0, None, ALU.add))
                        do(v.tensor_copy(c.win_src[:, :], taken("src")))
                    n_picked += len(tables)
                    v.sem_inc(ask, 1)

            @block.tensor
            def _(pe):
                for turn, (width, tiles, slots, tables) in enumerate(kinds):
                    pe.wait_ge(ask, 4 * turn + 1)
                    for k in range(JC):
                        mm = pe.matmul(c.ps[6][0:tiles, 0:1], past[:, k, 0:tiles], c.ones[0:JP, 0:1], start=(k == 0),
                                       stop=(k == JC - 1))
                    mm.then_inc(mm_done, 1)
                    pe.wait_ge(ask, 4 * turn + 2)
                    pe.matmul(c.ps[7][:, 0:slots], c.ones[0:tiles, :], passed[0:tiles, 0:slots], start=True,
                              stop=True).then_inc(mm_done, 1)
                    pe.wait_ge(ask, 4 * turn + 3)
                    for n, name in enumerate(tables):
                        for k in range(JC):
                            mm = pe.matmul(c.ps[n][0:P, 0:slots], flt[name][:, k, :], pick[:, k, 0:slots],
                                           start=(k == 0), stop=(k == JC - 1))
                        mm.then_inc(picked, 1)


def project(nc, c):
    G = EDGE_TILES // NODE_TILES
    with ExitStack() as ctx:
        def sb(name, shape, dt=F32):
            return ctx.enter_context(nc.sbuf_tensor(name, shape, dt))
        w = {n: sb("w_" + n, [128, NTYPES, KC, D]) for n in "qkv"}
        rel = {n: sb("rel_" + n, [128, RELS, KC, 128]) for n in ("att", "msg")}
        pri = sb("pri", [128, RELS, HEADS])
        xt = sb("xt", [128, 2, KC, P])
        src_i, lo, hi = sb("src_i", [P, EDGE_TILES], I32), sb("src_lo", [P, EDGE_TILES]), sb("src_hi", [P, EDGE_TILES])
        lo16, hi16 = sb("src_lo16", [P, EDGE_TILES], BF16), sb("src_hi16", [P, EDGE_TILES], BF16)
        iota16 = sb("iota16", [P, P], BF16)
        hot_lo, hot_hi = sb("hot_lo", [P, 2, G, P], BF16), sb("hot_hi", [P, 2, G, NODE_TILES], BF16)
        xm = sb("xm", [128, 2, NTYPES, KC, P])
        kvt = sb("kvt", [128, 2, 2, KC, P])
        stage = sb("stage", [P, 2, RELS, 2 * D])
        load, cleared, dve, xm_ready, proj, proj_out, rel_mm, rel_act, rel_dve, rel_w = (
            c.sem(n) for n in ("proj_loads", "rel_cleared", "proj_chain", "masked_x", "projected", "proj_copied",
                               "related", "related_by_act", "related_by_dve", "rel_weights"))
        src_load, w_load, rel_load, hist, hot_ready, counted, act_s = (
            c.sem(n) for n in ("src_load", "weight_loads", "rel_loads", "hist_chain", "hist_hot", "hist_counted",
                               "hist_sqrt"))
        xt_in = [c.sem("xt_in0"), c.sem("xt_in1")]
        stored = [c.sem("kv_stored0"), c.sem("kv_stored1")]

        with nc.Block() as block:
            @block.sync
            def _(sp):
                sp.dma_start(src_i[:, :], c.src.rearrange("(p k) -> p k", p=P)).then_inc(src_load, 16)
                sp.dma_start(c.type_row[:, :], c.node_type.partition_broadcast(128)).then_inc(load, 16)
                sp.dma_start(pri[:, :, :], c.pri.partition_broadcast(128)).then_inc(load, 16)

                def fetch(t, b, uses):
                    if known(t, 2):
                        sp.wait_ge(xm_ready, t - 1)
                    at = slice(t * P, (t + 1) * P) if isinstance(t, int) else ds(t * P, P)
                    sp.dma_start(xt[:, b], c.xT.rearrange("(c p) n -> p c n", p=128)[:, :, at]).then_inc(xt_in[b], 16)
                    if isinstance(t, int) and t == 0:
                        weights()

                def weights():
                    for n, a in (("q", c.wq), ("k", c.wk), ("v", c.wv)):
                        sp.dma_start(w[n][:, :, :, :], a.rearrange("t (c p) o -> p t c o", p=128)).then_inc(w_load, 16)
                    relation_weights()

                def relation_weights():
                    sp.wait_ge(cleared, 2)
                    for n, a in (("att", c.attT), ("msg", c.msg)):
                        for h in range(HEADS):
                            lo = h % 2 * DK
                            sp.dma_start(rel[n][lo:lo + DK, :, h // 2, lo:lo + DK],
                                         a[:, h].rearrange("r e d -> e r d")).then_inc(rel_load, 16)

                def store(t, b, uses):
                    sp.wait_ge(rel_act, 4 * t + 4)
                    sp.wait_ge(rel_dve, 4 * t + 4)
                    for k, table in enumerate((c.key_table, c.msg_table)):
                        to = table.rearrange("(r n) d -> n r d", r=RELS)
                        to = to[t * P:(t + 1) * P] if isinstance(t, int) else to[ds(t * P, P)]
                        sp.dma_start(to, stage[:, b, :, k * D:(k + 1) * D]).then_inc(stored[b], 16)
                in_steps(sp, (0, fetch), (3, store))
                sp.wait_ge(stored[0], 32 * 13)
                sp.wait_ge(stored[1], 32 * 12)

            @block.vector
            def _(v):
                do = Chain(v, dve)
                for n in rel:
                    v.memset(rel[n][:, :, :, :], 0.0).then_inc(cleared, 1)
                count = Chain(v, hist)
                v.wait_ge(src_load, 16)
                count(v.tensor_copy(lo[:, :], src_i[:, :]))
                count(v.memset(hi[:, :], 0.0))
                for t in range(1, NODE_TILES):
                    count(v.scalar_tensor_tensor(out=hi[:, :], in0=lo[:, :], scalar=float(P * t), in1=hi[:, :],
                                                 op0=ALU.is_ge, op1=ALU.add))
                count(v.scalar_tensor_tensor(out=lo[:, :], in0=hi[:, :], scalar=-float(P), in1=lo[:, :],
                                             op0=ALU.mult, op1=ALU.add))
                count(v.tensor_copy(lo16[:, :], lo[:, :]))
                count(v.tensor_copy(hi16[:, :], hi[:, :]))
                count(v.tensor_copy(iota16[:, :], c.iota[0:P, 0:P]))
                v.wait_ge(load, 32)

                def scale_relations():
                    v.wait_ge(rel_load, 16 * 2 * HEADS)
                    do(v.tensor_scalar(pri[:, :, :], pri[:, :, :], DK ** -0.5, None, ALU.mult))
                    for h in range(HEADS):
                        at = h % 2 * DK
                        blk = rel["att"][:, :, h // 2, at:at + DK]
                        do(v.tensor_tensor(blk, blk, pri[:, :, h:h + 1].to_broadcast([128, RELS, DK]), ALU.mult))
                    v.sem_inc(rel_w, 1)

                def one_hots(t, b, uses):
                    if known(t, 2):
                        v.wait_ge(counted, t - 1)
                    at = slice(t * G, (t + 1) * G) if isinstance(t, int) else ds(t * G, G)
                    for hot, digit, n in ((hot_lo, lo16, P), (hot_hi, hi16, NODE_TILES)):
                        v.tensor_tensor(hot[:, b], iota16[:, 0:n].unsqueeze(1).to_broadcast([P, G, n]),
                                        digit[:, at].unsqueeze(2).to_broadcast([P, G, n]),
                                        ALU.is_equal).then_inc(hot_ready, 1)
                    if isinstance(t, int) and t == 0:
                        scale_relations()

                def mask(t, b, uses):
                    if known(t, 2):
                        v.wait_ge(proj, t - 1)
                    v.wait_ge(xt_in[b], 16 * (uses + 1))
                    for y in range(NTYPES):
                        at = slice(t * P, (t + 1) * P) if isinstance(t, int) else ds(t * P, P)
                        m = v.scalar_tensor_tensor(
                            out=xm[:, b, y], in0=c.type_row[:, at].unsqueeze(1).to_broadcast([128, KC, P]),
                            scalar=float(y), in1=xt[:, b], op0=ALU.is_equal, op1=ALU.mult)
                    m.then_inc(xm_ready, 1)

                def take(t, b, uses):
                    for r in range(1, RELS, 2):
                        v.wait_ge(rel_mm, RELS * t + r + 1)
                        if r == 1 and known(t, 2):
                            v.wait_ge(stored[b], 32 * uses)
                        v.tensor_copy(stage[:, b, r, :], c.ps[3 + r % 4][0:P, :]).then_inc(rel_dve, 1)
                in_steps(v, (0, mask), (0, one_hots), (2, take))
                v.wait_ge(counted, NODE_TILES)
                count(v.tensor_scalar(c.rout[:, :], c.ps[7][0:P, 0:NODE_TILES], 1.0, None, ALU.max))
                v.wait_ge(act_s, 1)
                count(v.reciprocal(c.rout[:, :], c.rout[:, :]))

            @block.scalar
            def _(a):
                def projected(t, b, uses):
                    a.wait_ge(proj, t + 1)
                    tile = slice(t, t + 1) if isinstance(t, int) else ds(t, 1)
                    a.copy(c.nodes_b[:, tile, :], c.ps[0][0:P, 0:D].unsqueeze(1)).then_inc(proj_out, 1)
                    if known(t, 2):
                        a.wait_ge(rel_mm, RELS * (t - 1))
                    for k in range(2):
                        a.copy(kvt[:, b, k], c.ps[1 + k][:, 0:KC * P].rearrange("p (c n) -> p c n", c=KC))\
                            .then_inc(proj_out, 1)

                def take(t, b, uses):
                    for r in range(0, RELS, 2):
                        a.wait_ge(rel_mm, RELS * t + r + 1)
                        if r == 0 and known(t, 2):
                            a.wait_ge(stored[b], 32 * uses)
                        a.copy(stage[:, b, r, :], c.ps[3 + r % 4][0:P, :]).then_inc(rel_act, 1)
                in_steps(a, (0, projected), (1, take))
                a.wait_ge(hist, NODE_TILES + 6)
                a.activation(c.rout[:, :], c.rout[:, :], ACT.Sqrt).then_inc(act_s, 1)

            @block.tensor
            def _(pe):
                def project_tile(t, b, uses):
                    pe.wait_ge(xm_ready, t + 1)
                    if known(t, 1):
                        pe.wait_ge(proj_out, 3 * t)
                    steps = [(y, k) for y in range(NTYPES) for k in range(KC)]
                    for i, (y, k) in enumerate(steps):
                        pe.matmul(c.ps[0][0:P, 0:D], xm[:, b, y, k, :], w["q"][:, y, k, :], start=(i == 0),
                                  stop=(i == len(steps) - 1))
                    for n, name in enumerate("kv"):
                        for o in range(KC):
                            for i, (y, k) in enumerate(steps):
                                mm = pe.matmul(c.ps[1 + n][:, o * P:(o + 1) * P],
                                               w[name][:, y, k, o * 128:(o + 1) * 128], xm[:, b, y, k, :],
                                               start=(i == 0), stop=(i == len(steps) - 1))
                    mm.then_inc(proj, 1)

                def relate(t, b, uses):
                    pe.wait_ge(proj_out, 3 * t + 3)
                    if isinstance(t, int) and t == 0:
                        pe.wait_ge(rel_w, 1)
                    for r in range(RELS):
                        if known(t, 1) or r >= 4:
                            pe.wait_ge((rel_act, rel_dve)[r % 2], 4 * t + r // 2 - 1)
                        for n, name in enumerate(("att", "msg")):
                            for o in range(KC):
                                mm = pe.matmul(c.ps[3 + r % 4][0:P, n * D + o * 128:n * D + (o + 1) * 128],
                                               kvt[:, b, n, o, :], rel[name][:, r, o, :], start=True, stop=True)
                        mm.then_inc(rel_mm, 1)

                def count(t, b, uses):
                    pe.wait_ge(hot_ready, 2 * t + 2)
                    for k in range(G):
                        mm = pe.matmul(c.ps[7][0:P, 0:NODE_TILES], hot_lo[:, b, k, :], hot_hi[:, b, k, :],
                                       start=(isinstance(t, int) and t == 0 and k == 0), stop=True,
                                       skip_group_check=True)
                    mm.then_inc(counted, 1)
                pe.wait_ge(w_load, 48)
                in_steps(pe, (0, project_tile), (1, count), (1, relate))


def gather_rows(pool, rows, ring, ring_used, copied, table, filled, let_go, slots=SLOTS):
    def body(s, i):
        for r in range(RING):
            if r % GROUP == 0:
                pool.wait_ge(copied, RING // GROUP * i + r // GROUP + 1)
                pool.sem_inc(let_go, 1)
            if known(s, 1):
                pool.wait_ge(ring_used, s + r - RING + 1)
                pool.sem_inc(let_go, 1)
            pool.indirect_dma_start(ring[:, r, :], None, table,
                                    bass.IndirectOffsetOnAxis(rows[:, r:r + 1], 0)).then_inc(filled[r], 16)
    by_slots(pool, body, slots)


def copy_rows(a, s, i, r, table, rows, filled, copied):
    if known(s, 1):
        for k in range(GROUP):
            a.wait_ge(filled[r + k], 16 * i)
    a.copy(rows[:, r:r + GROUP], col(table, s + r, GROUP)).then_inc(copied, 1)


def copy_first_rows(a, table, rows, filled, copied):
    for r in range(0, RING, GROUP):
        copy_rows(a, 0, 0, r, table, rows, filled, copied)


def copy_next_rows(a, s, i, r, table, rows, filled, copied, slots=SLOTS):
    if r % GROUP == GROUP - 1 and before_end(s, r, RING, slots):
        copy_rows(a, s + RING, i + 1, r - GROUP + 1, table, rows, filled, copied)


def copy_all_rows(a, table, rows, filled, copied, slots=SLOTS):
    def body(s, i):
        for r in range(0, RING, GROUP):
            copy_rows(a, s, i, r, table, rows, filled, copied)
    by_slots(a, body, slots)


def one_hot(v, c, hot, s, r, hot_ready, key=None, columns=P, ahead=0):
    v.tensor_scalar(hot[:, (r + ahead) % RING, :], c.iota[0:P, 0:columns],
                    col(c.dloc if key is None else key, s + r + ahead), None, ALU.is_equal).then_inc(hot_ready, 1)


def attention_scores(nc, c):
    with ExitStack() as ctx:
        def sb(name, shape, dt=F32):
            return ctx.enter_context(nc.sbuf_tensor(name, shape, dt))
        keys = sb("keys", [P, RING, D])
        rows = sb("rows_a", [P, RING], I32)
        hot = sb("hot16", [P, RING, P], BF16)
        hot_t = sb("hot_t", [P, 2, P])
        prod = sb("prod", [P, BUFS, D])
        filled = [c.sem(f"keys_in{r}") for r in range(RING)]
        copied, let_go, hot_ready, turned, hot_t_ready, q_ready, prod_done, scored = (
            c.sem(n) for n in ("rows_copied_a", "pool_seen_a", "hot_ready_a", "turned_a", "hot_t_ready", "q_ready",
                               "prod_done", "scored"))
        with nc.Block() as block:
            @block.gpsimd
            def _(pool):
                gather_rows(pool, rows, keys, prod_done, copied, c.key_table, filled, let_go)

            @block.scalar
            def _(a):
                def body(s, i):
                    for r in range(RING):
                        if r % GROUP == 0:
                            copy_rows(a, s, i, r, c.kv_idx, rows, filled, copied)
                        a.wait_ge(turned, s + r + 1)
                        if known(s, 1) or r >= 2:
                            a.wait_ge(q_ready, s + r - 1)
                        a.copy(hot_t[:, r % 2, :], c.ps[r % 2][:, :].bitcast(BF16)[0:P, 0:P]).then_inc(hot_t_ready, 1)
                by_slots(a, body)

            @block.tensor
            def _(pe):
                tiles = Rows(pe, "q_tile", c.tile_row, NODE_TILES - 1)

                def turn(s, r, ahead=0):
                    n = r + ahead
                    pe.wait_ge(hot_ready, s + n + 1)
                    if known(s, 1) or n >= 2:
                        pe.wait_ge(hot_t_ready, s + n - 1)
                    pe.transpose(c.ps[n % 2][:, :].bitcast(BF16)[0:P, 0:P], hot[:, n % RING, :],
                                 c.ident16[0:P, 0:P]).then_inc(turned, 1)

                def body(s, i):
                    for r in range(RING):
                        t = tiles.at(i, r)
                        pe.wait_ge(hot_t_ready, s + r + 1)
                        if known(s, 1) or r >= BUFS:
                            pe.wait_ge(prod_done, s + r - BUFS + 1)
                        pe.matmul(c.ps[2 + r % BUFS][0:P, 0:D], hot_t[:, r % 2, :],
                                  c.nodes_b[:, ds(t, 1), :].rearrange("p a d -> p (a d)"), start=True,
                                  stop=True).then_inc(q_ready, 1)
                        if before_end(s, r, AHEAD):
                            turn(s, r, AHEAD)
                for r in range(AHEAD):
                    turn(0, r)
                by_slots(pe, body)
                tiles.free()

            @block.vector
            def _(v):
                def score(s, r):
                    v.wait_ge(prod_done, s + r + 1)
                    to = c.score[:, s + r, :] if isinstance(s, int) else \
                        c.score[:, ds(s + r, 1), :].rearrange("p a h -> p (a h)")
                    v.tensor_reduce(to, prod[:, r % BUFS, :].rearrange("p (h d) -> p h d", h=HEADS), AX,
                                    ALU.add).then_inc(scored, 1)

                def body(s, i):
                    for r in range(RING):
                        v.wait_ge(q_ready, s + r + 1)
                        v.wait_ge(filled[r], 16 * (i + 1))
                        if known(s, 1) or r >= BUFS:
                            v.wait_ge(scored, s + r - BUFS + 1)
                        v.tensor_tensor(prod[:, r % BUFS, :], keys[:, r, :], c.ps[2 + r % BUFS][0:P, 0:D],
                                        ALU.mult).then_inc(prod_done, 1)
                        if before_end(s, r, RING):
                            one_hot(v, c, hot, s, r, hot_ready, ahead=RING)
                        score(s, r)
                for r in range(RING):
                    one_hot(v, c, hot, 0, r, hot_ready)
                by_slots(v, body)


def segment_softmax(nc, c):
    with ExitStack() as ctx:
        def sb(name, shape, dt=F32):
            return ctx.enter_context(nc.sbuf_tensor(name, shape, dt))
        CH = HEADS * SCAN_C
        L = SCAN_S * P
        turned = sb("turned", [SLOT_P, HEADS + 2, SLOT_C, P])
        seq, fwd, bwd = sb("seq", [CH, L]), sb("fwd", [CH, L]), sb("bwd", [CH, L])
        reset = {n: sb("reset_" + n, [CH, L]) for n in ("start", "end")}
        ends2 = sb("ends2", [CH, 2])
        row = sb("row", [1, 2, CH])
        carry_row = sb("carry_row", [1, CH + 2])
        carry = sb("carry", [CH, 1])
        dve, pe_s, mm_done, out_t, dma_o, dma_i, ready = (
            c.sem(n) for n in ("softmax_chain", "softmax_turned", "softmax_mm", "seq_copied", "seq_stored",
                               "seq_loaded", "seq_ready"))
        n_turn = (HEADS + 2) * SLOT_C

        with nc.Block() as block:
            @block.vector
            def _(v):
                do = Chain(v, dve)
                valid = c.valid[:, :].unsqueeze(2).to_broadcast([P, SLOTS, HEADS])
                do(v.tensor_tensor(c.score[:, :, :], c.score[:, :, :], valid, ALU.mult))
                do(v.tensor_scalar(c.valid[:, :], c.valid[:, :], BIG, -BIG, ALU.mult, ALU.add))
                do(v.tensor_tensor(c.score[:, :, :], c.score[:, :, :], valid, ALU.add))
                v.sem_inc(ready, 1)
                for n in range(n_turn):
                    v.wait_ge(pe_s, n + 1)
                    v.tensor_copy(turned[:, n // SLOT_C, n % SLOT_C, :],
                                  c.ps[n % 8][0:SLOT_P, 0:P]).then_inc(out_t, 1)

                def scan(src, out, flags, step, at_last):
                    view = (lambda a: a[:, ::step])
                    do(v.tensor_tensor_scan(view(out), view(flags), view(src), -BIG, ALU.add, ALU.max))
                    do(v.tensor_copy(ends2[:, 0:1], out[:, at_last:at_last + 1]))
                    do(v.tensor_reduce(ends2[:, 1:2], flags[:, :], AX, ALU.min))
                    v.sem_inc(ready, 1)
                    turn = 0 if step == 1 else 1
                    v.wait_ge(mm_done, 3 * turn + 2)
                    for k in range(2):
                        do(v.tensor_copy(row[0:1, k, :], c.ps[k][0:1, 0:CH]))
                    do(v.memset(carry_row[0:1, :], -BIG))
                    mid = carry_row[0:1, 1:CH + 1]
                    do(v.tensor_tensor_scan(mid[:, ::step], row[0:1, 1, ::step], row[0:1, 0, ::step], -BIG,
                                            ALU.add, ALU.max))
                    v.sem_inc(ready, 1)
                    v.wait_ge(mm_done, 3 * turn + 3)
                    do(v.tensor_copy(carry[:, :], c.ps[2][0:CH, 0:1]))
                    do(v.tensor_tensor_scan(view(out), view(flags), view(src), carry[:, :], ALU.add, ALU.max))
                v.wait_ge(dma_i, 16 * (1 + 2 * HEADS))
                scan(seq, fwd, reset["start"], 1, L - 1)
                scan(fwd, bwd, reset["end"], -1, 0)
                v.sem_inc(ready, 1)
                for n in range(HEADS * SLOT_C):
                    h, k = n // SLOT_C, n % SLOT_C
                    v.wait_ge(pe_s, n_turn + n + 1)
                    at = c.score[:, k * SLOT_P:(k + 1) * SLOT_P, h]
                    v.tensor_tensor(at, at, c.ps[n % 8][0:P, 0:SLOT_P], ALU.subtract).then_inc(out_t, 1)

            @block.tensor
            def _(pe):
                pe.wait_ge(ready, 1)
                for n in range(n_turn):
                    a, k = n // SLOT_C, n % SLOT_C
                    if n >= 8:
                        pe.wait_ge(out_t, n - 7)
                    src = c.score[:, k * SLOT_P:(k + 1) * SLOT_P, a] if a < HEADS else \
                        (c.starts, c.ends)[a - HEADS][:, k * SLOT_P:(k + 1) * SLOT_P]
                    pe.transpose(c.ps[n % 8][0:SLOT_P, 0:P], src, c.ident[0:P, 0:P]).then_inc(pe_s, 1)
                pe.wait_ge(out_t, n_turn)
                for turn in range(2):
                    step = 1 if turn == 0 else -1
                    pe.wait_ge(ready, 2 + 2 * turn)
                    for k in range(2):
                        pe.transpose(c.ps[k][0:1, 0:CH], ends2[:, k:k + 1], c.ident[0:CH, 0:CH]).then_inc(mm_done, 1)
                    pe.wait_ge(ready, 3 + 2 * turn)
                    at = 1 - step
                    pe.transpose(c.ps[2][0:CH, 0:1], carry_row[0:1, at:at + CH],
                                 c.ident[0:1, 0:1]).then_inc(mm_done, 1)
                pe.wait_ge(ready, 6)
                pe.wait_ge(dma_i, 16 * (1 + 2 * HEADS + 1))
                for n in range(HEADS * SLOT_C):
                    if n >= 8:
                        pe.wait_ge(out_t, n_turn + n - 7)
                    pe.transpose(c.ps[n % 8][0:P, 0:SLOT_P], turned[:, n // SLOT_C, n % SLOT_C, :],
                                 c.ident[0:SLOT_P, 0:SLOT_P]).then_inc(pe_s, 1)

            @block.sync
            def _(sp):
                sp.wait_ge(out_t, n_turn)
                for a in range(HEADS + 2):
                    sp.dma_start(c.seq_dram[a].rearrange("(k p) e -> p k e", p=SLOT_P),
                                 turned[:, a]).then_inc(dma_o, 16)
                sp.wait_ge(dma_o, 16 * (HEADS + 2))
                chunks = "(c s) e -> c (s e)"
                sp.dma_start(seq[:, :], c.seq_dram[0:HEADS].rearrange("h (c s) e -> (h c) (s e)", s=SCAN_S))\
                    .then_inc(dma_i, 16)
                for h in range(HEADS):
                    for k, n in enumerate(("start", "end")):
                        sp.dma_start(reset[n][h * SCAN_C:(h + 1) * SCAN_C, :],
                                     c.seq_dram[HEADS + k].rearrange(chunks, s=SCAN_S)).then_inc(dma_i, 16)
                sp.wait_ge(ready, 6)
                sp.dma_start(c.max_dram.rearrange("h (c s) e -> (h c) (s e)", s=SCAN_S), bwd[:, :]).then_inc(dma_o, 16)
                sp.wait_ge(dma_o, 16 * (HEADS + 3))
                sp.dma_start(turned[:, 0:HEADS].rearrange("p h k e -> p (h k) e"),
                             c.max_dram.rearrange("h (k p) e -> p (h k) e", p=SLOT_P)).then_inc(dma_i, 16)

            @block.scalar
            def _(a):
                a.wait_ge(out_t, n_turn + HEADS * SLOT_C)
                a.activation(c.edge_cols[:, :, 0:HEADS], c.score[:, :, :], ACT.Exp).then_inc(dma_o, 1)


def add_sum(v, s, n, i, places, summed, added, to_of, part):
    t = places.at(i, n)
    v.wait_ge(summed, s + n + 1)
    if known(s, 1) or n >= 1:
        v.wait_ge(added, s + n)
    to = to_of(t)
    v.tensor_tensor(to, to, part, ALU.add).then_inc(added, 1)


def weighted_messages(nc, c):
    W = D + EXTRA
    LAG = 2
    with ExitStack() as ctx:
        def sb(name, shape, dt=F32):
            return ctx.enter_context(nc.sbuf_tensor(name, shape, dt))
        got = sb("got_b", [P, RING, D])
        rows = sb("rows_b", [P, RING], I32)
        hot = sb("hot_b", [P, RING, P])
        msg = sb("msg_b", [P, BUFS, W])
        filled = [c.sem(f"msgs_in{r}") for r in range(RING)]
        copied, let_go, hot_ready, weighted, cols_in, summed, added = (
            c.sem(n) for n in ("rows_copied_b", "pool_seen_b", "hot_ready_b", "weighted", "edge_cols_in", "summed_b", "added_b"))
        clear = c.sem("acc_clear_b")
        with nc.Block() as block:
            @block.gpsimd
            def _(pool):
                gather_rows(pool, rows, got, weighted, copied, c.msg_table, filled, let_go)

            @block.sync
            def _(sp):
                sp.dma_start(c.nodes[:, :, :], c.x.rearrange("(t p) d -> p t d", p=P)).then_inc(c.ahead, 16)
                sp.dma_start(c.wa_s[:, :, :, :], c.wa.rearrange("t (c p) o -> p t c o", p=128)).then_inc(c.ahead, 16)

            @block.scalar
            def _(a):
                def body(s, i):
                    for r in range(RING):
                        if known(s, 1) or r >= BUFS:
                            a.wait_ge(summed, s + r - BUFS + 1)
                        cols = c.edge_cols[:, s + r, :] if isinstance(s, int) else flat(c.edge_cols[:, ds(s + r, 1), :])
                        a.copy(msg[:, r % BUFS, D:W], cols).then_inc(cols_in, 1)
                        copy_next_rows(a, s, i, r, c.kv_idx, rows, filled, copied)
                copy_first_rows(a, c.kv_idx, rows, filled, copied)
                by_slots(a, body)

            @block.tensor
            def _(pe):
                def body(s, i):
                    for r in range(RING):
                        pe.wait_ge(weighted, s + r + 1)
                        pe.wait_ge(hot_ready, s + r + 1)
                        if known(s, 1) or r >= BUFS:
                            pe.wait_ge(added, s + r - BUFS + 1)
                        pe.wait_ge(cols_in, s + r + 1)
                        pe.matmul(c.ps[r % BUFS][0:P, 0:W], hot[:, r, :], msg[:, r % BUFS, :], start=True,
                                  stop=True).then_inc(summed, 1)
                by_slots(pe, body)

            @block.vector
            def _(v):
                v.memset(c.acc[:, :, :], 0.0).then_inc(clear, 1)
                v.wait_ge(clear, 1)

                places = Rows(v, "msg_tile", c.tile_row, NODE_TILES - 1)

                def add(s, n, i):
                    add_sum(v, s, n, i, places, summed, added, lambda t: c.acc[:, ds(t, 1), 0:W],
                            c.ps[n % BUFS][0:P, 0:W].unsqueeze(1))
                    if before_end(s, n, RING):
                        one_hot(v, c, hot, s, n, hot_ready, ahead=RING)

                def body(s, i):
                    for r in range(RING):
                        v.wait_ge(filled[r], 16 * (i + 1))
                        if known(s, 1) or r >= BUFS:
                            v.wait_ge(summed, s + r - BUFS + 1)
                        cols = c.edge_cols[:, s + r, 0:HEADS] if isinstance(s, int) else \
                            c.edge_cols[:, ds(s + r, 1), 0:HEADS].rearrange("p a h -> p (a h)")
                        v.tensor_tensor(msg[:, r % BUFS, 0:D].rearrange("p (h d) -> p h d", h=HEADS),
                                        got[:, r, :].rearrange("p (h d) -> p h d", h=HEADS),
                                        cols.unsqueeze(2).to_broadcast([P, HEADS, DK]), ALU.mult)\
                            .then_inc(weighted, 1)
                        if known(s, 1) or r >= LAG:
                            add(s - RING, r - LAG + RING, i - 1) if r < LAG else add(s, r - LAG, i)
                for r in range(RING):
                    one_hot(v, c, hot, 0, r, hot_ready)
                by_slots(v, body)
                for r in range(RING - LAG, RING):
                    add(SLOTS - RING, r, ROUNDS - 1)
                places.free()


def attention_output(nc, c):
    with ExitStack() as ctx:
        def sb(name, shape, dt=F32):
            return ctx.enter_context(nc.sbuf_tensor(name, shape, dt))
        wa = c.wa_s
        am = sb("am", [128, 2, NTYPES, KC, P])
        agg = sb("agg", [P, 2, D])
        rden = sb("rden", [P, NODE_TILES, HEADS])
        skip, gate_e = sb("skip", [P, NTYPES]), sb("gate_e", [P, NTYPES])
        ntype_i, ntype = sb("ntype_i", [P, NODE_TILES], I32), sb("ntype", [P, NODE_TILES])
        gate, tmp = sb("gate", [P, NODE_TILES]), sb("gate_tmp", [P, NODE_TILES])
        load, dve, act_s, agg_ready, turned, masked, mixed, out_done = (
            c.sem(n) for n in ("att_loads", "att_chain", "att_act", "agg_ready", "agg_turned", "agg_masked",
                               "agg_mixed", "att_out"))
        with nc.Block() as block:
            @block.sync
            def _(sp):
                sp.dma_start(skip[:, :], c.skip.partition_broadcast(P)).then_inc(load, 16)
                sp.dma_start(ntype_i[:, :], c.node_type_cols).then_inc(load, 16)

            @block.scalar
            def _(a):
                a.wait_ge(load, 32)
                a.activation(gate_e[:, :], skip[:, :], ACT.Exp, scale=-1.0).then_inc(act_s, 1)
                a.wait_ge(dve, 2)
                a.activation(c.rdeg[:, :], c.cnt[:, :, 0], ACT.Sqrt).then_inc(act_s, 1)

            @block.vector
            def _(v):
                do = Chain(v, dve)
                v.wait_ge(c.ahead, 32)
                do(v.tensor_scalar(c.cnt[:, :, :], c.acc[:, :, D + HEADS:D + EXTRA], 1.0, None, ALU.max))
                do(v.tensor_scalar(rden[:, :, :], c.acc[:, :, D:D + HEADS], 1e-30, None, ALU.max))
                do(v.reciprocal(rden[:, :, :], rden[:, :, :]))
                v.wait_ge(act_s, 2)
                do(v.reciprocal(c.rdeg[:, :], c.rdeg[:, :]))
                do(v.reciprocal(c.cnt[:, :, :], c.cnt[:, :, :]))
                do(v.tensor_scalar(gate_e[:, :], gate_e[:, :], 1.0, None, ALU.add))
                do(v.reciprocal(gate_e[:, :], gate_e[:, :]))
                do(v.tensor_copy(ntype[:, :], ntype_i[:, :]))
                do(v.memset(gate[:, :], 0.0))
                for y in range(NTYPES):
                    do(v.tensor_scalar(tmp[:, :], ntype[:, :], float(y), gate_e[:, y:y + 1], ALU.is_equal, ALU.mult))
                    do(v.tensor_tensor(gate[:, :], gate[:, :], tmp[:, :], ALU.add))

                def average(t, b, uses):
                    tile = slice(t, t + 1) if isinstance(t, int) else ds(t, 1)
                    if known(t, 2):
                        v.wait_ge(turned, t - 1)
                    v.tensor_tensor(agg[:, b, :].rearrange("p (h d) -> p h d", h=HEADS),
                                    c.acc[:, tile, 0:D].rearrange("p a (h d) -> p (a h) d", h=HEADS),
                                    rden[:, tile, :].rearrange("p a h -> p (a h)").unsqueeze(2)
                                    .to_broadcast([P, HEADS, DK]), ALU.mult).then_inc(agg_ready, 1)

                def mask(t, b, uses):
                    at = slice(t * P, (t + 1) * P) if isinstance(t, int) else ds(t * P, P)
                    v.wait_ge(turned, t + 1)
                    if known(t, 2):
                        v.wait_ge(mixed, t - 1)
                    for y in range(NTYPES):
                        m = v.scalar_tensor_tensor(
                            out=am[:, b, y], in0=c.type_row[:, at].unsqueeze(1).to_broadcast([128, KC, P]),
                            scalar=float(y), in1=c.ps[b][:, 0:KC * P].rearrange("p (c n) -> p c n", c=KC),
                            op0=ALU.is_equal, op1=ALU.mult)
                    m.then_inc(masked, 1)

                def residual(t, b, uses):
                    tile = slice(t, t + 1) if isinstance(t, int) else ds(t, 1)
                    v.wait_ge(mixed, t + 1)
                    v.scalar_tensor_tensor(out=c.nodes_b[:, tile, :], in0=c.ps[2 + b][0:P, 0:D].unsqueeze(1),
                                           scalar=gate[:, tile], in1=c.nodes[:, tile, :], op0=ALU.mult,
                                           op1=ALU.add).then_inc(out_done, 1)
                in_steps(v, (0, average), (1, mask), (3, residual))

            @block.tensor
            def _(pe):
                pe.wait_ge(c.ahead, 32)

                def turn(t, b, uses):
                    pe.wait_ge(agg_ready, t + 1)
                    if known(t, 2):
                        pe.wait_ge(masked, t - 1)
                    for k in range(KC):
                        mm = pe.transpose(c.ps[b][:, k * P:(k + 1) * P], agg[:, b, k * 128:(k + 1) * 128],
                                          c.ident[0:P, 0:P])
                    mm.then_inc(turned, 1)

                def mix(t, b, uses):
                    pe.wait_ge(masked, t + 1)
                    if known(t, 2):
                        pe.wait_ge(out_done, t - 1)
                    steps = [(y, k) for y in range(NTYPES) for k in range(KC)]
                    for i, (y, k) in enumerate(steps):
                        mm = pe.matmul(c.ps[2 + b][0:P, 0:D], am[:, b, y, k, :], wa[:, y, k, :], start=(i == 0),
                                       stop=(i == len(steps) - 1))
                    mm.then_inc(mixed, 1)
                in_steps(pe, (0, turn), (2, mix))


def row_norm(nc, c, name, src, to_dram, scale=None, final=False):
    with ExitStack() as ctx:
        def sb(n, shape, dt=F32):
            return ctx.enter_context(nc.sbuf_tensor(name + n, shape, dt))
        parts, mv = sb("_parts", [P, NODE_TILES, 6]), sb("_mv", [P, NODE_TILES, 2])
        rstd = sb("_rstd", [P, NODE_TILES])
        G = 5
        chain, act_s, rows, stored = (c.sem(name + n) for n in ("_chain", "_sqrt", "_rows", "_stored"))
        scaled = sb("_scaled", [P, NODE_TILES, D]) if scale is not None else c.nodes
        with nc.Block() as block:
            @block.vector
            def _(v):
                do = Chain(v, chain)

                def stats(t, b, uses):
                    tile = slice(t, t + 1) if isinstance(t, int) else ds(t, 1)
                    v.bn_stats(flat(parts[:, tile, :]), flat(src[:, tile, :])).then_inc(chain, 1)

                by_tiles(v, stats)
                v.wait_ge(chain, NODE_TILES)
                for t in range(NODE_TILES):
                    v.bn_aggr(mv[:, t, :], parts[:, t, :]).then_inc(chain, 1)
                v.wait_ge(chain, 2 * NODE_TILES)
                do.at(2 * NODE_TILES)
                do(v.tensor_scalar(rstd[:, :], mv[:, :, 1], LN_EPS, None, ALU.add))
                v.wait_ge(act_s, 1)
                do(v.reciprocal(rstd[:, :], rstd[:, :]))

                def apply(t, b, uses):
                    tile = slice(t, t + 1) if isinstance(t, int) else ds(t, 1)
                    v.tensor_scalar(c.nodes[:, tile, :], src[:, tile, :], flat(mv[:, tile, 0:1]), rstd[:, tile],
                                    ALU.subtract, ALU.mult).then_inc(rows, 1)
                    if scale is not None:
                        v.wait_ge(rows, 2 * t + 1)
                        v.tensor_scalar(scaled[:, tile, :], c.nodes[:, tile, :], scale[:, tile], None,
                                        ALU.mult).then_inc(rows, 1)
                by_tiles(v, apply)

            @block.scalar
            def _(a):
                a.wait_ge(chain, 2 * NODE_TILES + 1)
                a.activation(rstd[:, :], rstd[:, :], ACT.Sqrt).then_inc(act_s, 1)

            @block.sync
            def _(sp):
                to = to_dram.rearrange("(t p) d -> p t d", p=P)
                for t in range(0, NODE_TILES, G):
                    sp.wait_ge(rows, (t + G) * (1 if scale is None else 2))
                    sp.dma_start(to[:, t:t + G, :], scaled[:, t:t + G, :]).then_inc(stored, 16)
                sp.wait_ge(stored, 16 * (NODE_TILES // G))


EXPERTS, HIDDEN, TOPK, CAP = 64, 512, 2, 1024
HC = HIDDEN // 128
ROW_TILES = N * TOPK // P
STEPS = ROW_TILES + EXPERTS - 1
WRING = 6
BN_EPS = 1e-5


def by_ring(eng, body, count, ring):
    for s in range(ring + 1):
        body(s, s % ring, s // ring)
    with eng.Fori(1, (count - 1) // ring) as k:
        for i in range(ring):
            body(ring * k + 1 + i, (1 + i) % ring, k + (1 + i) // ring)
    for s in range((count - 1) // ring * ring + 1, count):
        body(s, s % ring, s // ring)


def graph_sum(nc, c, name, table, acc):
    with ExitStack() as ctx:
        def sb(n, shape, dt=F32):
            return ctx.enter_context(nc.sbuf_tensor(name + n, shape, dt))
        got = sb("_got", [P, RING, D])
        rows = sb("_rows", [P, RING], I32)
        hot = sb("_hot", [P, RING, P])
        filled = [c.sem(f"{name}_in{r}") for r in range(RING)]
        copied, let_go, hot_ready, summed, added, clear = (
            c.sem(name + n) for n in ("_rows_copied", "_pool_seen", "_hot_ready", "_summed", "_added", "_clear"))
        with nc.Block() as block:
            @block.gpsimd
            def _(pool):
                gather_rows(pool, rows, got, summed, copied, table, filled, let_go)

            @block.scalar
            def _(a):
                copy_all_rows(a, c.src_idx, rows, filled, copied)

            @block.tensor
            def _(pe):
                def body(s, i):
                    for r in range(RING):
                        pe.wait_ge(filled[r], 16 * (i + 1))
                        pe.wait_ge(hot_ready, s + r + 1)
                        if known(s, 1) or r >= BUFS:
                            pe.wait_ge(added, s + r - BUFS + 1)
                        pe.matmul(c.ps[r % BUFS][0:P, 0:D], hot[:, r, :], got[:, r, :], start=True,
                                  stop=True).then_inc(summed, 1)
                by_slots(pe, body)

            @block.vector
            def _(v):
                v.memset(acc[:, :, :], 0.0).then_inc(clear, 1)
                v.wait_ge(clear, 1)

                places = Rows(v, name + "_tile", c.tile_row, NODE_TILES - 1)

                def body(s, i):
                    for r in range(RING):
                        add_sum(v, s, r, i, places, summed, added, lambda t: acc[:, ds(t, 1), :],
                                c.ps[r % BUFS][0:P, 0:D].unsqueeze(1))
                        if before_end(s, r, RING):
                            one_hot(v, c, hot, s, r, hot_ready, ahead=RING)
                for r in range(RING):
                    one_hot(v, c, hot, 0, r, hot_ready)
                by_slots(v, body)
                places.free()


def conv_and_router(nc, c, acc, x1, logits):
    with ExitStack() as ctx:
        def sb(name, shape, dt=F32):
            return ctx.enter_context(nc.sbuf_tensor(name, shape, dt))
        w = sb("w_conv", [128, 2, KC, D])
        wg = sb("w_router", [128, KC, EXPERTS])
        bias, bias2, bg = sb("conv_bias", [P, D]), sb("conv_bias2", [P, D]), sb("router_bias", [P, EXPERTS])
        cat = sb("conv_cat", [P, 2, 2 * D])
        cat_t = sb("conv_t", [128, 2, 2 * KC, P])
        x1s = sb("x1s", [P, 2, D])
        x1_t = sb("x1_t", [128, 2, KC, P])
        load, chain, cat_ready, turned, t_ready, conv, x1_ready, x1_turned, x1_t_ready, routed, log_ready = (
            c.sem(n) for n in ("conv_loads", "conv_chain", "conv_cat_ready", "conv_turned", "conv_t_ready", "conv_done",
                               "x1_ready", "x1_turned", "x1_t_ready", "routed", "logits_ready"))
        cat_half, copied = c.sem("conv_cat_half"), c.sem("x1_kept")
        with nc.Block() as block:
            @block.sync
            def _(sp):
                for k, a in enumerate((c.W_gc, c.W_res)):
                    sp.dma_start(w[:, k], a.rearrange("(c p) o -> p c o", p=128)).then_inc(load, 16)
                sp.dma_start(wg[:, :, :], c.Wg.rearrange("(c p) o -> p c o", p=128)).then_inc(load, 16)
                sp.dma_start(bias[:, :], c.b_gc.partition_broadcast(P)).then_inc(load, 16)
                sp.dma_start(bias2[:, :], c.b_res.partition_broadcast(P)).then_inc(load, 16)
                sp.dma_start(bg[:, :], c.bg.partition_broadcast(P)).then_inc(load, 16)

            @block.vector
            def _(v):
                do = Chain(v, chain)
                v.wait_ge(load, 96)
                do(v.tensor_tensor(bias[:, :], bias[:, :], bias2[:, :], ALU.add))

                def scale(t, b, uses):
                    if known(t, 2):
                        v.wait_ge(turned, t - 1)
                    v.tensor_scalar(cat[:, b, 0:D], flat(acc[:, tile_at(t), :]), c.rdeg[:, tile_at(t)], None,
                                    ALU.mult).then_inc(cat_ready, 1)

                def add_bias(t, b, uses):
                    v.wait_ge(conv, t + 1)
                    if known(t, 2):
                        v.wait_ge(x1_turned, t - 1)
                        v.wait_ge(copied, t - 1)
                    v.tensor_tensor(x1s[:, b, :], c.ps[2 + b][0:P, 0:D], bias[:, :], ALU.add).then_inc(x1_ready, 1)

                def logit(t, b, uses):
                    v.wait_ge(routed, t + 1)
                    v.tensor_tensor(flat(logits[:, tile_at(t), :]), c.ps[6 + b][0:P, 0:EXPERTS], bg[:, :],
                                    ALU.add).then_inc(log_ready, 1)
                in_steps(v, (0, scale), (3, logit), (1, add_bias))

            @block.scalar
            def _(a):
                def join(t, b, uses):
                    if known(t, 2):
                        a.wait_ge(turned, t - 1)
                    a.copy(cat[:, b, D:2 * D], flat(c.nodes[:, tile_at(t), :])).then_inc(cat_half, 1)

                def take_turned(t, b, uses):
                    a.wait_ge(turned, t + 1)
                    if known(t, 2):
                        a.wait_ge(conv, t - 1)
                    a.copy(cat_t[:, b], c.ps[b][:, 0:2 * KC * P].rearrange("p (c n) -> p c n", n=P)).then_inc(t_ready, 1)

                def take_x1_turned(t, b, uses):
                    a.wait_ge(x1_turned, t + 1)
                    if known(t, 2):
                        a.wait_ge(routed, t - 1)
                    a.copy(x1_t[:, b], c.ps[4 + b][:, 0:KC * P].rearrange("p (c n) -> p c n", n=P)).then_inc(x1_t_ready, 1)

                def keep_x1(t, b, uses):
                    a.wait_ge(x1_ready, t + 1)
                    a.copy(flat(x1[:, tile_at(t), :]), x1s[:, b, :]).then_inc(copied, 1)
                in_steps(a, (0, join), (1, take_turned), (2, keep_x1), (3, take_x1_turned))

            @block.tensor
            def _(pe):
                pe.wait_ge(load, 96)

                def turn(t, b, uses):
                    pe.wait_ge(cat_ready, t + 1)
                    pe.wait_ge(cat_half, t + 1)
                    if known(t, 2):
                        pe.wait_ge(t_ready, t - 1)
                    for k in range(2 * KC):
                        mm = pe.transpose(c.ps[b][:, k * P:(k + 1) * P], cat[:, b, k * 128:(k + 1) * 128],
                                          c.ident[0:P, 0:P])
                    mm.then_inc(turned, 1)

                def convolve(t, b, uses):
                    pe.wait_ge(t_ready, t + 1)
                    if known(t, 2):
                        pe.wait_ge(x1_ready, t - 1)
                    for k in range(2 * KC):
                        mm = pe.matmul(c.ps[2 + b][0:P, 0:D], cat_t[:, b, k, :], w[:, k // KC, k % KC, :],
                                       start=(k == 0), stop=(k == 2 * KC - 1))
                    mm.then_inc(conv, 1)

                def turn_x1(t, b, uses):
                    pe.wait_ge(x1_ready, t + 1)
                    if known(t, 2):
                        pe.wait_ge(x1_t_ready, t - 1)
                    for k in range(KC):
                        mm = pe.transpose(c.ps[4 + b][:, k * P:(k + 1) * P], x1s[:, b, k * 128:(k + 1) * 128],
                                          c.ident[0:P, 0:P])
                    mm.then_inc(x1_turned, 1)

                def router(t, b, uses):
                    pe.wait_ge(x1_t_ready, t + 1)
                    if known(t, 2):
                        pe.wait_ge(log_ready, t - 1)
                    for k in range(KC):
                        mm = pe.matmul(c.ps[6 + b][0:P, 0:EXPERTS], x1_t[:, b, k, :], wg[:, k, :],
                                       start=(k == 0), stop=(k == KC - 1))
                    mm.then_inc(routed, 1)
                in_steps(pe, (0, turn), (3, router), (1, convolve), (2, turn_x1))


def route(nc, c, x1, logits):
    with ExitStack() as ctx:
        def sb(name, shape, dt=F32):
            return ctx.enter_context(nc.sbuf_tensor(name, shape, dt))
        T, X = NODE_TILES, EXPERTS
        wide = [P, T, X]
        iota_m = sb("iota_m", [P, X])
        pick = [sb("pick0", wide), sb("pick1", wide)]
        both, before, work, run = sb("both", wide), sb("before", wide), sb("work", wide), sb("run", [P, T + 1, X])
        val = [sb("val0", [P, T]), sb("val1", [P, T])]
        idx, base, total = sb("idx", [P, T]), sb("base", [P, X]), sb("total", [P, X])
        rank, gap = sb("rank", [P, T]), sb("gap", [P, T])
        pos_f = sb("pos_f", [P, T])
        row_i, row_f = sb("row_ids_i", [P, ROW_TILES], I32), sb("row_ids", [P, ROW_TILES])
        key, key_i = sb("step_key", [P, X]), sb("step_key_i", [P, X], I32)
        lim_i, lim = sb("step_lim_i", [P, STEPS], I32), sb("step_lim", [P, STEPS])
        step_i, tile = sb("step_i", [P, STEPS], I32), sb("step_tile", [P, STEPS])
        grid = sb("grid", [P, STEPS, X])
        chain, act_s, pe_s, iotas, run_ready, pfx, rows_in, pos_ready = (
            c.sem(n) for n in ("route_chain", "route_exp", "route_mm", "route_iotas", "run_ready", "prefix_copied",
                               "rows_stored", "positions_ready"))

        def over_experts(ap):
            return ap.unsqueeze(2).to_broadcast(wide)

        def over_tiles(ap):
            return ap.unsqueeze(1).to_broadcast(wide)

        with nc.Block() as block:
            @block.gpsimd
            def _(pool):
                pool.iota(row_i[:, :], [[P, ROW_TILES]], base=0, channel_multiplier=1).then_inc(iotas, 1)
                pool.iota(key_i[:, :], [[P, X]], base=0, channel_multiplier=0).then_inc(iotas, 1)
                pool.iota(lim_i[:, :], [[P, STEPS]], base=P, channel_multiplier=0).then_inc(iotas, 1)
                pool.iota(step_i[:, :], [[1, STEPS]], base=0, channel_multiplier=0).then_inc(iotas, 1)
                pool.wait_ge(pos_ready, 1)
                for k in range(TOPK):
                    for t in range(T):
                        pool.indirect_dma_start(c.row_table, bass.IndirectOffsetOnAxis(c.pos[k][:, t:t + 1], 0),
                                                x1[:, t, :], None).then_inc(rows_in, 16)
                pool.wait_ge(rows_in, 16 * TOPK * T)

            @block.scalar
            def _(a):
                a.wait_ge(run_ready, 1)
                a.activation(gap[:, :], gap[:, :], ACT.Exp).then_inc(act_s, 1)

                def body(t, b, uses):
                    a.wait_ge(pe_s, t + 1)
                    a.copy(flat(before[:, tile_at(t), :]), c.ps[b][0:P, 0:X]).then_inc(pfx, 1)
                by_tiles(a, body)

            @block.tensor
            def _(pe):
                pe.wait_ge(run_ready, 2)

                def body(t, b, uses):
                    if known(t, 2):
                        pe.wait_ge(pfx, t - 1)
                    pe.matmul(c.ps[b][0:P, 0:X], c.below[0:P, 0:P], flat(both[:, tile_at(t), :]), start=True, stop=False)
                    pe.matmul(c.ps[b][0:P, 0:X], c.ones[0:P, 0:P], flat(run[:, tile_at(t), :]), start=False,
                              stop=True).then_inc(pe_s, 1)
                by_tiles(pe, body)
                pe.matmul(c.ps[2][0:P, 0:X], c.ones[0:P, 0:P], run[:, T, :], start=True, stop=True).then_inc(pe_s, 1)

            @block.vector
            def _(v):
                do = Chain(v, chain)
                do(v.tensor_scalar(iota_m[:, :], c.iota[0:P, 0:X], -float(X), None, ALU.add))
                for k in range(TOPK):
                    do(v.tensor_reduce(val[k][:, :], logits[:, :, :], AX, ALU.max))
                    do(v.tensor_tensor(work[:, :, :], logits[:, :, :], over_experts(val[k][:, :]), ALU.is_equal))
                    do(v.scalar_tensor_tensor(out=work[:, :, :], in0=work[:, :, :], scalar=-float(X),
                                              in1=over_tiles(c.iota[0:P, 0:X]), op0=ALU.mult, op1=ALU.add))
                    do(v.tensor_reduce(idx[:, :], work[:, :, :], AX, ALU.min))
                    do(v.tensor_tensor(pick[k][:, :, :], over_tiles(iota_m[:, :]), over_experts(idx[:, :]), ALU.is_equal))
                    if k == 0:
                        do(v.scalar_tensor_tensor(out=logits[:, :, :], in0=pick[0][:, :, :], scalar=-BIG,
                                                  in1=logits[:, :, :], op0=ALU.mult, op1=ALU.add))
                do(v.tensor_tensor(gap[:, :], val[1][:, :], val[0][:, :], ALU.subtract))
                v.sem_inc(run_ready, 1)
                do(v.tensor_tensor(both[:, :, :], pick[0][:, :, :], pick[1][:, :, :], ALU.add))
                do(v.memset(run[:, 0, :], 0.0))
                at = do.n

                def body(t, b, uses):
                    do.at(at + t)
                    n = t + 1
                    do(v.tensor_tensor(run[:, tile_at(n), :], run[:, tile_at(t), :], both[:, tile_at(t), :], ALU.add))
                by_tiles(v, body)
                do.at(at + T)
                v.sem_inc(run_ready, 1)
                v.wait_ge(act_s, 1)
                do(v.tensor_scalar(rank[:, :], gap[:, :], 1.0, None, ALU.add))
                do(v.reciprocal(c.gate[0][:, :], rank[:, :]))
                do(v.tensor_tensor(c.gate[1][:, :], gap[:, :], c.gate[0][:, :], ALU.mult))
                v.wait_ge(pe_s, T + 1)
                v.wait_ge(pfx, T)
                do(v.tensor_copy(total[:, :], c.ps[2][0:P, 0:X]))
                do(v.tensor_tensor_scan(base[:, :], c.ones[0:P, 0:X], total[:, :], 0.0, ALU.mult, ALU.add))
                do(v.tensor_tensor(base[:, :], base[:, :], total[:, :], ALU.subtract))
                for k in range(TOPK):
                    do(v.tensor_tensor(work[:, :, :], pick[k][:, :, :], before[:, :, :], ALU.mult))
                    do(v.tensor_reduce(rank[:, :], work[:, :, :], AX, ALU.add))
                    do(v.scalar_tensor_tensor(out=c.gate[k][:, :], in0=rank[:, :], scalar=float(CAP),
                                              in1=c.gate[k][:, :], op0=ALU.is_lt, op1=ALU.mult))
                    do(v.tensor_tensor(work[:, :, :], pick[k][:, :, :], over_tiles(base[:, :]), ALU.mult))
                    do(v.tensor_reduce(pos_f[:, :], work[:, :, :], AX, ALU.add))
                    do(v.tensor_tensor(pos_f[:, :], pos_f[:, :], rank[:, :], ALU.add))
                    do(v.tensor_copy(c.pos[k][:, :], pos_f[:, :]))
                v.sem_inc(pos_ready, 1)
                v.wait_ge(iotas, 4)
                for f, i in ((row_f, row_i), (key, key_i), (lim, lim_i), (tile, step_i)):
                    do(v.tensor_copy(f[:, :], i[:, :]))
                g = grid[:, 0:ROW_TILES, :]
                do(v.tensor_tensor(g, row_f[:, :].unsqueeze(2).to_broadcast([P, ROW_TILES, X]),
                                   base[:, :].unsqueeze(1).to_broadcast([P, ROW_TILES, X]), ALU.is_ge))
                do(v.tensor_reduce(c.row_expert[:, :], g, AX, ALU.add))
                do(v.tensor_scalar(c.row_expert[:, :], c.row_expert[:, :], -1.0, None, ALU.add))
                do(v.scalar_tensor_tensor(out=key[:, :], in0=base[:, :], scalar=float(ROW_TILES * P - 1), in1=key[:, :],
                                          op0=ALU.min, op1=ALU.add))
                do(v.tensor_tensor(grid[:, :, :], lim[:, :].unsqueeze(2).to_broadcast([P, STEPS, X]),
                                   key[:, :].unsqueeze(1).to_broadcast([P, STEPS, X]), ALU.is_gt))
                do(v.tensor_reduce(c.step_expert[:, :], grid[:, :, :], AX, ALU.add))
                do(v.tensor_scalar(c.step_expert[:, :], c.step_expert[:, :], -1.0, None, ALU.add))
                do(v.tensor_tensor(tile[:, :], tile[:, :], c.step_expert[:, :], ALU.subtract))
                do(v.tensor_copy(c.step_rows[0:1, 0, :], tile[0:1, :]))
                do(v.tensor_copy(c.step_rows[0:1, 1, :], c.step_expert[0:1, :]))


def experts(nc, c):
    with ExitStack() as ctx:
        def sb(name, shape, dt=F32):
            return ctx.enter_context(nc.sbuf_tensor(name, shape, dt))
        w1, w2 = sb("w1", [128, WRING, KC, HIDDEN]), sb("w2", [128, WRING, HC, D])
        b1, b2 = sb("b1", [128, WRING, HC]), sb("b2", [1, WRING, D])
        xr = sb("xr", [P, WRING, D])
        xt = sb("xr_t", [128, 2, KC, P])
        h = sb("hidden", [128, 2, HC, P])
        mask = sb("row_mask", [P, 2, 1])
        y = sb("expert_rows", [P, ROW_TILES, D])
        loaded = [c.sem(f"weights_in{b}") for b in range(WRING)]
        turned, xt_ready, up, act_s, down, kept, mask_s, clear, stored, seen = (
            c.sem(n) for n in ("rows_turned", "rows_t_ready", "up_done", "gelu_done", "down_done", "rows_kept",
                               "row_mask_ready", "rows_clear", "expert_rows_stored", "expert_seen"))
        with nc.Block() as block:
            @block.sync
            def _(sp):
                def body(s, b, uses):
                    j = sp.value_load(c.step_rows[0:1, 0, tile_at(s)], min_val=0, max_val=ROW_TILES - 1)
                    e = sp.value_load(c.step_rows[0:1, 1, tile_at(s)], min_val=0, max_val=EXPERTS - 1)
                    if known(s, WRING):
                        sp.wait_ge(down, s - WRING + 1)
                    sp.dma_start(xr[:, b, :], c.row_table[ds(j * P, P), :]).then_inc(loaded[b], 16)
                    sp.dma_start(w1[:, b], c.w1[ds(e, 1)].rearrange("a (c p) h -> p (a c) h", p=128)).then_inc(loaded[b], 16)
                    sp.dma_start(b1[:, b, :], c.b1[ds(e, 1)].rearrange("a p c -> (a p) c")).then_inc(loaded[b], 16)
                    sp.dma_start(w2[:, b], c.w2[ds(e, 1)].rearrange("a (c p) h -> p (a c) h", p=128)).then_inc(loaded[b], 16)
                    sp.dma_start(b2[:, b, :], c.b2[ds(e, 1)]).then_inc(loaded[b], 16)
                by_ring(sp, body, STEPS, WRING)
                sp.wait_ge(kept, STEPS)
                sp.dma_start(c.expert_table.rearrange("(j p) d -> p j d", p=P), y[:, :, :]).then_inc(stored, 16)
                sp.wait_ge(stored, 16)

            @block.tensor
            def _(pe):
                def down_layer(s, b):
                    pe.wait_ge(act_s, HC * s + HC)
                    if known(s, 2):
                        pe.wait_ge(kept, s - 1)
                    for m in range(HC):
                        pe.matmul(c.ps[4 + b % 2][0:P, 0:D], h[:, b % 2, m, :], w2[:, b, m, :], start=(m == 0), stop=False)
                    pe.matmul(c.ps[4 + b % 2][0:P, 0:D], c.ones[0:1, 0:P], b2[:, b, :], start=False,
                              stop=True).then_inc(down, 1)

                def turn(s, b, uses):
                    pe.wait_ge(loaded[b], 80 * (uses + 1))
                    if known(s, 2):
                        pe.wait_ge(xt_ready, s - 1)
                    for k in range(KC):
                        mm = pe.transpose(c.ps[b % 2][:, k * P:(k + 1) * P], xr[:, b, k * 128:(k + 1) * 128],
                                          c.ident[0:P, 0:P])
                    mm.then_inc(turned, 1)

                def up_layer(s, b):
                    pe.wait_ge(xt_ready, s + 1)
                    if known(s, 2):
                        pe.wait_ge(act_s, HC * s - HC)
                    for m in range(HC):
                        for k in range(KC):
                            mm = pe.matmul(c.ps[2 + b % 2][:, m * P:(m + 1) * P], w1[:, b, k, m * 128:(m + 1) * 128],
                                           xt[:, b % 2, k, :], start=(k == 0), stop=(k == KC - 1))
                    mm.then_inc(up, 1)

                def body(s, b, uses):
                    turn(s, b, uses)
                    if known(s, 1):
                        up_layer(s - 1, (b - 1) % WRING)
                    if known(s, 2):
                        down_layer(s - 2, (b - 2) % WRING)
                by_ring(pe, body, STEPS, WRING)
                up_layer(STEPS - 1, (STEPS - 1) % WRING)
                down_layer(STEPS - 2, (STEPS - 2) % WRING)
                down_layer(STEPS - 1, (STEPS - 1) % WRING)

            @block.scalar
            def _(a):
                def body(s, b, uses):
                    a.wait_ge(up, s + 1)
                    if known(s, 2):
                        a.wait_ge(down, s - 1)
                    for m in range(HC):
                        a.activation(h[:, b % 2, m, :], c.ps[2 + b % 2][:, m * P:(m + 1) * P], ACT.Gelu,
                                     bias=b1[:, b, m:m + 1]).then_inc(act_s, 1)
                by_ring(a, body, STEPS, WRING)

            @block.vector
            def _(v):
                v.memset(y[:, :, :], 0.0).then_inc(clear, 1)
                v.wait_ge(clear, 1)

                def keep(s, b):
                    j = v.value_load(c.step_rows[0:1, 0, tile_at(s)], min_val=0, max_val=ROW_TILES - 1)
                    if known(s, 1):
                        v.wait_ge(kept, s)
                    v.tensor_scalar(mask[:, b % 2, :], c.row_expert[:, ds(j, 1)], c.step_expert[:, tile_at(s)], None,
                                    ALU.is_equal).then_inc(mask_s, 1)
                    v.wait_ge(mask_s, s + 1)
                    v.wait_ge(down, s + 1)
                    to = y[:, ds(j, 1), :]
                    v.scalar_tensor_tensor(out=to, in0=c.ps[4 + b % 2][0:P, 0:D].unsqueeze(1), scalar=mask[:, b % 2, :],
                                           in1=to, op0=ALU.mult, op1=ALU.add).then_inc(kept, 1)

                def body(s, b, uses):
                    v.wait_ge(turned, s + 1)
                    if known(s, 2):
                        v.wait_ge(up, s - 1)
                    v.tensor_copy(xt[:, b % 2], c.ps[b % 2][:, 0:KC * P].rearrange("p (c n) -> p c n", n=P)).then_inc(xt_ready, 1)
                    if known(s, 2):
                        keep(s - 2, (b - 2) % WRING)
                by_ring(v, body, STEPS, WRING)
                keep(STEPS - 2, (STEPS - 2) % WRING)
                keep(STEPS - 1, (STEPS - 1) % WRING)


def combine(nc, c, x1):
    with nc.sbuf_tensor("chosen0", [P, NODE_TILES, D], F32) as y0, nc.sbuf_tensor("chosen1", [P, NODE_TILES, D], F32) as y1:
        G = 5
        got = [c.sem(f"chosen_in{g}") for g in range(NODE_TILES // G)]
        added = c.sem("chosen_added")
        with nc.Block() as block:
            @block.gpsimd
            def _(pool):
                for t in range(NODE_TILES):
                    for k, y in enumerate((y0, y1)):
                        pool.indirect_dma_start(y[:, t, :], None, c.expert_table,
                                                bass.IndirectOffsetOnAxis(c.pos[k][:, t:t + 1], 0)).then_inc(got[t // G], 16)

            @block.tensor
            def _(pe):
                for t in range(NODE_TILES):
                    if t % G == 0:
                        pe.wait_ge(added, TOPK * (t + G))
                    pe.matmul(c.ps[7][0:P, 0:D], c.ones[0:P, 0:P], x1[:, t, :], start=(t == 0),
                              stop=(t == NODE_TILES - 1))

            @block.vector
            def _(v):
                for g in range(NODE_TILES // G):
                    v.wait_ge(got[g], 16 * G * TOPK)
                    for k, y in enumerate((y0, y1)):
                        if k:
                            v.wait_ge(added, TOPK * G * g + G)
                        for t in range(g * G, (g + 1) * G):
                            v.scalar_tensor_tensor(out=x1[:, t, :], in0=y[:, t, :], scalar=c.gate[k][:, t:t + 1],
                                                   in1=x1[:, t, :], op0=ALU.mult, op1=ALU.add).then_inc(added, 1)


def batch_norm(nc, c, name, y, gamma, beta):
    with ExitStack() as ctx:
        def sb(n, shape, dt=F32):
            return ctx.enter_context(nc.sbuf_tensor(name + n, shape, dt))
        g, be = sb("_gamma", [P, D]), sb("_beta", [P, D])
        mean, rstd = sb("_mean", [P, D]), sb("_rstd", [P, D])
        sq = sb("_sq", [P, NODE_TILES, D])
        load, chain, mm, act_s, centred, squared = (
            c.sem(name + n) for n in ("_loads", "_chain", "_sums", "_act", "_centred", "_squared"))
        G = 5

        def over_tiles(ap, n):
            return ap.unsqueeze(1).to_broadcast([P, n, D])
        with nc.Block() as block:
            @block.sync
            def _(sp):
                sp.dma_start(g[:, :], gamma.partition_broadcast(P)).then_inc(load, 16)
                sp.dma_start(be[:, :], beta.partition_broadcast(P)).then_inc(load, 16)

            @block.tensor
            def _(pe):
                for t in range(NODE_TILES):
                    if t % G == 0:
                        pe.wait_ge(squared, t // G + 1)
                    m = pe.matmul(c.ps[1][0:P, 0:D], c.ones[0:P, 0:P], sq[:, t, :], start=(t == 0),
                                  stop=(t == NODE_TILES - 1))
                m.then_inc(mm, 1)

            @block.scalar
            def _(a):
                for t in range(0, NODE_TILES, G):
                    a.wait_ge(centred, t // G + 1)
                    a.activation(sq[:, t:t + G, :], y[:, t:t + G, :], ACT.Square).then_inc(squared, 1)
                a.wait_ge(chain, 3)
                a.activation(rstd[:, :], rstd[:, :], ACT.Sqrt).then_inc(act_s, 1)

            @block.vector
            def _(v):
                do = Chain(v, chain)
                do(v.tensor_scalar(mean[:, :], c.ps[7][0:P, 0:D], 1.0 / N, None, ALU.mult))
                for t in range(0, NODE_TILES, G):
                    v.tensor_tensor(y[:, t:t + G, :], y[:, t:t + G, :], over_tiles(mean[:, :], G),
                                    ALU.subtract).then_inc(centred, 1)
                v.wait_ge(load, 32)
                do(v.tensor_tensor(c.nodes[:, :, :], c.nodes[:, :, :], over_tiles(be[:, :], NODE_TILES), ALU.add))
                v.wait_ge(mm, 1)
                do(v.tensor_scalar(rstd[:, :], c.ps[1][0:P, 0:D], 1.0 / N, BN_EPS, ALU.mult, ALU.add))
                v.wait_ge(act_s, 1)
                do(v.reciprocal(rstd[:, :], rstd[:, :]))
                do(v.tensor_tensor(rstd[:, :], rstd[:, :], g[:, :], ALU.mult))
                do(v.tensor_tensor(y[:, :, :], y[:, :, :], over_tiles(rstd[:, :], NODE_TILES), ALU.mult))
                do(v.tensor_tensor(y[:, :, :], y[:, :, :], c.nodes[:, :, :], ALU.add))


def linear(nc, c, acc, y):
    with ExitStack() as ctx:
        def sb(name, shape, dt=F32):
            return ctx.enter_context(nc.sbuf_tensor(name, shape, dt))
        w, bias = sb("w_lin", [128, KC, D]), sb("lin_bias", [P, D])
        hs, ht = sb("lin_h", [P, 2, D]), sb("lin_ht", [128, 2, KC, P])
        load, ready, turned, t_ready, mixed, out = (
            c.sem(n) for n in ("lin_loads", "lin_h_ready", "lin_turned", "lin_t_ready", "lin_mixed", "lin_out"))
        with nc.Block() as block:
            @block.sync
            def _(sp):
                sp.dma_start(w[:, :, :], c.w_linT.rearrange("(c p) o -> p c o", p=128)).then_inc(load, 16)
                sp.dma_start(bias[:, :], c.b_lin.partition_broadcast(P)).then_inc(load, 16)

            @block.vector
            def _(v):
                v.wait_ge(load, 32)

                def last(t, b, uses):
                    v.wait_ge(mixed, t + 1)
                    v.tensor_tensor(flat(y[:, tile_at(t), :]), c.ps[2 + b][0:P, 0:D], bias[:, :], ALU.add).then_inc(out, 1)

                def total(t, b, uses):
                    if known(t, 2):
                        v.wait_ge(turned, t - 1)
                    v.tensor_tensor(hs[:, b, :], flat(acc[:, tile_at(t), :]), flat(c.nodes[:, tile_at(t), :]),
                                    ALU.add).then_inc(ready, 1)
                in_steps(v, (0, total), (2, last))

            @block.scalar
            def _(a):
                def body(t, b, uses):
                    a.wait_ge(turned, t + 1)
                    if known(t, 2):
                        a.wait_ge(mixed, t - 1)
                    a.copy(ht[:, b], c.ps[b][:, 0:KC * P].rearrange("p (c n) -> p c n", n=P)).then_inc(t_ready, 1)
                by_tiles(a, body)

            @block.tensor
            def _(pe):
                pe.wait_ge(load, 32)

                def turn(t, b, uses):
                    pe.wait_ge(ready, t + 1)
                    if known(t, 2):
                        pe.wait_ge(t_ready, t - 1)
                    for k in range(KC):
                        mm = pe.transpose(c.ps[b][:, k * P:(k + 1) * P], hs[:, b, k * 128:(k + 1) * 128], c.ident[0:P, 0:P])
                    mm.then_inc(turned, 1)

                def mix(t, b, uses):
                    pe.wait_ge(t_ready, t + 1)
                    if known(t, 2):
                        pe.wait_ge(out, t - 1)
                    for k in range(KC):
                        mm = pe.matmul(c.ps[2 + b][0:P, 0:D], ht[:, b, k, :], w[:, k, :], start=(k == 0), stop=(k == KC - 1))
                    mm.then_inc(mixed, 1)

                def column_sums(t, b, uses):
                    pe.wait_ge(out, t + 1)
                    pe.matmul(c.ps[7][0:P, 0:D], c.ones[0:P, 0:P], flat(y[:, tile_at(t), :]),
                              start=(isinstance(t, int) and t == 0), stop=True, skip_group_check=True)
                in_steps(pe, (0, turn), (1, mix), (3, column_sums))


PARTS = 3


def split_edge_product(nc, c):
    G, H = 5, 2
    T, K = EDGE_TILES // G, ATTRS // H
    B = 3
    steps = [(g, h) for g in range(G) for h in range(H)]
    with ExitStack() as ctx:
        def sb(name, shape, dt=F32):
            return ctx.enter_context(nc.sbuf_tensor(name, shape, dt))
        a = sb("attr_in", [T, B, K, P])
        parts = sb("attr_split", [T, B, PARTS, K, 2, P], BF16)
        w, w_parts = sb("edge_w_in", [ATTRS + 1, D]), sb("edge_w_split", [ATTRS + 1, PARTS, D], BF16)
        loaded = [c.sem(f"attr_loaded{b}") for b in range(B)]
        stored = [c.sem(f"attr_stored{b}") for b in range(B)]
        w_load, w_chain, w_done, w_put, high, rest, mid, low, high_copy, by_pool, by_dve, mid_copy = (
            c.sem(n) for n in ("edge_w_loads", "edge_w_chain", "edge_w_done", "edge_w_put", "attr_high", "attr_rest",
                               "attr_mid", "attr_low", "attr_high_copy", "attr_high_by_pool", "attr_high_by_dve", "attr_mid_copy"))
        with nc.Block() as block:
            @block.sync
            def _(sp):
                def fetch(n):
                    g, h = steps[n]
                    sp.dma_start(a[:, n % B], c.attrT[g * T:(g + 1) * T, h * K:(h + 1) * K, :])\
                        .then_inc(loaded[n % B], 16)
                sp.dma_start(w[0:ATTRS, :], c.edge_w).then_inc(w_load, 16)
                sp.dma_start(w[ATTRS:ATTRS + 1, :], c.edge_b).then_inc(w_load, 16)
                for n in range(B):
                    fetch(n)
                for n, (g, h) in enumerate(steps):
                    sp.wait_ge(low, n + 1)
                    if n + B < len(steps):
                        fetch(n + B)
                    for copy in (high_copy, mid_copy):
                        sp.wait_ge(copy, n + 1)
                    sp.wait_ge((by_pool, by_dve)[n % 2], n // 2 + 1)
                    sp.dma_start(c.attr_parts[g * T:(g + 1) * T].rearrange("j (q k) b e -> j q (k b e)", q=PARTS)
                                 [:, :, h * K * 2 * P:(h + 1) * K * 2 * P],
                                 parts[:, n % B].rearrange("j q k b e -> j q (k b e)")).then_inc(stored[n % B], 16)
                sp.wait_ge(w_done, 1)
                for row, b, part in ((0, 0, 0), (1, 0, 1), (2, 0, 2), (0, 1, 0), (1, 1, 1), (2, 1, 0)):
                    sp.dma_start(c.ew_parts[row * ATTRS:(row + 1) * ATTRS, b, :], w_parts[0:ATTRS, part, :])\
                        .then_inc(w_put, 16)
                for q in range(PARTS):
                    row = PARTS * ATTRS + q
                    sp.dma_start(c.ew_parts[row:row + 1, 0, :], w_parts[ATTRS:ATTRS + 1, q, :]).then_inc(w_put, 16)
                sp.wait_ge(w_put, 16 * (2 * PARTS + PARTS))
                for b in range(B):
                    sp.wait_ge(stored[b], 16 * len(steps[b::B]))

            @block.scalar
            def _(act):
                for n in range(len(steps) + 1):
                    if n < len(steps):
                        act.wait_ge(loaded[n % B], 16 * (n // B + 1))
                        if n >= B:
                            act.wait_ge(stored[n % B], 16 * (n // B))
                        act.copy(parts[:, n % B, 0, :, 0, :], a[:, n % B]).then_inc(high, 1)
                        act.wait_ge(high, n + 1)
                        act.copy(parts[:, n % B, 1, :, 0, :], parts[:, n % B, 0, :, 0, :]).then_inc(high_copy, 1)
                    if n >= 1:
                        act.wait_ge(rest, n)
                        act.copy(parts[:, (n - 1) % B, 0, :, 1, :], a[:, (n - 1) % B]).then_inc(mid, 1)

            @block.gpsimd
            def _(pool):
                for n in range(0, len(steps), 2):
                    pool.wait_ge(high, n + 1)
                    pool.tensor_copy(parts[:, n % B, 2, :, 0, :], parts[:, n % B, 0, :, 0, :]).then_inc(by_pool, 1)

            @block.vector
            def _(v):
                do = Chain(v, w_chain)
                v.wait_ge(w_load, 32)
                do(v.tensor_copy(w_parts[:, 0, :], w[:, :]))
                do(v.tensor_tensor(w[:, :], w[:, :], w_parts[:, 0, :], ALU.subtract))
                do(v.tensor_copy(w_parts[:, 1, :], w[:, :]))
                do(v.tensor_tensor(w_parts[:, 2, :], w[:, :], w_parts[:, 1, :], ALU.subtract))
                v.sem_inc(w_done, 1)
                for n in range(len(steps) + 1):
                    if n < len(steps):
                        v.wait_ge(high, n + 1)
                        v.tensor_tensor(a[:, n % B], a[:, n % B], parts[:, n % B, 0, :, 0, :], ALU.subtract)\
                            .then_inc(rest, 1)
                        if n % 2:
                            v.tensor_copy(parts[:, n % B, 2, :, 0, :], parts[:, n % B, 0, :, 0, :]).then_inc(by_dve, 1)
                    if n >= 1:
                        b = (n - 1) % B
                        v.wait_ge(mid, n)
                        v.tensor_tensor(parts[:, b, 2, :, 1, :], a[:, b], parts[:, b, 0, :, 1, :], ALU.subtract)\
                            .then_inc(low, 1)
                        v.tensor_copy(parts[:, b, 1, :, 1, :], parts[:, b, 0, :, 1, :]).then_inc(mid_copy, 1)


def relation_pass(nc, c, name, table, acc):
    COLS, LAG, EW = REL3 * WIN, 2, BUFS
    K = PARTS * ATTRS
    HALF = KC * REL3 // 2
    with ExitStack() as ctx:
        def sb(n, shape, dt=F32):
            return ctx.enter_context(nc.sbuf_tensor(name + n, shape, dt))
        got = sb("_got", [P, RING, D])
        rows = sb("_rows", [P, RING], I32)
        hot = sb("_hot", [P, RING, COLS])
        attr = sb("_attr", [K + PARTS, RING, 2, P], BF16)
        prod = sb("_prod", [P, BUFS, D])
        msg = sb("_msg", [P, BUFS, D])
        filled = [c.sem(f"{name}_in{r}") for r in range(RING)]
        attr_in = [c.sem(f"{name}_attr_in{r}") for r in range(RING)]
        (copied, let_go, hot_ready, scaled, prod_done, msg_ready, summed, added, clear, act_clear) = (
            c.sem(name + n) for n in ("_rows_copied", "_pool_seen", "_hot_ready", "_edge_scale", "_prod_done",
                                      "_msg_ready", "_summed", "_added", "_clear", "_act_clear"))
        with nc.Block() as block:
            @block.gpsimd
            def _(pool):
                gather_rows(pool, rows, got, prod_done, copied, table, filled, let_go, WSLOTS)

            @block.sync
            def _(sp):
                tiles = Rows(sp, name + "_edge_tile", c.win_edge_row, EDGE_TILES - 1)

                def body(s, i):
                    for r in range(RING):
                        j = tiles.at(i, r)
                        if known(s, 1):
                            sp.wait_ge(scaled, s + r - RING + 1)
                        sp.dma_start(attr[0:K, r], c.attr_parts[ds(j, 1)].rearrange("a k b e -> (a k) b e"))\
                            .then_inc(attr_in[r], 16)
                by_slots(sp, body, WSLOTS)
                tiles.free()

            @block.scalar
            def _(a):
                def body(s, i):
                    for r in range(RING):
                        a.wait_ge(prod_done, s + r + 1)
                        if known(s, 1) or r >= BUFS:
                            a.wait_ge(summed, s + r - BUFS + 1)
                        a.activation(msg[:, r % BUFS, :], prod[:, r % BUFS, :], ACT.Relu).then_inc(msg_ready, 1)
                        copy_next_rows(a, s, i, r, c.win_src, rows, filled, copied, WSLOTS)
                copy_first_rows(a, c.win_src, rows, filled, copied)
                for k in range(HALF, KC * REL3):
                    a.activation(acc[:, k, :], c.ones[:, 0:1].to_broadcast([128, WIN * WINS]), ACT.Copy,
                                 scale=0.0).then_inc(act_clear, 1)
                by_slots(a, body, WSLOTS)

            @block.tensor
            def _(pe):
                def scale(s, r, i, ahead=0):
                    n = r + ahead
                    pe.wait_ge(attr_in[n % RING], 16 * (i + n // RING + 1))
                    if known(s, 1) or n >= EW:
                        pe.wait_ge(prod_done, s + n - EW + 1)
                    pe.matmul(c.ps[n % EW][0:P, 0:D], attr[:, n % RING, 0, :], c.ew_parts[:, 0, :], start=True,
                              stop=False)
                    pe.matmul(c.ps[n % EW][0:P, 0:D], attr[0:K, n % RING, 1, :], c.ew_parts[0:K, 1, :], start=False,
                              stop=True).then_inc(scaled, 1)

                def body(s, i):
                    for r in range(RING):
                        if before_end(s, r, EW - 1, WSLOTS):
                            scale(s, r, i, EW - 1)
                        pe.wait_ge(msg_ready, s + r + 1)
                        pe.wait_ge(hot_ready, s + r + 1)
                        if known(s, 1) or r >= 2:
                            pe.wait_ge(added, s + r - 1)
                        for k in range(KC):
                            mm = pe.matmul(c.ps[6 + r % 2][:, k * COLS:(k + 1) * COLS],
                                           msg[:, r % BUFS, k * 128:(k + 1) * 128], hot[:, r, :], start=True, stop=True)
                        mm.then_inc(summed, 1)
                pe.wait_ge(clear, 1)
                for r in range(EW - 1):
                    scale(0, r, 0)
                by_slots(pe, body, WSLOTS)

            @block.vector
            def _(v):
                v.memset(attr[K:K + PARTS, :, 0, :], 1.0).then_inc(clear, 1)
                v.memset(acc[:, 0:HALF, :], 0.0).then_inc(clear, 1)
                v.wait_ge(clear, 2)

                places = Rows(v, name + "_win", c.win_row, WIN * (WINS - 1))

                def add(s, n, i):
                    add_sum(v, s, n, i, places, summed, added, lambda t: acc[:, :, ds(t, WIN)],
                            c.ps[6 + n % 2][:, 0:KC * COLS].rearrange("p (g n) -> p g n", n=WIN))
                    if before_end(s, n, RING, WSLOTS):
                        one_hot(v, c, hot, s, n, hot_ready, c.win_key, COLS, RING)

                def body(s, i):
                    for r in range(RING):
                        if isinstance(s, int) and s + r == LAG:
                            v.wait_ge(act_clear, KC * REL3 - HALF)
                        v.wait_ge(scaled, s + r + 1)
                        v.wait_ge(filled[r], 16 * (i + 1))
                        if known(s, 1) or r >= BUFS:
                            v.wait_ge(msg_ready, s + r - BUFS + 1)
                        v.tensor_tensor(prod[:, r % BUFS, :], got[:, r, :], c.ps[r % EW][0:P, 0:D],
                                        ALU.mult).then_inc(prod_done, 1)
                        if known(s, 1) or r >= LAG:
                            add(s - RING, r - LAG + RING, i - 1) if r < LAG else add(s, r - LAG, i)
                for r in range(RING):
                    one_hot(v, c, hot, 0, r, hot_ready, c.win_key, COLS)
                by_slots(v, body, WSLOTS)
                for r in range(RING - LAG, RING):
                    add(WSLOTS - RING, r, WSLOTS // RING - 1)
                places.free()


def relation_mix(nc, c, name, layer, acc, x_table):
    R = REL3 + 1
    with ExitStack() as ctx:
        def sb(n, shape, dt=F32):
            return ctx.enter_context(nc.sbuf_tensor(name + n, shape, dt))
        w, bias = sb("_w", [128, R, KC, D]), sb("_bias", [P, D])
        agg, xs, xt = sb("_agg", [128, 2, KC * REL3, P]), sb("_x", [P, 2, D]), sb("_xt", [128, 2, KC, P])
        out_s = sb("_sum", [P, 2, D])
        load, agg_ready, turned, t_ready, mixed, chain, out, stored = (
            c.sem(name + n) for n in ("_loads", "_agg_ready", "_turned", "_t_ready", "_mixed", "_sum_chain", "_out",
                                      "_stored"))
        with nc.Block() as block:
            @block.sync
            def _(sp):
                sp.dma_start(w[:, 0:REL3], c.weights[layer].rearrange("r (c p) o -> p r c o", p=128)).then_inc(load, 16)
                sp.dma_start(w[:, REL3], c.roots[layer].rearrange("(c p) o -> p c o", p=128)).then_inc(load, 16)
                sp.dma_start(bias[:, :], c.biases[layer].partition_broadcast(P)).then_inc(load, 16)
                if x_table is not None:
                    sp.wait_ge(out, NODE_TILES)
                    sp.dma_start(x_table.rearrange("(t p) d -> p t d", p=P), c.nodes[:, :, :]).then_inc(stored, 16)
                    sp.wait_ge(stored, 16)

            @block.scalar
            def _(a):
                def body(t, b, uses):
                    at = slice(t * P, (t + 1) * P) if isinstance(t, int) else ds(t * P, P)
                    if known(t, 2):
                        a.wait_ge(mixed, t - 1)
                    a.copy(xs[:, b, :], flat(c.nodes[:, tile_at(t), :])).then_inc(agg_ready, 1)
                    a.copy(agg[:, b], acc[:, :, at]).then_inc(agg_ready, 1)
                by_tiles(a, body)

            @block.tensor
            def _(pe):
                def turn(t, b):
                    pe.wait_ge(agg_ready, 2 * t + 1)
                    if known(t, 2):
                        pe.wait_ge(t_ready, t - 1)
                    for k in range(KC):
                        mm = pe.transpose(c.ps[4 + b][:, k * P:(k + 1) * P], xs[:, b, k * 128:(k + 1) * 128],
                                          c.ident[0:P, 0:P])
                    mm.then_inc(turned, 1)

                def body(t, b, uses):
                    turn(t, b)
                    pe.wait_ge(agg_ready, 2 * t + 2)
                    if known(t, 2):
                        pe.wait_ge(out, t - 1)
                    for r in range(R):
                        if r == REL3:
                            pe.wait_ge(t_ready, t + 1)
                        for k in range(KC):
                            lhs = agg[:, b, k * REL3 + r, :] if r < REL3 else xt[:, b, k, :]
                            mm = pe.matmul(c.pair[b][0:P, r * D:(r + 1) * D], lhs, w[:, r, k, :], start=(k == 0),
                                           stop=(k == KC - 1), skip_group_check=True)
                    mm.then_inc(mixed, 1)
                pe.wait_ge(load, 48)
                by_tiles(pe, body)

            @block.vector
            def _(v):
                v.wait_ge(load, 48)
                do = Chain(v, chain)

                def turn(t, b):
                    v.wait_ge(turned, t + 1)
                    v.tensor_copy(xt[:, b], c.ps[4 + b][:, 0:KC * P].rearrange("p (c n) -> p c n", n=P))\
                        .then_inc(t_ready, 1)

                def last(t, b):
                    do.at(R * t)
                    v.wait_ge(mixed, t + 1)
                    part = bias[:, :]
                    for r in range(REL3):
                        do(v.scalar_tensor_tensor(out=out_s[:, b, :], in0=c.pair[b][0:P, r * D:(r + 1) * D],
                                                  scalar=flat(c.cnt[:, tile_at(t), 1 + r:2 + r]), in1=part,
                                                  op0=ALU.mult, op1=ALU.add))
                        part = out_s[:, b, :]
                    do(v.tensor_tensor(part, part, c.pair[b][0:P, REL3 * D:R * D], ALU.add))
                    x = flat(c.nodes[:, tile_at(t), :])
                    v.scalar_tensor_tensor(out=x, in0=part, scalar=0.0, in1=x, op0=ALU.max,
                                           op1=ALU.add).then_inc(out, 1)

                def body(t, b, uses):
                    if known(t, 2):
                        v.wait_ge(mixed, t - 1)
                    turn(t, b)
                    if known(t, 1):
                        last(t - 1, 1 - b)
                by_tiles(v, body)
                last(NODE_TILES - 1, (NODE_TILES - 1) % 2)


def program(nc, c):
    outer = ExitStack()
    with outer:
        c.in_use = []

        def sem(name):
            c.in_use.append(nc.alloc_semaphore(name))
            return c.in_use[-1]
        c.sem = sem
        c.pair = [outer.enter_context(nc.psum_tensor(f"banks{k}", [128, 1024], F32)) for k in range(4)]
        c.ps = [c.pair[k // 2][:, k % 2 * 512:(k % 2 + 1) * 512] for k in range(8)]
        c.iota = outer.enter_context(nc.sbuf_tensor("iota", [128, IOTA], F32))
        c.part = outer.enter_context(nc.sbuf_tensor("part", [128, 1], F32))
        c.ident = outer.enter_context(nc.sbuf_tensor("ident", [128, 128], F32))
        c.ident16 = outer.enter_context(nc.sbuf_tensor("ident16", [128, 128], BF16))
        c.ones = outer.enter_context(nc.sbuf_tensor("ones", [128, 128], F32))
        c.below = outer.enter_context(nc.sbuf_tensor("below", [128, 128], F32))
        c.tile_row = outer.enter_context(nc.sbuf_tensor("tile_row", [1, ROUNDS, ROW16], I16))
        c.win_row = outer.enter_context(nc.sbuf_tensor("win_row", [1, WSLOTS // RING, ROW16], I16))
        c.win_edge_row = outer.enter_context(nc.sbuf_tensor("win_edge_row", [1, WSLOTS // RING, ROW16], I16))
        c.win_key = outer.enter_context(nc.sbuf_tensor("win_key", [P, WSLOTS], F32))
        c.win_src = outer.enter_context(nc.sbuf_tensor("win_src", [P, WSLOTS], I32))
        c.dloc = outer.enter_context(nc.sbuf_tensor("dloc", [P, SLOTS], F32))
        c.src_idx = outer.enter_context(nc.sbuf_tensor("src_idx", [P, SLOTS], I32))
        c.cnt = outer.enter_context(nc.sbuf_tensor("cnt", [P, NODE_TILES, 1 + REL3], F32))
        c.rdeg = outer.enter_context(nc.sbuf_tensor("rdeg", [P, NODE_TILES], F32))
        c.nodes = outer.enter_context(nc.sbuf_tensor("nodes", [P, NODE_TILES, D], F32))
        c.nodes_b = outer.enter_context(nc.sbuf_tensor("nodes_b", [P, NODE_TILES, D], F32))
        c.key_table = nc.dram_tensor("key_table", (RELS * N, D), F32, kind="Internal").ap()
        c.msg_table = nc.dram_tensor("msg_table", (RELS * N, D), F32, kind="Internal").ap()
        c.seq_dram = nc.dram_tensor("seq_dram", (HEADS + 2, SLOTS, P), F32, kind="Internal").ap()
        c.max_dram = nc.dram_tensor("max_dram", (HEADS, SLOTS, P), F32, kind="Internal").ap()

        c.x_table = [nc.dram_tensor(f"x_table{k}", (N, D), F32, kind="Internal").ap() for k in range(5)]
        c.row_table = nc.dram_tensor("row_table", (N * TOPK, D), F32, kind="Internal").ap()
        c.expert_table = nc.dram_tensor("expert_table", (N * TOPK, D), F32, kind="Internal").ap()
        c.attr_parts = nc.dram_tensor("attr_parts", (EDGE_TILES, PARTS * ATTRS, 2, P), BF16, kind="Internal").ap()
        c.rout = outer.enter_context(nc.sbuf_tensor("rout", [P, NODE_TILES], F32))

        constants(nc, c)
        with ExitStack() as layer0:
            c.kv_idx = layer0.enter_context(nc.sbuf_tensor("kv_idx", [P, SLOTS], I32))
            c.valid = layer0.enter_context(nc.sbuf_tensor("valid", [P, SLOTS], F32))
            c.starts = layer0.enter_context(nc.sbuf_tensor("starts", [P, SLOTS], F32))
            c.ends = layer0.enter_context(nc.sbuf_tensor("ends", [P, SLOTS], F32))
            c.edge_cols = layer0.enter_context(nc.sbuf_tensor("edge_cols", [P, SLOTS, EXTRA], F32))
            c.type_row = layer0.enter_context(nc.sbuf_tensor("type_row", [128, N], I32))
            slot_tables(nc, c)
            project(nc, c)
            c.score = layer0.enter_context(nc.sbuf_tensor("score", [P, SLOTS, HEADS], F32))
            attention_scores(nc, c)
            segment_softmax(nc, c)
            c.acc = layer0.enter_context(nc.sbuf_tensor("acc0", [P, NODE_TILES, D + EXTRA], F32))
            c.wa_s = layer0.enter_context(nc.sbuf_tensor("wa_s", [128, NTYPES, KC, D], F32))
            c.ahead = c.sem("loads_ahead")
            weighted_messages(nc, c)
            attention_output(nc, c)
        row_norm(nc, c, "norm0", c.nodes_b, c.x_table[0], scale=c.rout)
        clear_semaphores(nc, c)

        with ExitStack() as layer1:
            x1 = c.nodes_b
            logits = layer1.enter_context(nc.sbuf_tensor("logits", [P, NODE_TILES, EXPERTS], F32))
            with nc.sbuf_tensor("acc1", [P, NODE_TILES, D], F32) as acc:
                graph_sum(nc, c, "sum1", c.x_table[0], acc)
                conv_and_router(nc, c, acc, x1, logits)
            c.gate = [layer1.enter_context(nc.sbuf_tensor(f"gate{k}", [P, NODE_TILES], F32)) for k in range(TOPK)]
            c.pos = [layer1.enter_context(nc.sbuf_tensor(f"pos{k}", [P, NODE_TILES], I32)) for k in range(TOPK)]
            c.row_expert = layer1.enter_context(nc.sbuf_tensor("row_expert", [P, ROW_TILES], F32))
            c.step_expert = layer1.enter_context(nc.sbuf_tensor("step_expert", [P, STEPS], F32))
            c.step_rows = layer1.enter_context(nc.sbuf_tensor("step_rows", [1, 2, STEPS], I32))
            route(nc, c, x1, logits)
            experts(nc, c)
            combine(nc, c, x1)
            batch_norm(nc, c, "bn1", x1, c.gamma, c.beta)
        row_norm(nc, c, "norm1", c.nodes_b, c.x_table[1])
        clear_semaphores(nc, c)

        with nc.sbuf_tensor("acc2", [P, NODE_TILES, D], F32) as acc:
            graph_sum(nc, c, "sum2", c.x_table[1], acc)
            linear(nc, c, acc, c.nodes_b)
        batch_norm(nc, c, "bn2", c.nodes_b, c.bn_w, c.bn_b)
        row_norm(nc, c, "norm2", c.nodes_b, c.x_table[2])

        clear_semaphores(nc, c)

        keep_input(nc, c)
        c.ew_parts = outer.enter_context(nc.sbuf_tensor("ew_parts", [PARTS * (ATTRS + 1), 2, D], BF16))
        split_edge_product(nc, c)
        for layer in range(3):
            with nc.sbuf_tensor(f"acc3_{layer}", [128, KC * REL3, WIN * WINS], F32) as acc:
                relation_pass(nc, c, f"rel{layer}", c.x_table[2 + layer], acc)
                relation_mix(nc, c, f"mix{layer}", layer, acc, c.x_table[3 + layer] if layer < 2 else None)
        add_input(nc, c)
        row_norm(nc, c, "norm3", c.nodes_b, c.out)


def clear_semaphores(nc, c):
    nc.all_engine_barrier()
    nc.clear_and_free_semaphores(c.in_use)
    c.in_use.clear()
    nc.all_engine_barrier()


def keep_input(nc, c):
    done = c.sem("input_kept")
    with nc.Block() as block:
        @block.vector
        def _(v):
            v.tensor_copy(c.nodes_b[:, :, :], c.nodes[:, :, :]).then_inc(done, 1)


def add_input(nc, c):
    done = c.sem("input_added")
    with nc.Block() as block:
        @block.vector
        def _(v):
            v.tensor_tensor(c.nodes_b[:, :, :], c.nodes_b[:, :, :], c.nodes[:, :, :], ALU.add).then_inc(done, 1)


_INS = {
    "x": ("x", lambda a: a), "xT": ("x", lambda a: a.T), "src": ("src", lambda a: a), "dst": ("dst", lambda a: a),
    "t3": ("edge_type_3", lambda a: a), "t8": ("edge_type_8", lambda a: a),
    "node_type": ("node_type_4", lambda a: a), "node_type_cols": ("node_type_4", lambda a: a.reshape(NODE_TILES, P).T),
    "wq": ("L0_gnn_q_linears", lambda a: a), "wk": ("L0_gnn_k_linears", lambda a: a),
    "wv": ("L0_gnn_v_linears", lambda a: a), "wa": ("L0_gnn_a_linears", lambda a: a),
    "attT": ("L0_gnn_relation_att", lambda a: a.transpose(0, 1, 3, 2)), "msg": ("L0_gnn_relation_msg", lambda a: a),
    "pri": ("L0_gnn_relation_pri", lambda a: a), "skip": ("L0_gnn_skip", lambda a: a),
    "W_gc": ("L1_gnn_W_gc", lambda a: a), "W_res": ("L1_gnn_W_res", lambda a: a), "b_gc": ("L1_gnn_b_gc", lambda a: a),
    "b_res": ("L1_gnn_b_res", lambda a: a), "Wg": ("L1_gnn_Wg", lambda a: a), "bg": ("L1_gnn_bg", lambda a: a),
    "w1": ("L1_gnn_w1", lambda a: a), "b1": ("L1_gnn_b1", lambda a: a.reshape(EXPERTS, HC, 128).transpose(0, 2, 1)),
    "w2": ("L1_gnn_w2", lambda a: a), "b2": ("L1_gnn_b2", lambda a: a), "gamma": ("L1_gnn_gamma", lambda a: a),
    "beta": ("L1_gnn_beta", lambda a: a), "w_linT": ("L2_gnn_W", lambda a: a.T), "b_lin": ("L2_gnn_b", lambda a: a),
    "bn_w": ("L2_gnn_bn_w", lambda a: a), "bn_b": ("L2_gnn_bn_b", lambda a: a),
    "weights": ("L3_gnn_weights", lambda a: a), "roots": ("L3_gnn_roots", lambda a: a),
    "biases": ("L3_gnn_biases", lambda a: a), "edge_w": ("L3_gnn_edge_w", lambda a: a),
    "edge_b": ("L3_gnn_edge_b", lambda a: a.reshape(1, D)),
    "attrT": ("edge_attr_32", lambda a: a.reshape(EDGE_TILES, P, 32).transpose(0, 2, 1)),
}


def kernel(**inputs):
    import numpy as _np
    import concourse.bacc as _bacc
    from concourse import mybir as _mybir
    from concourse.bass_utils import run_bass_kernel_spmd as _run

    nc = _bacc.Bacc("TRN2", target_bir_lowering=False, num_devices=1)
    c = Core()
    arrays = {}
    for name, (arg, lay) in _INS.items():
        a = _np.ascontiguousarray(lay(_np.asarray(inputs[arg])))
        arrays[f"in_{name}"] = a
        c.__dict__[name] = nc.dram_tensor(f"in_{name}", a.shape, _mybir.dt.from_np(a.dtype), kind="ExternalInput").ap()
    c.out = nc.dram_tensor("out_x", (N, D), F32, kind="ExternalOutput").ap()
    program(nc, c)
    r = _run(nc, [arrays], core_ids=[0])
    return r.results[0]["out_x"]
```
